# Optimizing a Trainium2 kernel written in Bass

```python
import numpy as np
import jax
import jax.numpy as jnp

def _softmax(x, axis=-1):
    return jax.nn.softmax(x, axis=axis)

def _gelu(x):
    return jax.nn.gelu(x, approximate=True)

def _silu(x):
    return jax.nn.silu(x)

def _sigmoid(x):
    return jax.nn.sigmoid(x)

def _layernorm(x, axis=-1, eps=1e-05):
    m = jnp.mean(x, axis=axis, keepdims=True)
    v = jnp.var(x, axis=axis, keepdims=True)
    return (x - m) / jnp.sqrt(v + eps)

def _scatter_add(tgt, idx, src, axis=0):
    return tgt.at[idx].add(src)

def _segment_sum(src, seg, n):
    return jax.ops.segment_sum(src, seg, n)
kernel_name = 'mk_seq_postln_d1_jaxref_r4_6d01df'

def setup_inputs(seed: int=0):
    np.random.seed(seed)
    _w = jnp.asarray

    def _L0_attn_setup():
        import jax, jax.numpy as jnp
        import numpy as np
        N_HEADS = 16
        key = jax.random.key(seed)
        ks = jax.random.split(key, 9)
        B, S, E = (2, 512, 256)
        s = 1.0 / np.sqrt(E)
        return {'x': jax.random.normal(ks[0], (B, S, E), jnp.float32), 'Wq': jax.random.normal(ks[1], (E, E), jnp.float32) * s, 'bq': jax.random.normal(ks[2], (E,), jnp.float32) * 0.01, 'Wk': jax.random.normal(ks[3], (E, E), jnp.float32) * s, 'bk': jax.random.normal(ks[4], (E,), jnp.float32) * 0.01, 'Wv': jax.random.normal(ks[5], (E, E), jnp.float32) * s, 'bv': jax.random.normal(ks[6], (E,), jnp.float32) * 0.01, 'Wo': jax.random.normal(ks[7], (E, E), jnp.float32) * s, 'bo': jax.random.normal(ks[8], (E,), jnp.float32) * 0.01}
    _L0_attn_in = _L0_attn_setup()

    def _L0_ffn_setup():
        import jax, jax.numpy as jnp
        import numpy as np
        DIM = 256
        DEPTH = 2
        HEADS = 8
        DIM_HEAD = 64
        WINDOW = 128
        INNER = HEADS * DIM_HEAD
        HID = int(DIM * 4 * 2 / 3)
        B, N = (2, 2048)
        QK_SCALE = 8.0

        def shift_token(t):
            t1, t2 = jnp.split(t, 2, axis=-1)
            t2 = jnp.pad(t2, ((0, 0), (1, 0), (0, 0)))[:, :-1]
            return jnp.concatenate([t1, t2], axis=-1)

        def l2norm(t):
            return t / jnp.clip(jnp.linalg.norm(t, axis=-1, keepdims=True), 1e-12)

        def rotate_half(x):
            x1, x2 = jnp.split(x, 2, axis=-1)
            return jnp.concatenate([-x2, x1], axis=-1)

        def rotary_xpos(q, k):
            n = q.shape[-2]
            half_idx = jnp.arange(0, DIM_HEAD, 2, dtype=jnp.float32)
            inv_freq = 1.0 / 10000.0 ** (half_idx / DIM_HEAD)
            t = jnp.arange(n, dtype=jnp.float32)
            freqs = t[:, None] * inv_freq[None, :]
            freqs = jnp.concatenate([freqs, freqs], axis=-1)
            base = (half_idx + 0.4 * DIM_HEAD) / (1.4 * DIM_HEAD)
            power = (t - n // 2) / float(WINDOW // 2)
            scale = base[None, :] ** power[:, None]
            scale = jnp.concatenate([scale, scale], axis=-1)
            cos, sin = (jnp.cos(freqs), jnp.sin(freqs))
            q = q * cos * scale + rotate_half(q) * sin * scale
            k = k * cos / scale + rotate_half(k) * sin / scale
            return (q, k)

        def local_attention(q, k, v):
            b, h, n, d = q.shape
            w = n // WINDOW
            bq = q.reshape(b, h, w, WINDOW, d) * QK_SCALE
            bk = k.reshape(b, h, w, WINDOW, d)
            bv = v.reshape(b, h, w, WINDOW, d)

            def look_around(t):
                p = jnp.pad(t, ((0, 0), (0, 0), (1, 0), (0, 0), (0, 0)))
                return jnp.concatenate([p[:, :, :w], p[:, :, 1:]], axis=3)
            bk, bv = (look_around(bk), look_around(bv))
            bt = jnp.arange(n).reshape(w, WINDOW)
            btp = jnp.pad(bt, ((1, 0), (0, 0)), constant_values=-1)
            btk = jnp.concatenate([btp[:w], btp[1:]], axis=1)
            sim = jnp.einsum('bhwid,bhwjd->bhwij', bq, bk)
            i = bt[:, :, None]
            j = btk[:, None, :]
            mask = (i < j) | (i > j + WINDOW) | (j == -1)
            sim = jnp.where(mask, -jnp.finfo(sim.dtype).max, sim)
            attn = jax.nn.softmax(sim, axis=-1)
            out = jnp.einsum('bhwij,bhwjd->bhwid', attn, bv)
            return out.reshape(b, h, n, d)

        def _layer(x, wqkv, qs, ksc, wo, lg, lb, w1, b1, w2, b2):
            b, n, _ = x.shape
            h = shift_token(x)
            qkv = h @ wqkv
            q, k, v = jnp.split(qkv, 3, axis=-1)
            to_heads = lambda t: t.reshape(b, n, HEADS, DIM_HEAD).transpose(0, 2, 1, 3)
            q, k, v = (to_heads(q), to_heads(k), to_heads(v))
            q = l2norm(q) * qs
            k = l2norm(k) * ksc
            q, k = rotary_xpos(q, k)
            o = local_attention(q, k, v)
            o = o.transpose(0, 2, 1, 3).reshape(b, n, INNER)
            x = x + o @ wo
            h = shift_token(x)
            mu = h.mean(-1, keepdims=True)
            var = h.var(-1, keepdims=True)
            h = (h - mu) / jnp.sqrt(var + 1e-05) * lg + lb
            h = h @ w1 + b1
            a, g = jnp.split(h, 2, axis=-1)
            h = a * jax.nn.gelu(g, approximate=False)
            x = x + h @ w2 + b2
            return x
        key = jax.random.key(seed)
        ks = jax.random.split(key, 6)
        return {'x': jax.random.normal(ks[0], (B, N, DIM), jnp.float32), 'wqkv': jax.random.normal(ks[1], (DEPTH, DIM, 3 * INNER), jnp.float32) * 0.02, 'q_scale': jnp.ones((DEPTH, DIM_HEAD), jnp.float32), 'k_scale': jnp.ones((DEPTH, DIM_HEAD), jnp.float32), 'wo': jax.random.normal(ks[2], (DEPTH, INNER, DIM), jnp.float32) * 0.02, 'ln_g': jnp.ones((DEPTH, DIM), jnp.float32), 'ln_b': jnp.zeros((DEPTH, DIM), jnp.float32), 'w1': jax.random.normal(ks[3], (DEPTH, DIM, 2 * HID), jnp.float32) * 0.02, 'b1': jnp.zeros((DEPTH, 2 * HID), jnp.float32), 'w2': jax.random.normal(ks[4], (DEPTH, HID, DIM), jnp.float32) * 0.02, 'b2': jnp.zeros((DEPTH, DIM), jnp.float32)}
    _L0_ffn_in = _L0_ffn_setup()
    _d = {'L0_attn_x': _L0_attn_in['x'], 'L0_attn_Wq': _L0_attn_in['Wq'], 'L0_attn_bq': _L0_attn_in['bq'], 'L0_attn_Wk': _L0_attn_in['Wk'], 'L0_attn_bk': _L0_attn_in['bk'], 'L0_attn_Wv': _L0_attn_in['Wv'], 'L0_attn_bv': _L0_attn_in['bv'], 'L0_attn_Wo': _L0_attn_in['Wo'], 'L0_attn_bo': _L0_attn_in['bo'], 'L0_ffn_wqkv': _L0_ffn_in['wqkv'], 'L0_ffn_q_scale': _L0_ffn_in['q_scale'], 'L0_ffn_k_scale': _L0_ffn_in['k_scale'], 'L0_ffn_wo': _L0_ffn_in['wo'], 'L0_ffn_ln_g': _L0_ffn_in['ln_g'], 'L0_ffn_ln_b': _L0_ffn_in['ln_b'], 'L0_ffn_w1': _L0_ffn_in['w1'], 'L0_ffn_b1': _L0_ffn_in['b1'], 'L0_ffn_w2': _L0_ffn_in['w2'], 'L0_ffn_b2': _L0_ffn_in['b2']}
    _x0 = _d['L0_attn_x']
    _d['L0_attn_x'] = jax.random.normal(jax.random.fold_in(jax.random.key(seed), 1), (16, 512, 256), dtype=_x0.dtype)
    del _x0
    return _d

def reference(L0_attn_x, L0_attn_Wq, L0_attn_bq, L0_attn_Wk, L0_attn_bk, L0_attn_Wv, L0_attn_bv, L0_attn_Wo, L0_attn_bo, L0_ffn_wqkv, L0_ffn_q_scale, L0_ffn_k_scale, L0_ffn_wo, L0_ffn_ln_g, L0_ffn_ln_b, L0_ffn_w1, L0_ffn_b1, L0_ffn_w2, L0_ffn_b2):

    def _L0_attn_ref(x, Wq, bq, Wk, bk, Wv, bv, Wo, bo):
        import jax, jax.numpy as jnp
        import numpy as np
        N_HEADS = 16
        B, S, E = x.shape
        H = N_HEADS
        D = E // H
        q = (x @ Wq.T + bq).reshape(B, S, H, D)
        k = (x @ Wk.T + bk).reshape(B, S, H, D)
        v = (x @ Wv.T + bv).reshape(B, S, H, D)
        scores = jnp.einsum('bqnd,bknd->bnqk', q, k) / jnp.sqrt(jnp.float32(D))
        attn = jax.nn.softmax(scores, axis=1)
        out = jnp.einsum('bnqk,bknd->bnqd', attn, v)
        out = out.transpose(0, 2, 1, 3).reshape(B, S, E)
        return out @ Wo.T + bo

    def _L0_ffn_ref(x, wqkv, q_scale, k_scale, wo, ln_g, ln_b, w1, b1, w2, b2):
        import jax, jax.numpy as jnp
        import numpy as np
        DIM = 256
        DEPTH = 2
        HEADS = 8
        DIM_HEAD = 64
        WINDOW = 128
        INNER = HEADS * DIM_HEAD
        HID = int(DIM * 4 * 2 / 3)
        B, N = (2, 2048)
        QK_SCALE = 8.0

        def shift_token(t):
            t1, t2 = jnp.split(t, 2, axis=-1)
            t2 = jnp.pad(t2, ((0, 0), (1, 0), (0, 0)))[:, :-1]
            return jnp.concatenate([t1, t2], axis=-1)

        def l2norm(t):
            return t / jnp.clip(jnp.linalg.norm(t, axis=-1, keepdims=True), 1e-12)

        def rotate_half(x):
            x1, x2 = jnp.split(x, 2, axis=-1)
            return jnp.concatenate([-x2, x1], axis=-1)

        def rotary_xpos(q, k):
            n = q.shape[-2]
            half_idx = jnp.arange(0, DIM_HEAD, 2, dtype=jnp.float32)
            inv_freq = 1.0 / 10000.0 ** (half_idx / DIM_HEAD)
            t = jnp.arange(n, dtype=jnp.float32)
            freqs = t[:, None] * inv_freq[None, :]
            freqs = jnp.concatenate([freqs, freqs], axis=-1)
            base = (half_idx + 0.4 * DIM_HEAD) / (1.4 * DIM_HEAD)
            power = (t - n // 2) / float(WINDOW // 2)
            scale = base[None, :] ** power[:, None]
            scale = jnp.concatenate([scale, scale], axis=-1)
            cos, sin = (jnp.cos(freqs), jnp.sin(freqs))
            q = q * cos * scale + rotate_half(q) * sin * scale
            k = k * cos / scale + rotate_half(k) * sin / scale
            return (q, k)

        def local_attention(q, k, v):
            b, h, n, d = q.shape
            w = n // WINDOW
            bq = q.reshape(b, h, w, WINDOW, d) * QK_SCALE
            bk = k.reshape(b, h, w, WINDOW, d)
            bv = v.reshape(b, h, w, WINDOW, d)

            def look_around(t):
                p = jnp.pad(t, ((0, 0), (0, 0), (1, 0), (0, 0), (0, 0)))
                return jnp.concatenate([p[:, :, :w], p[:, :, 1:]], axis=3)
            bk, bv = (look_around(bk), look_around(bv))
            bt = jnp.arange(n).reshape(w, WINDOW)
            btp = jnp.pad(bt, ((1, 0), (0, 0)), constant_values=-1)
            btk = jnp.concatenate([btp[:w], btp[1:]], axis=1)
            sim = jnp.einsum('bhwid,bhwjd->bhwij', bq, bk)
            i = bt[:, :, None]
            j = btk[:, None, :]
            mask = (i < j) | (i > j + WINDOW) | (j == -1)
            sim = jnp.where(mask, -jnp.finfo(sim.dtype).max, sim)
            attn = jax.nn.softmax(sim, axis=-1)
            out = jnp.einsum('bhwij,bhwjd->bhwid', attn, bv)
            return out.reshape(b, h, n, d)

        def _layer(x, wqkv, qs, ksc, wo, lg, lb, w1, b1, w2, b2):
            b, n, _ = x.shape
            h = shift_token(x)
            qkv = h @ wqkv
            q, k, v = jnp.split(qkv, 3, axis=-1)
            to_heads = lambda t: t.reshape(b, n, HEADS, DIM_HEAD).transpose(0, 2, 1, 3)
            q, k, v = (to_heads(q), to_heads(k), to_heads(v))
            q = l2norm(q) * qs
            k = l2norm(k) * ksc
            q, k = rotary_xpos(q, k)
            o = local_attention(q, k, v)
            o = o.transpose(0, 2, 1, 3).reshape(b, n, INNER)
            x = x + o @ wo
            h = shift_token(x)
            mu = h.mean(-1, keepdims=True)
            var = h.var(-1, keepdims=True)
            h = (h - mu) / jnp.sqrt(var + 1e-05) * lg + lb
            h = h @ w1 + b1
            a, g = jnp.split(h, 2, axis=-1)
            h = a * jax.nn.gelu(g, approximate=False)
            x = x + h @ w2 + b2
            return x
        for l in range(DEPTH):
            x = _layer(x, wqkv[l], q_scale[l], k_scale[l], wo[l], ln_g[l], ln_b[l], w1[l], b1[l], w2[l], b2[l])
        return x
    x = L0_attn_x
    x = _layernorm(x + _L0_attn_ref(x, L0_attn_Wq, L0_attn_bq, L0_attn_Wk, L0_attn_bk, L0_attn_Wv, L0_attn_bv, L0_attn_Wo, L0_attn_bo), axis=-1)
    x = _layernorm(x + _L0_ffn_ref(x, L0_ffn_wqkv, L0_ffn_q_scale, L0_ffn_k_scale, L0_ffn_wo, L0_ffn_ln_g, L0_ffn_ln_b, L0_ffn_w1, L0_ffn_b1, L0_ffn_w2, L0_ffn_b2), axis=-1)
    return x

_drawn_inputs = setup_inputs


def setup_inputs(seed=0):
    import zlib

    import numpy as np

    out = dict(_drawn_inputs(seed))
    spreads = {'L0_ffn_q_scale': (1.0, 0.6),
     'L0_ffn_k_scale': (1.0, 0.6),
     'L0_ffn_ln_g': (1.0, 0.6),
     'L0_ffn_ln_b': (0.0, 0.8),
     'L0_ffn_b1': (0.0, 0.8),
     'L0_ffn_b2': (0.0, 0.1)}
    factors = {'L0_attn_bq': 6.222, 'L0_attn_bk': 7.406, 'L0_attn_bo': 8.0}
    for name, (base, spread) in spreads.items():
        noise = np.random.default_rng([zlib.crc32(name.encode()), seed]).standard_normal(out[name].shape)
        drawn = base * np.exp(spread * noise) if base else spread * noise
        out[name] = jnp.asarray(drawn.astype(out[name].dtype))
    for name, factor in factors.items():
        out[name] = (out[name] * factor).astype(out[name].dtype)
    return out
```

```python
from contextlib import ExitStack

import numpy as np

import concourse.bass as bass
from concourse import mybir

F32 = mybir.dt.float32
F32R = mybir.dt.float32r
BF16 = mybir.dt.bfloat16
ACT = mybir.ActivationFunctionType
ALU = mybir.AluOpType
AX = mybir.AxisListType

P = 128
SEQS, SEQ, CH = 16, 512, 256
TILES = SEQ // P
CT = CH // P
HEADS, HDIM = 16, 16
JH = HEADS // CT
UNITS = TILES * TILES
EPS = 1e-5
TERMS = [(0, 0), (0, 1), (1, 0), (1, 1), (0, 2), (2, 0), (1, 2), (2, 1)]


def need(engine, sem, value):
    if not (isinstance(value, int) and value <= 0):
        engine.wait_ge(sem, value)


def lagged(n, u, lag, steps):
    return (n, 0, u - lag) if u >= lag else (n - 1, 1, u - lag + steps)


def exists(n):
    return not isinstance(n, int) or 0 <= n < SEQS


def head_attention(nc, ctx, x_in, w, x_out, consts, W0=None):
    ident, identr, half = consts["ident"], consts["identr"], consts["minus_half"]
    ones_row = consts["ones_row"]

    def sb(name, shape, dtype=F32):
        return ctx.enter_context(nc.sbuf_tensor("a_" + name, shape, dtype))

    def sem(name):
        return ctx.enter_context(nc.semaphore("a_" + name))

    def bank(name, shape=(P, 512)):
        return ctx.enter_context(nc.psum_tensor("a_" + name, list(shape), F32))

    wq, wk, wv, wo = (sb(n, [P, CT, CH]) for n in ("wq", "wk", "wv", "wo"))
    bq, bk, bq_scaled = (sb(n, [P, CT]) for n in ("bq", "bk", "bqs"))
    bv_rows, bo_row = sb("bv", [P, CH]), sb("bo", [1, CH])
    x_tok = [sb(f"x{i}", [P, TILES, CH]) for i in range(2)]
    xT = sb("xT", [P, CT, SEQ])
    qk32 = [sb(f"qk32{i}", [P, CT, SEQ]) for i in range(2)]
    parts = [sb(f"parts{i}", [P, 3, CT, SEQ], BF16) for i in range(2)]
    qk8 = [[sb(f"{n}8{i}", [P, JH, CT, SEQ], BF16) for n in "qk"] for i in range(2)]
    v_pad = [sb(f"v{i}", [P, TILES, HEADS // 2, 64]) for i in range(2)]
    NE = 4
    probs = [sb(f"p{i}", [P, HEADS, P]) for i in range(NE)]
    z8, z4, z2 = sb("z8", [P, 8, P]), sb("z4", [P, 4, P]), sb("z2", [P, 2, P])
    zsum, zinv = ([sb(f"{n}{i}", [P, P]) for i in range(2)] for n in ("zs", "zi"))
    negmax = [sb(f"nm{i}", [P, P], F32R) for i in range(2)]
    oT = [sb(f"oT{i}", [P, CT, P]) for i in range(2)]
    resid = [sb(f"r{i}", [P, CH]) for i in range(2)]
    stats, carrier, mv = sb("stats", [P, 6]), sb("carrier", [P, 1]), [sb(f"mv{i}", [P, 2]) for i in range(2)]
    vareps, rstd = ([sb(f"{n}{i}", [P, 1]) for i in range(2)] for n in ("ve", "rs"))
    normed = [sb(f"n{i}", [P, CH]) for i in range(2)]

    S = bank("S", (P, HEADS, P))
    O = bank("O", (P, CT, P))
    Y = bank("Y", (P, CH))
    B = [bank("B0"), bank("B1")]

    s_w = sem("weights_loaded")
    s_w0 = sem("next_weights_loaded")
    s_x = [sem(f"x_loaded{i}") for i in range(2)]
    s_bqs = sem("bq_scaled")
    s_pz = sem("vpad_zeroed")
    s_pt = sem("proj_psum")
    s_pv = sem("proj_evacuated")
    s_vv = sem("v_evacuated")
    s_rest = sem("rest_ready")
    s_mid = sem("middle_part")
    s_low = sem("low_part")
    s_pack = [sem(f"packed{i}") for i in range(2)]
    s_S = sem("scores")
    s_nm = sem("negmax")
    s_sub = sem("scores_less_max")
    s_exp = sem("exp")
    s_zt = sem("z_tree")
    s_z = sem("z")
    s_zi = sem("zinv")
    s_p = sem("probs")
    s_av = sem("av")
    s_oT = sem("oT")
    s_Y = sem("Y")
    s_r = sem("resid")
    s_st = sem("stats_done")
    s_rs = sem("rstd")
    s_n = sem("normed")
    s_out = [sem(f"stored{i}") for i in range(2)]

    PACKED = 16 * 2 * len(TERMS)
    T_AT, Q_AT, K_AT, V_AT = 5, 6, 7, 8
    LAST_LAG = 6

    block = ctx.enter_context(nc.Block())

    def sequences(engine, one):
        one(0, 0, 0)
        with engine.Fori(0, (SEQS - 2) // 2) as i:
            one(2 * i + 1, 1, i)
            one(2 * i + 2, 0, i + 1)
        one(SEQS - 1, 1, SEQS // 2 - 1)
        one(SEQS, 0, SEQS // 2)

    def units_of(n):
        return range(UNITS if exists(n) else LAST_LAG + 1)

    @block.sync
    def _(sp):
        def load_x(n, par):
            sp.dma_start(x_tok[par][:], x_in[bass.ts(n, 1), :, :].rearrange("a (t p) c -> p (a t) c", p=P)
                         ).then_inc(s_x[par], 16)

        def pack(n, par, which):
            sp.wait_ge(s_low, 2 * n + which + 1)
            for t, (of_k, of_q) in enumerate(TERMS):
                part = of_k if which else of_q
                sp.dma_start(qk8[par][which][16 * t:16 * t + 16], parts[which][:, part]).then_inc(s_pack[par], 16)

        for dst, name in ((wq, "Wq"), (wk, "Wk"), (wv, "Wv"), (wo, "Wo")):
            sp.dma_start(dst[:], w[name].rearrange("(k p) o -> p k o", p=P)).then_inc(s_w, 16)
        sp.dma_start(bq[:], w["bq"]).then_inc(s_w, 16)
        sp.dma_start(bk[:], w["bk"]).then_inc(s_w, 16)
        sp.dma_start(bv_rows[:], w["bv"].partition_broadcast(P)).then_inc(s_w, 16)
        sp.dma_start(bo_row[:], w["bo"].unsqueeze(0)).then_inc(s_w, 16)
        load_x(0, 0)
        if W0 is not None:
            start_layer_loads(sp, W0, w, 0, s_w0)
        pack(0, 0, 0)
        pack(0, 0, 1)

        def one(n, par, r):
            for u in units_of(n):
                if u == LAST_LAG - 2 and exists(n) and exists(n + 1):
                    need(sp, s_r, TILES * n)
                    load_x(n + 1, 1 - par)
                if u == K_AT + 2 and exists(n) and exists(n + 1):
                    pack(n + 1, 1 - par, 0)
                    pack(n + 1, 1 - par, 1)
                nn, back, uu = lagged(n, u, 6, UNITS)
                if uu % TILES == TILES - 1 and exists(nn):
                    qt = uu // TILES
                    sp.wait_ge(s_n, TILES * nn + qt + 1)
                    sp.dma_start(x_out[bass.ts(nn, 1), qt * P:(qt + 1) * P, :].rearrange("a p c -> p (a c)"),
                                 normed[qt % 2][:]).then_inc(s_out[qt % 2], 16)

        sequences(sp, one)
        for i in range(2):
            sp.wait_ge(s_out[i], 16 * SEQS * TILES // 2)
        if W0 is not None:
            sp.wait_ge(s_w0, 16 * LAYER_LOADS)

    @block.gpsimd
    def _(pool):
        def split(n, which):
            pool.wait_ge(s_pv, 6 * n + 4 + 2 * which)
            nc.gpsimd.tensor_tensor(qk32[which][:], qk32[which][:], parts[which][:, 0], ALU.subtract
                                    ).then_inc(s_rest, 1)

        def split_low(n, which):
            pool.wait_ge(s_mid, 2 * n + which + 1)
            nc.gpsimd.tensor_tensor(parts[which][:, 2], qk32[which][:], parts[which][:, 1], ALU.subtract
                                    ).then_inc(s_low, 1)

        def sum_heads(n, u):
            U = UNITS * n + u
            e = probs[u % NE]
            pool.wait_ge(s_exp, U + 1)
            nc.gpsimd.tensor_tensor(z8[:], e[:, 0:8], e[:, 8:16], ALU.add).then_inc(s_zt, 1)
            pool.wait_ge(s_zt, 3 * U + 1)
            nc.gpsimd.tensor_tensor(z4[:], z8[:, 0:4], z8[:, 4:8], ALU.add).then_inc(s_zt, 1)
            pool.wait_ge(s_zt, 3 * U + 2)
            nc.gpsimd.tensor_tensor(z2[:], z4[:, 0:2], z4[:, 2:4], ALU.add).then_inc(s_zt, 1)
            pool.wait_ge(s_zt, 3 * U + 3)
            need(pool, s_zi, U - 1)
            nc.gpsimd.tensor_tensor(zsum[u % 2][:], z2[:, 0], z2[:, 1], ALU.add).then_inc(s_z, 1)

        def rstd_of(n, qt):
            m = TILES * n + qt
            pool.wait_ge(s_st, 3 * m + 3)
            need(pool, s_n, m - 1)
            nc.gpsimd.tensor_tensor(rstd[qt % 2][:], vareps[qt % 2][:], half[:, 0:1], ALU.pow).then_inc(s_rs, 1)

        for i in range(2):
            nc.gpsimd.memset(v_pad[i][:], 0.0).then_inc(s_pz, 1)
        split(0, 0)
        split(0, 1)
        split_low(0, 0)
        split_low(0, 1)

        def one(n, par, r):
            for u in units_of(n):
                nn, back, uu = lagged(n, u, 5, UNITS)
                if exists(n) and exists(n + 1):
                    if u == Q_AT + 1:
                        split(n + 1, 0)
                    if u == K_AT + 1:
                        split(n + 1, 1)
                        split_low(n + 1, 0)
                    if u == K_AT + 2:
                        split_low(n + 1, 1)
                if exists(n):
                    sum_heads(n, u)
                if uu % TILES == TILES - 1 and exists(nn):
                    rstd_of(nn, uu // TILES)

        sequences(pool, one)

    @block.scalar
    def _(act):
        def evacuate_xT(n):
            for ct in range(CT):
                act.wait_ge(s_pt, 8 * n + ct + 1)
                nc.scalar.activation(xT[:, ct], B[ct][:], ACT.Copy).then_inc(s_pv, 1)

        def evacuate_qk(n, which):
            bias, scale = ((bq_scaled, HDIM ** -0.5), (bk, 1.0))[which]
            for ot in range(CT):
                act.wait_ge(s_pt, 8 * n + 3 + 2 * which + ot)
                nc.scalar.activation(qk32[which][:, ot], B[ot][:], ACT.Identity, bias=bias[:, ot:ot + 1], scale=scale)
                nc.scalar.activation(parts[which][:, 0, ot], B[ot][:], ACT.Identity, bias=bias[:, ot:ot + 1],
                                     scale=scale).then_inc(s_pv, 1)

        def middle(n, which):
            act.wait_ge(s_rest, 2 * n + which + 1)
            nc.scalar.activation(parts[which][:, 1], qk32[which][:], ACT.Copy).then_inc(s_mid, 1)

        act.wait_ge(s_w, 16 * 8)
        nc.scalar.mul(bq_scaled[:], bq[:], HDIM ** -0.5).then_inc(s_bqs, 1)
        act.wait_ge(s_bqs, 1)
        evacuate_xT(0)
        evacuate_qk(0, 0)
        evacuate_qk(0, 1)
        middle(0, 0)
        middle(0, 1)

        def one(n, par, r):
            for u in units_of(n):
                if exists(n):
                    U = UNITS * n + u
                    act.wait_ge(s_sub, U + 1)
                    need(act, s_av, U - NE + 1)
                    nc.scalar.activation(probs[u % NE][:], S[:], ACT.Exp).then_inc(s_exp, 1)
                nn, back, uu = lagged(n, u, 3, UNITS)
                if uu % TILES == TILES - 1 and exists(nn):
                    qt = uu // TILES
                    act.wait_ge(s_av, UNITS * nn + uu + 1)
                    need(act, s_Y, TILES * nn + qt - 1)
                    nc.scalar.activation(oT[qt % 2][:], O[:], ACT.Copy).then_inc(s_oT, 1)
                if exists(n) and exists(n + 1):
                    if u == T_AT:
                        evacuate_xT(n + 1)
                    if u == Q_AT:
                        evacuate_qk(n + 1, 0)
                    if u == K_AT:
                        evacuate_qk(n + 1, 1)
                    if u == K_AT + 1:
                        middle(n + 1, 0)
                    if u == K_AT + 2:
                        middle(n + 1, 1)

        sequences(act, one)

    @block.vector
    def _(dve):
        def evacuate_v(n, par):
            need(dve, s_av, UNITS * (n - 1))
            for j in range(2):
                dve.wait_ge(s_pt, 8 * n + 7 + j)
                src = B[j][:].rearrange("p (t h e d) -> p t h e d", t=2, e=2, d=HDIM)
                bias = bv_rows[:].rearrange("p (h e d) -> p h e d", e=2, d=HDIM)
                for e in range(2):
                    last = nc.vector.tensor_tensor(
                        v_pad[par][:, 2 * j:2 * j + 2, :, 48 * e:48 * e + HDIM], src[:, :, :, e],
                        bias[:, :, e].unsqueeze(1).to_broadcast([P, 2, HEADS // 2, HDIM]), ALU.add)
                last.then_inc(s_vv, 1)

        dve.wait_ge(s_w, 16 * 8)
        dve.wait_ge(s_pz, 2)
        evacuate_v(0, 0)

        def one(n, par, r):
            for u in units_of(n):
                if exists(n):
                    U = UNITS * n + u
                    dve.wait_ge(s_S, U + 1)
                    need(dve, s_sub, U - 1)
                    nc.vector.tensor_reduce(out=negmax[u % 2][:], in_=S[:].rearrange("p h q -> p q h"),
                                            axis=AX.X, op=ALU.max, negate=True).then_inc(s_nm, 1)
                nn, back, uu = lagged(n, u, 2, UNITS)
                if exists(nn):
                    U = UNITS * nn + uu
                    dve.wait_ge(s_z, U + 1)
                    nc.vector.reciprocal(zinv[uu % 2][:], zsum[uu % 2][:]).then_inc(s_zi, 1)
                    dve.wait_ge(s_zi, U + 1)
                    e = probs[uu % NE]
                    nc.vector.tensor_tensor(e[:], e[:], zinv[uu % 2][:].unsqueeze(1).to_broadcast([P, HEADS, P]),
                                            ALU.mult).then_inc(s_p, 1)
                nn, back, uu = lagged(n, u, 6, UNITS)
                if uu % TILES == TILES - 1 and exists(nn):
                    qt = uu // TILES
                    m = TILES * nn + qt
                    rn = r if not back else (r if par else r - 1)
                    dve.wait_ge(s_rs, m + 1)
                    need(dve, s_out[qt % 2], 16 * (2 * nn + qt // 2))
                    nc.vector.tensor_scalar(normed[qt % 2][:], resid[qt % 2][:], mv[qt % 2][:, 0:1],
                                            rstd[qt % 2][:, 0:1], ALU.subtract, ALU.mult).then_inc(s_n, 1)
                nn, back, uu = lagged(n, u, 5, UNITS)
                if uu % TILES == TILES - 1 and exists(nn):
                    qt = uu // TILES
                    m = TILES * nn + qt
                    pn = par if not back else 1 - par
                    dve.wait_ge(s_Y, m + 1)
                    nc.vector.tensor_tensor(resid[qt % 2][:], Y[:], x_tok[pn][:, qt], ALU.add).then_inc(s_r, 1)
                    dve.wait_ge(s_r, m + 1)
                    nc.vector.bn_stats(stats[:], resid[qt % 2][:]).then_inc(s_st, 1)
                    dve.wait_ge(s_st, 3 * m + 1)
                    nc.vector.memset(carrier[:], 0.0)
                    nc.vector.bn_aggr(mv[qt % 2][:], stats[:]).then_inc(s_st, 1)
                    dve.wait_ge(s_st, 3 * m + 2)
                    nc.vector.tensor_scalar(vareps[qt % 2][:], mv[qt % 2][:, 1:2], EPS, None, ALU.add).then_inc(s_st, 1)
                if u == V_AT and exists(n) and exists(n + 1):
                    evacuate_v(n + 1, 1 - par)

        sequences(dve, one)

    @block.tensor
    def _(pe):
        def piece_free(n, piece):
            if piece < 2:
                need(pe, s_vv, 2 * n - 1 + piece)
            else:
                pe.wait_ge(s_pv, 6 * n + piece - 1)

        def transpose_x(n, par):
            for ct in range(CT):
                piece_free(n, ct)
                for t in range(TILES):
                    last = nc.tensor.transpose(B[ct][:, t * P:(t + 1) * P], x_tok[par][:, t, ct * P:(ct + 1) * P], ident[:])
                last.then_inc(s_pt, 1)

        def project_qk(n, which):
            for ot in range(CT):
                piece_free(n, 2 + 2 * which + ot)
                if which == 0:
                    pe.wait_ge(s_pv, 6 * n + 2)
                for k in range(CT):
                    last = nc.tensor.matmul(B[ot][:], (wq, wk)[which][:, k, ot * P:(ot + 1) * P], xT[:, k],
                                            start=(k == 0), stop=(k == CT - 1))
                last.then_inc(s_pt, 1)

        def project_v(n):
            for j in range(2):
                piece_free(n, 6 + j)
                for t in range(2):
                    for k in range(CT):
                        last = nc.tensor.matmul(B[j][:, t * CH:(t + 1) * CH],
                                                xT[:, k, (2 * j + t) * P:(2 * j + t + 1) * P], wv[:, k],
                                                start=(k == 0), stop=(k == CT - 1))
                last.then_inc(s_pt, 1)

        pe.wait_ge(s_w, 16 * 8)
        pe.wait_ge(s_x[0], 16)
        transpose_x(0, 0)
        project_qk(0, 0)
        project_qk(0, 1)
        project_v(0)

        def one(n, par, r):
            for u in units_of(n):
                if exists(n):
                    U = UNITS * n + u
                    if u == 0:
                        pe.wait_ge(s_pack[par], PACKED * (r + 1))
                    need(pe, s_exp, U)
                    qt, kt = u // TILES, u % TILES
                    q8, k8 = qk8[par]
                    for h in range(HEADS):
                        last = nc.tensor.matmul(S[:, h], k8[:, h % JH, h // JH, kt * P:(kt + 1) * P],
                                                q8[:, h % JH, h // JH, qt * P:(qt + 1) * P],
                                                start=(h % 4 == 0), stop=(h % 4 == 3))
                    last.then_inc(s_S, 1)
                nn, back, uu = lagged(n, u, 3, UNITS)
                if exists(nn):
                    qt, kt = uu // TILES, uu % TILES
                    pn = par if not back else 1 - par
                    if kt == 0:
                        need(pe, s_oT, TILES * nn + qt)
                    pe.wait_ge(s_p, UNITS * nn + uu + 1)
                    if uu == 0:
                        pe.wait_ge(s_vv, 2 * nn + 2)
                    for t in range(CT):
                        for e in range(2):
                            for g in range(4):
                                last = nc.tensor.matmul(
                                    O[32 * g:32 * g + 32, t], v_pad[pn][:, kt, 4 * t + g, 32 * e:32 * e + 32],
                                    probs[uu % NE][:, JH * t + 2 * g + e], start=(kt == 0 and t == 0 and e == 0),
                                    stop=(kt == TILES - 1 and e == 1 and t == 1), tile_position=(0, 32 * g),
                                    skip_group_check=True)
                    last.then_inc(s_av, 1)
                nn, back, uu = lagged(n, u, 4, UNITS)
                if uu % TILES == TILES - 1 and exists(nn):
                    qt = uu // TILES
                    m = TILES * nn + qt
                    pe.wait_ge(s_oT, m + 1)
                    need(pe, s_r, m)
                    nc.tensor.matmul(Y[:], ones_row[0:1, :], bo_row[0:1, :], start=True, stop=False)
                    for k in range(CT):
                        last = nc.tensor.matmul(Y[:], oT[qt % 2][:, k], wo[:, k], start=False, stop=(k == CT - 1))
                    last.then_inc(s_Y, 1)
                if exists(n) and exists(n + 1):
                    if u == T_AT:
                        pe.wait_ge(s_x[1 - par], 16 * (r + 1 + par))
                        transpose_x(n + 1, 1 - par)
                    if u == Q_AT:
                        project_qk(n + 1, 0)
                    if u == K_AT:
                        project_qk(n + 1, 1)
                    if u == V_AT:
                        project_v(n + 1)
                if exists(n):
                    U = UNITS * n + u
                    pe.wait_ge(s_nm, U + 1)
                    for b in range(4):
                        last = nc.tensor.matmul(S[:, 4 * b:4 * b + 4], identr[:],
                                                negmax[u % 2][:].unsqueeze(1).to_broadcast([P, 4, P]),
                                                start=False, stop=True, skip_group_check=True)
                    last.then_inc(s_sub, 1)

        sequences(pe, one)


def make_constants(nc, ctx):
    def sb(name, shape, dtype=F32):
        return ctx.enter_context(nc.sbuf_tensor("c_" + name, shape, dtype))

    c = {"ident": sb("ident", [P, P]), "identr": sb("identr", [P, P], F32R),
         "identb": sb("identb", [P, P], BF16),
         "minus_half": sb("half", [P, 16]), "ones_row": sb("ones", [1, P])}
    s_i = ctx.enter_context(nc.semaphore("c_identity"))
    with nc.Block() as block:
        @block.gpsimd
        def _(pool):
            nc.gpsimd.memset(c["minus_half"][:], -0.5).then_inc(s_i, 1)
            nc.gpsimd.memset(c["ones_row"][:], 1.0).then_inc(s_i, 1)
            nc.gpsimd.memset(c["ident"][:], 0.0).then_inc(s_i, 1)
            pool.wait_ge(s_i, 3)
            nc.gpsimd.affine_select(out=c["ident"][:], in_=c["ident"][:], compare_op=ALU.not_equal, fill=1.0, base=0,
                                    pattern=[[-1, P]], channel_multiplier=1).then_inc(s_i, 1)

        @block.vector
        def _(dve):
            dve.wait_ge(s_i, 4)
            nc.vector.tensor_copy(c["identr"][:], c["ident"][:]).then_inc(s_i, 1)
            nc.vector.tensor_copy(c["identb"][:], c["ident"][:]).then_inc(s_i, 1)
            dve.wait_ge(s_i, 6)
    return c


LAYERS = 2
LHEADS, LDIM = 8, 64
INNER = LHEADS * LDIM
HID = int(CH * 4 * 2 / 3)
CHUNKS = -(-HID // P)
LAST = HID - (CHUNKS - 1) * P
ALL_SEQS = LAYERS * SEQS
ALL_TILES = ALL_SEQS * TILES
MASKED = -1e30
PAIRS = INNER // P
IH = INNER // P


def layer_of(n):
    return n // SEQS


def load_layer(nc, ctx, tag):
    def sb(name, shape, dtype=F32):
        return ctx.enter_context(nc.sbuf_tensor(f"w{tag}_" + name, shape, dtype))

    return {"qkv": sb("qkv", [P, CT, 3 * INNER]), "o": sb("o", [P, IH, CH]),
            "w1": sb("w1", [P, CT, 2 * HID]), "w2": sb("w2", [P, CHUNKS, CH]),
            "b1": sb("b1", [P, 2, CHUNKS]), "ln_g": sb("g", [P, CT]), "ln_b": sb("b", [P, CT])}


LAYER_LOADS = 9


def start_layer_loads(engine, dst, w, layer, sem):
    full = (CHUNKS - 1) * P
    def load(out, src):
        engine.dma_start(out, src).then_inc(sem, 16)

    load(dst["qkv"][:], w["wqkv"][layer].rearrange("(k p) o -> p k o", p=P))
    load(dst["o"][:], w["wo2"][layer].rearrange("(k p) o -> p k o", p=P))
    load(dst["w1"][:], w["w1"][layer].rearrange("(k p) o -> p k o", p=P))
    load(dst["w2"][:, 0:CHUNKS - 1], w["w2"][layer, 0:full].rearrange("(k p) o -> p k o", p=P))
    load(dst["w2"][0:LAST, CHUNKS - 1], w["w2"][layer, full:HID])
    load(dst["w2"][LAST:LAST + 1, CHUNKS - 1], w["b2"][layer:layer + 1])
    for name in ("b1", "ln_g", "ln_b"):
        load(dst[name][:], w[name][layer])


def layers(nc, ctx, x_a, x_b, y_out, w, W, consts):
    ident, half, identb = consts["ident"], consts["minus_half"], consts["identb"]

    def sb(name, shape, dtype=F32):
        return ctx.enter_context(nc.sbuf_tensor("b_" + name, shape, dtype))

    def sem(name):
        return ctx.enter_context(nc.semaphore("b_" + name))

    def bank(name, shape=(P, 512)):
        return ctx.enter_context(nc.psum_tensor("b_" + name, list(shape), F32))

    x_tok = [sb(f"x{i}", [P, TILES, CH]) for i in range(2)]
    x2 = [sb(f"x2{i}", [P, TILES, CH]) for i in range(2)]
    base_tab = sb("base_tab", [P, TILES, 4, LDIM])
    tab = [sb(f"tab{i}", [P, TILES, 4, LDIM]) for i in range(LAYERS)]
    srow = [sb(f"srow{i}", [P, 4, LDIM]) for i in range(LAYERS)]
    mask = [sb(f"mask{i}", [P, 2, P], BF16) for i in range(2)]
    zero_col = sb("zero_col", [P, 1])
    carrier = sb("carrier", [P, 1])
    hT0 = [sb(f"hT0{i}", [P, P]) for i in range(2)]
    hT1 = [sb(f"hT1{i}", [P, P + 1]) for i in range(2)]
    sq = sb("sq", [P, 2, LHEADS, LDIM])
    t1 = [sb(f"t1{i}", [P, LHEADS, LDIM]) for i in range(2)]
    t2 = [sb(f"t2{i}", [P, LHEADS, LDIM]) for i in range(2)]
    q_rot, k_sum, k_rot = (sb(n, [P, LHEADS, LDIM]) for n in ("q_rot", "k_sum", "k_rot"))
    ss = sb("ss", [P, 2 * LHEADS])
    ssc = sb("ssc", [P, 2 * LHEADS])
    rn = [sb(f"rn{i}", [P, 2 * LHEADS]) for i in range(2)]
    qT = sb("qT", [P, PAIRS, P])
    kT = sb("kT", [P, PAIRS, 2, P])
    v = sb("v", [P, TILES, INNER])
    mx = sb("mx", [P, 4])
    nb = [sb(f"nb{i}", [P, 4]) for i in range(2)]
    probs = [sb(f"p{i}", [P, 4, 2 * P]) for i in range(2)]
    rs = [sb(f"rs{i}", [P, LHEADS]) for i in range(2)]
    rinv = sb("rinv", [P, LHEADS])
    PT = [sb(f"PT{i}", [P, 4, 2 * P]) for i in range(2)]
    o_n = sb("o_n", [P, INNER])
    oT = sb("oT", [P, IH, P])
    hs = sb("hs", [P, TILES, P])
    stats = sb("stats", [P, 2, 6])
    mv, ve, rstd = ([sb(f"{n}{i}", [P, 2]) for i in range(2)] for n in ("mv", "ve", "rstd"))
    hn = sb("hn", [P, CH])
    hnT = sb("hnT", [P, CT, SEQ])
    a_sb = [sb(f"a{i}", [P, CHUNKS, 2 * P]) for i in range(2)]
    g_sb = [sb(f"g{i}", [P, CHUNKS, 2 * P]) for i in range(2)]
    xo = [sb(f"xo{i}", [P, 2, CH]) for i in range(2)]
    x0 = [sb(f"x0{i}", [P, 2, CH]) for i in range(2)]
    fstats = sb("fstats", [P, 2, 6])
    fmv, fve, frstd = (sb(n, [P, 2, 2]) for n in ("fmv", "fve", "frstd"))
    y = [sb(f"y{i}", [P, 2, CH]) for i in range(2)]

    X = [bank(f"X{i}") for i in range(3)]
    SB = bank("S", (P, 4, 2 * P))
    M = bank("M")
    F = [bank(f"F{i}", (P, 2, 2 * P)) for i in range(2)]

    s_w = sem("weights")
    s_c = sem("constants")
    s_tab = sem("tables")
    s_x = [sem(f"x_loaded{i}") for i in range(2)]
    s_x0 = [sem(f"x0_loaded{i}") for i in range(2)]
    s_hT = sem("hT")
    s_hTe = sem("hT_evacuated")
    s_q, s_k, s_v = sem("q"), sem("k"), sem("v")
    s_sq = sem("squares")
    s_ve = sem("v_evacuated")
    s_rot = sem("rot_products")
    s_ss = sem("sums_of_squares")
    s_qr = sem("q_rotated")
    s_ks = sem("k_sum")
    s_rn = sem("norms")
    s_kr = sem("k_rotated")
    s_qkT = sem("qkT")
    s_qkTe = sem("qkT_evacuated")
    s_S = sem("scores")
    s_mx = sem("row_max")
    s_nb = sem("exp_bias")
    s_pr = sem("probs")
    s_PT = sem("probs_transposed")
    s_PTe = sem("PT_evacuated")
    s_AV = sem("av")
    s_ri = sem("row_sums_inverted")
    s_on = sem("o_normalised")
    s_oT = sem("oT")
    s_oTe = sem("oT_evacuated")
    s_wo = sem("o_projected")
    s_x2 = sem("x2")
    s_sh = [sem(f"shifted{i}") for i in range(TILES)]
    s_st = sem("ln_stats")
    s_rs = sem("ln_rstd")
    s_hn = sem("ln_normed")
    s_F = sem("F")
    s_Fg = sem("F_gate")
    s_Fa = sem("F_value")
    s_ge = sem("gelu")
    s_um = sem("gated")
    s_w2 = sem("w2")
    s_xo = sem("xo")
    s_fs = sem("final_stats")
    s_fr = sem("final_rstd")
    s_y = sem("y")
    s_stored = [sem(f"stored{i}") for i in range(2)]

    WEIGHTS = 16 * (LAYER_LOADS + 1 + 8)

    block = ctx.enter_context(nc.Block())

    def tile_exists(t):
        return not isinstance(t, int) or 0 <= t < ALL_TILES

    def seq_exists(n):
        return not isinstance(n, int) or 0 <= n < ALL_SEQS

    def sequences(engine, one):
        def peeled(n):
            one(n, n % 2, n // 2, lambda d: (n + d) // SEQS)

        for n in range(4):
            peeled(n)
        for layer, first, end in ((0, 4, SEQS - 2), (1, SEQS + 2, 2 * SEQS - 2)):
            with engine.Fori(0, (end - first) // 2) as i:
                for j in range(2):
                    one(2 * i + (first + j), j, i + first // 2, lambda d: layer)
            for n in range(end, end + 4):
                peeled(n)

    def back(n, w, lag):
        return (n, w - lag) if w >= lag else (n - 1, w - lag + TILES)

    @block.sync
    def _(sp):
        def load_x(n, par, r, layer):
            src = x_a if layer == 0 else x_b
            s = n - layer * SEQS
            sp.dma_start(x_tok[par][:], src[bass.ts(s, 1), :, :].rearrange("a (t p) c -> p (a t) c", p=P)
                         ).then_inc(s_x[par], 16)

        start_layer_loads(sp, W[1], w, 1, s_w)
        sp.dma_start(base_tab[:], w["tab"].rearrange("(t p) k d -> p t k d", p=P)).then_inc(s_w, 16)
        H = LDIM // 2
        for layer in range(LAYERS):
            for i, name in enumerate(("q_scale", "k_scale")):
                row = w[name][layer]
                sp.dma_start(srow[layer][:, 2 * i], row.partition_broadcast(P)).then_inc(s_w, 16)
                swapped = w[name + "_swapped"][layer]
                sp.dma_start(srow[layer][:, 2 * i + 1], swapped.partition_broadcast(P)).then_inc(s_w, 16)
        load_x(0, 0, 0, 0)

        def one(n, par, r, layer):
            for w_ in range(TILES):
                T = TILES * n + w_
                if w_ == 1 and seq_exists(n + 1) and seq_exists(n):
                    need(sp, s_x2, TILES * n)
                    if isinstance(n, int) and SEQS <= n + 1 <= SEQS + 2:
                        for h in range(2):
                            sp.wait_ge(s_stored[h], 16 * (n - SEQS + 2 if n + 1 < SEQS + 2 else SEQS))
                    load_x(n + 1, 1 - par, None, layer(1))
                n1, w1 = back(n, w_, 1)
                if tile_exists(T - 1):
                    p1 = par if w_ >= 1 else 1 - par
                    sp.wait_ge(s_x2, T)
                    src = x2[p1][:, w1, P:CH]
                    for lo, hi in ((0, 112), (112, 127)):
                        sp.dma_start(hs[lo + 1:hi + 1, w1], src[lo:hi]).then_inc(s_sh[w1], 16)
                    if w1 < TILES - 1:
                        sp.dma_start(hs[0:1, w1 + 1], src[127:128]).then_inc(s_sh[w1], 16)
                if w_ % 2 == 0:
                    h, d = (1, 2) if w_ == 0 else (0, 1)
                    m = n - d
                    if seq_exists(m):
                        if layer(-d) == LAYERS - 1:
                            sp.wait_ge(s_y, 2 * (m - SEQS) + h + 1)
                            dst, src, s = y_out, y[h], m - SEQS
                        else:
                            sp.wait_ge(s_xo, 2 * m + h + 1)
                            dst, src, s = x_b, xo[h], m
                        sp.dma_start(dst[bass.ts(s, 1), h * 2 * P:(h + 1) * 2 * P, :].rearrange("a (t p) c -> p (a t) c", p=P),
                                     src[:]).then_inc(s_stored[h], 16)
                if w_ % 2 == 1:
                    h, d = (0, 1) if w_ == 1 else (1, 1)
                    m = n - d
                    if seq_exists(m) and layer(-d) == LAYERS - 1:
                        if not (isinstance(m, int) and m == SEQS):
                            sp.wait_ge(s_fs, 6 * (2 * (m - SEQS - 1) + h) + 1)
                        sp.dma_start(x0[h][:], x_a[bass.ts(m - SEQS, 1), h * 2 * P:(h + 1) * 2 * P, :]
                                     .rearrange("a (t p) c -> p (a t) c", p=P)).then_inc(s_x0[h], 16)
                if isinstance(n, int) and n == ALL_SEQS + 1:
                    break

        sequences(sp, one)
        for h in range(2):
            sp.wait_ge(s_stored[h], 16 * ALL_SEQS)

    @block.gpsimd
    def _(pool):
        def rotate(t):
            pool.wait_ge(s_rot, 2 * t + 1)
            need(pool, s_qkT, 2 * t - 1)
            nc.gpsimd.tensor_tensor(q_rot[:], t1[0][:], t2[0][:], ALU.add).then_inc(s_qr, 1)
            pool.wait_ge(s_rot, 2 * t + 2)
            need(pool, s_kr, t)
            nc.gpsimd.tensor_tensor(k_sum[:], t1[1][:], t2[1][:], ALU.add).then_inc(s_ks, 1)

        def norms(t, p):
            pool.wait_ge(s_ss, 2 * t + 2)
            need(pool, s_pr, 2 * t - 2)
            nc.gpsimd.tensor_tensor(rn[p][:], ssc[:], half[:], ALU.pow).then_inc(s_rn, 1)

        nc.gpsimd.memset(zero_col[:], 0.0).then_inc(s_c, 1)
        for i in range(2):
            nc.gpsimd.memset(hT1[i][:], 0.0).then_inc(s_c, 1)
            nc.gpsimd.memset(a_sb[i][:], 1.0).then_inc(s_c, 1)
            nc.gpsimd.memset(mask[i][:], 0.0).then_inc(s_c, 1)
        nc.gpsimd.memset(hs[:], 0.0).then_inc(s_c, 1)
        pool.wait_ge(s_c, 8)
        for i in range(2):
            nc.gpsimd.affine_select(out=mask[i][:, i], in_=mask[i][:, i], compare_op=ALU.is_ge, fill=MASKED, base=0,
                                    pattern=[[-1, P]], channel_multiplier=1).then_inc(s_c, 1)
            nc.gpsimd.affine_select(out=mask[i][:, 1 - i], in_=mask[i][:, 1 - i], compare_op=ALU.is_ge, fill=MASKED,
                                    base=0, pattern=[[1, P]], channel_multiplier=-1).then_inc(s_c, 1)
        rotate(0)
        norms(0, 0)

        def one(n, par, r, layer):
            for w_ in range(TILES):
                T = TILES * n + w_
                if w_ % 2 == 0:
                    h, d = (1, 2) if w_ == 0 else (0, 1)
                    m = n - d
                    if seq_exists(m):
                        pool.wait_ge(s_ge, 2 * m + h + 1)
                        pool.wait_ge(s_Fa, 3 * (TILES * m + 2 * h + 2))
                        nc.gpsimd.tensor_tensor(a_sb[h][:, 0:CHUNKS - 1], a_sb[h][:, 0:CHUNKS - 1],
                                                g_sb[h][:, 0:CHUNKS - 1], ALU.mult)
                        nc.gpsimd.tensor_tensor(a_sb[h][0:LAST, CHUNKS - 1], a_sb[h][0:LAST, CHUNKS - 1],
                                                g_sb[h][0:LAST, CHUNKS - 1], ALU.mult).then_inc(s_um, 1)
                if tile_exists(T + 1):
                    rotate(T + 1)
                    norms(T + 1, (w_ + 1) % 2)
                if tile_exists(T - 1):
                    p = (w_ + 1) % 2
                    pool.wait_ge(s_st, 4 * (T - 1) + 4)
                    need(pool, s_hn, T - 2)
                    nc.gpsimd.tensor_tensor(rstd[p][:, 0:1], ve[p][:, 0:1], half[:, 0:1], ALU.pow).then_inc(s_rs, 1)
                if w_ % 2 == 0:
                    if seq_exists(m) and layer(-d) == LAYERS - 1:
                        j = 2 * (m - SEQS) + h
                        pool.wait_ge(s_fs, 6 * j + 6)
                        nc.gpsimd.tensor_tensor(frstd[:, :, 0], fve[:, :, 0], half[:, 0:2], ALU.pow).then_inc(s_fr, 1)
                if isinstance(n, int) and n == ALL_SEQS + 1:
                    break

        sequences(pool, one)

    @block.scalar
    def _(act):
        def evacuate_hT(T, n, w_, layer):
            act.wait_ge(s_hT, T + 2)
            if tile_exists(T + 1):
                p = (w_ + 1) % 2
                nc.scalar.activation(hT0[p][:], X[2][:, 0:P], ACT.Copy)
                nc.scalar.activation(hT1[p][:, 1:P + 1], X[2][:, P:2 * P], ACT.Copy)
                last_col = zero_col[:] if (w_ + 1) % TILES == TILES - 1 else X[2][:, 2 * P - 1:2 * P]
                last = nc.scalar.activation(hT1[1 - p][:, 0:1], last_col, ACT.Copy)
            if tile_exists(T - 2):
                n2, w2_ = back(n, w_, 2)
                W2 = W[layer(0 if w_ >= 2 else -1)]
                for ct in range(CT):
                    last = nc.scalar.activation(hnT[:, ct, w2_ * P:(w2_ + 1) * P], X[2][:, (2 + ct) * P:(3 + ct) * P],
                                                ACT.Identity, bias=W2["ln_b"][:, ct:ct + 1], scale=W2["ln_g"][:, ct:ct + 1])
            last.then_inc(s_hTe, 1)

        def squares_and_v(t, w_):
            act.wait_ge(s_q, t + 1)
            need(act, s_ss, 2 * t - 1)
            nc.scalar.activation(sq[:, 0], X[0][:], ACT.Square).then_inc(s_sq, 1)
            act.wait_ge(s_k, t + 1)
            nc.scalar.activation(sq[:, 1], X[1][:], ACT.Square).then_inc(s_sq, 1)
            act.wait_ge(s_v, t + 1)
            need(act, s_AV, t - 2)
            nc.scalar.activation(v[:, w_], X[2][:], ACT.Copy).then_inc(s_ve, 1)

        def gate(T, i, w_, layer):
            c = 3 * (w_ % 2) + i
            rows = P if c < CHUNKS - 1 else LAST
            act.wait_ge(s_F, 3 * (T - TILES) + i + 1)
            nc.scalar.activation(g_sb[w_ // 2][0:rows, c], F[i % 2][0:rows, 1], ACT.Identity,
                                 bias=W[layer(-1)]["b1"][0:rows, 1, c:c + 1]).then_inc(s_Fg, 1)

        act.wait_ge(s_w, WEIGHTS)
        act.wait_ge(s_c, 12)
        evacuate_hT(-1, -1, 3, lambda d: 0)
        squares_and_v(0, 0)

        def one(n, par, r, layer):
            for w_ in range(TILES):
                T = TILES * n + w_
                p = w_ % 2
                live, feed = tile_exists(T), seq_exists(n - 1)
                if live:
                    act.wait_ge(s_qkT, 2 * T + 1)
                    nc.scalar.activation(qT[:], X[0][:], ACT.Copy).then_inc(s_qkTe, 1)
                    act.wait_ge(s_qkT, 2 * T + 2)
                    nc.scalar.activation(kT[:, :, p], X[1][:].rearrange("p (b q) -> p b q", q=P), ACT.Copy
                                         ).then_inc(s_qkTe, 1)
                if w_ % 2 == 0:
                    h, d = (1, 2) if w_ == 0 else (0, 1)
                    m = n - d
                    if seq_exists(m):
                        act.wait_ge(s_Fg, 3 * (TILES * m + 2 * h + 2))
                        nc.scalar.activation(g_sb[h][:, 0:CHUNKS - 1], g_sb[h][:, 0:CHUNKS - 1], ACT.Gelu)
                        nc.scalar.activation(g_sb[h][0:LAST, CHUNKS - 1], g_sb[h][0:LAST, CHUNKS - 1], ACT.Gelu
                                             ).then_inc(s_ge, 1)
                if feed:
                    gate(T, 0, w_, layer)
                if tile_exists(T - 1):
                    act.wait_ge(s_oT, T)
                    nc.scalar.activation(oT[:], M[:], ACT.Copy).then_inc(s_oTe, 1)
                if tile_exists(T + 1) or tile_exists(T - 2):
                    evacuate_hT(T, n, w_, layer)
                if live:
                    exps(T, w_, 0)
                if tile_exists(T + 1):
                    squares_and_v(T + 1, (w_ + 1) % TILES)
                if live:
                    act.wait_ge(s_PT, 2 * T + 1)
                    evacuate_PT(w_, 0)
                if feed:
                    gate(T, 1, w_, layer)
                if live:
                    exps(T, w_, 1)
                if feed:
                    gate(T, 2, w_, layer)
                if live:
                    act.wait_ge(s_PT, 2 * T + 2)
                    evacuate_PT(w_, 1)
                if isinstance(n, int) and n == ALL_SEQS + 1:
                    break

        def keys(w_):
            return slice(0, P) if w_ == 0 else slice(0, 2 * P)

        def exps(T, w_, hf):
            act.wait_ge(s_nb, 2 * T + hf + 1)
            for e in range(2):
                for ps in range(2):
                    i, h = 2 * e + ps, 4 * hf + 2 * ps + e
                    last = nc.scalar.activation(probs[hf][:, i, keys(w_)], SB[:, i, keys(w_)], ACT.Exp,
                                                bias=nb[hf][:, i:i + 1], scale=rn[w_ % 2][:, h:h + 1],
                                                accum_out=rs[w_ % 2][:, h:h + 1])
            last.then_inc(s_pr, 1)

        def evacuate_PT(w_, hf):
            nc.scalar.activation(PT[hf][:, :, keys(w_)], SB[:, :, keys(w_)], ACT.Copy).then_inc(s_PTe, 1)

        sequences(act, one)

    @block.vector
    def _(dve):
        def rot_products(t, w_, layer):
            for i in range(2):
                dve.wait_ge(s_sq, 2 * t + i + 1)
                if i == 0:
                    need(dve, s_qr, t)
                else:
                    need(dve, s_ks, t)
                src = X[i][:].rearrange("p (h d) -> p h d", d=LDIM)
                rows = tab[layer][:, w_]
                cos = rows[:, 2 * i].unsqueeze(1).to_broadcast([P, LHEADS, LDIM])
                sin = rows[:, 2 * i + 1].unsqueeze(1).to_broadcast([P, LHEADS, LDIM])
                H = LDIM // 2
                nc.vector.tensor_tensor(t1[i][:], src, cos, ALU.mult)
                nc.vector.tensor_tensor(t2[i][:, :, 0:H], src[:, :, H:LDIM], sin[:, :, 0:H], ALU.mult)
                nc.vector.tensor_tensor(t2[i][:, :, H:LDIM], src[:, :, 0:H], sin[:, :, H:LDIM], ALU.mult
                                        ).then_inc(s_rot, 1)
            nc.vector.tensor_reduce(out=ss[:].rearrange("p (a h) -> p a h", a=2), in_=sq[:], axis=AX.X, op=ALU.add
                                    ).then_inc(s_ss, 1)
            dve.wait_ge(s_ss, 2 * t + 1)
            need(dve, s_rn, t)
            nc.vector.tensor_scalar(ssc[:], ss[:], 1e-24, None, ALU.max).then_inc(s_ss, 1)

        def scale_k(t, p):
            dve.wait_ge(s_rn, t + 1)
            need(dve, s_qkT, 2 * t)
            nc.vector.tensor_tensor(k_rot[:], k_sum[:], rn[p][:, LHEADS:2 * LHEADS].unsqueeze(2)
                                    .to_broadcast([P, LHEADS, LDIM]), ALU.mult).then_inc(s_kr, 1)

        def row_max(T, w_, hf):
            cols = slice(0, P) if w_ == 0 else slice(0, 2 * P)
            dve.wait_ge(s_S, 2 * T + hf + 1)
            nc.vector.tensor_reduce(out=mx[:], in_=SB[:, :, cols], axis=AX.X, op=ALU.max).then_inc(s_mx, 1)
            dve.wait_ge(s_mx, 2 * T + hf + 1)
            nc.vector.scalar_tensor_tensor(
                out=nb[hf][:].rearrange("p (e s) -> p e s", e=2), in0=mx[:].rearrange("p (e s) -> p e s", e=2),
                scalar=-1.0, in1=rn[w_ % 2][:, 4 * hf:4 * hf + 4].rearrange("p (s e) -> p e s", e=2),
                op0=ALU.mult, op1=ALU.mult).then_inc(s_nb, 1)

        def value(T, i, w_, layer):
            c = 3 * (w_ % 2) + i
            rows = P if c < CHUNKS - 1 else LAST
            dve.wait_ge(s_Fg, 3 * (T - TILES) + i + 1)
            nc.vector.tensor_scalar(a_sb[w_ // 2][0:rows, c], F[i % 2][0:rows, 0],
                                    W[layer(-1)]["b1"][0:rows, 0, c:c + 1], None, ALU.add).then_inc(s_Fa, 1)

        dve.wait_ge(s_w, WEIGHTS)
        dve.wait_ge(s_c, 12)
        for layer in range(LAYERS):
            for t in range(TILES):
                nc.vector.tensor_tensor(tab[layer][:, t], base_tab[:, t], srow[layer][:], ALU.mult).then_inc(s_tab, 1)
        dve.wait_ge(s_tab, LAYERS * TILES)
        rot_products(0, 0, 0)
        scale_k(0, 0)

        def one(n, par, r, layer):
            for w_ in range(TILES):
                T = TILES * n + w_
                p = w_ % 2
                live, feed = tile_exists(T), seq_exists(n - 1)
                if tile_exists(T - 1):
                    dve.wait_ge(s_AV, T)
                    nc.vector.reciprocal(rinv[:], rs[1 - p][:]).then_inc(s_ri, 1)
                    dve.wait_ge(s_ri, T)
                    nc.vector.tensor_tensor(o_n[:].rearrange("p (h d) -> p h d", d=LDIM),
                                            M[:].rearrange("p (h d) -> p h d", d=LDIM),
                                            rinv[:].unsqueeze(2).to_broadcast([P, LHEADS, LDIM]), ALU.mult
                                            ).then_inc(s_on, 1)
                if tile_exists(T - 2):
                    n2, w2_ = back(n, w_, 2)
                    p2 = par if w_ >= 2 else 1 - par
                    dve.wait_ge(s_rs, T - 1)
                    need(dve, s_hT, T + 1)
                    nc.vector.tensor_scalar(hn[:, 0:P], x2[p2][:, w2_, 0:P], mv[p][:, 0:1], rstd[p][:, 0:1],
                                            ALU.subtract, ALU.mult)
                    nc.vector.tensor_scalar(hn[:, P:CH], hs[:, w2_], mv[p][:, 0:1], rstd[p][:, 0:1],
                                            ALU.subtract, ALU.mult).then_inc(s_hn, 1)
                if feed:
                    value(T, 0, w_, layer)
                if live:
                    row_max(T, w_, 0)
                if tile_exists(T - 1):
                    n1, w1_ = back(n, w_, 1)
                    p1 = par if w_ >= 1 else 1 - par
                    dve.wait_ge(s_wo, T)
                    nc.vector.tensor_tensor(x2[p1][:, w1_], M[:, 0:CH], x_tok[p1][:, w1_], ALU.add).then_inc(s_x2, 1)
                if tile_exists(T + 1):
                    rot_products(T + 1, (w_ + 1) % TILES, layer(0 if w_ < 3 else 1))
                if feed:
                    value(T, 1, w_, layer)
                if live:
                    row_max(T, w_, 1)
                if tile_exists(T + 1):
                    scale_k(T + 1, 1 - p)
                if feed:
                    value(T, 2, w_, layer)
                if tile_exists(T - 1):
                    q = 1 - p
                    n1_count = n1 + 1
                    dve.wait_ge(s_sh[w1_], (48 if w1_ < TILES - 1 else 32) * n1_count)
                    if w1_ > 0:
                        dve.wait_ge(s_sh[w1_ - 1], 48 * n1_count)
                    nc.vector.bn_stats(stats[:, 0], x2[p1][:, w1_, 0:P]).then_inc(s_st, 1)
                    nc.vector.bn_stats(stats[:, 1], hs[:, w1_]).then_inc(s_st, 1)
                    dve.wait_ge(s_st, 4 * (T - 1) + 2)
                    nc.vector.memset(carrier[:], 0.0)
                    nc.vector.bn_aggr(mv[q][:], stats[:]).then_inc(s_st, 1)
                    dve.wait_ge(s_st, 4 * (T - 1) + 3)
                    nc.vector.tensor_scalar(ve[q][:, 0:1], mv[q][:, 1:2], EPS, None, ALU.add).then_inc(s_st, 1)
                if w_ % 2 == 0:
                    h, d = (1, 2) if w_ == 0 else (0, 1)
                    m = n - d
                    pm = par if d == 2 else 1 - par
                    if seq_exists(m):
                        dve.wait_ge(s_w2, 2 * m + h + 1)
                        if not (isinstance(m, int) and m == 0):
                            dve.wait_ge(s_stored[h], 16 * m)
                        nc.vector.tensor_tensor(xo[h][:], F[1][:], x2[pm][:, 2 * h:2 * h + 2], ALU.add).then_inc(s_xo, 1)
                        if layer(-d) == LAYERS - 1:
                            final(m, h)
                if isinstance(n, int) and n == ALL_SEQS + 1:
                    break

        def final(m, h):
            j = 2 * (m - SEQS) + h
            dve.wait_ge(s_xo, 2 * m + h + 1)
            dve.wait_ge(s_x0[h], 16 * (m - SEQS + 1))
            nc.vector.tensor_tensor(xo[h][:], xo[h][:], x0[h][:], ALU.add).then_inc(s_fs, 1)
            dve.wait_ge(s_fs, 6 * j + 1)
            for t in range(2):
                nc.vector.bn_stats(fstats[:, t], xo[h][:, t]).then_inc(s_fs, 1)
            dve.wait_ge(s_fs, 6 * j + 3)
            nc.vector.memset(carrier[:], 0.0)
            for t in range(2):
                nc.vector.bn_aggr(fmv[:, t], fstats[:, t]).then_inc(s_fs, 1)
            dve.wait_ge(s_fs, 6 * j + 5)
            nc.vector.tensor_scalar(fve[:, :, 0], fmv[:, :, 1], EPS, None, ALU.add).then_inc(s_fs, 1)
            dve.wait_ge(s_fr, j + 1)
            for t in range(2):
                last = nc.vector.tensor_scalar(y[h][:, t], xo[h][:, t], fmv[:, t, 0:1], frstd[:, t, 0:1],
                                               ALU.subtract, ALU.mult)
            last.then_inc(s_y, 1)

        sequences(dve, one)

    @block.tensor
    def _(pe):
        def keys(w_):
            return slice(0, P) if w_ == 0 else slice(0, 2 * P)

        def transpose_h(T, n, w_, par):
            need(pe, s_ve, min(T + 1, ALL_TILES) if isinstance(T, int) else T + 1)
            if not (isinstance(T, int) and T < 0):
                pe.wait_ge(s_hTe, T + 1)
            if tile_exists(T + 1):
                wn = (w_ + 1) % TILES
                pn = par if w_ < TILES - 1 else 1 - par
                if wn == 0:
                    pe.wait_ge(s_x[pn], x_count(n + 1, pn))
                for ct in range(CT):
                    last = nc.tensor.transpose(X[2][:, ct * P:(ct + 1) * P], x_tok[pn][:, wn, ct * P:(ct + 1) * P], ident[:])
            if tile_exists(T - 2):
                pe.wait_ge(s_hn, T - 1)
                for ct in range(CT):
                    last = nc.tensor.transpose(X[2][:, (2 + ct) * P:(3 + ct) * P], hn[:, ct * P:(ct + 1) * P], ident[:])
            last.then_inc(s_hT, 1)

        counts = {}

        def x_count(n, pn):
            return 16 * (n // 2 + 1) if isinstance(n, int) else counts["next"]

        def qkv(t, layer):
            pe.wait_ge(s_hTe, t + 1)
            need(pe, s_qkTe, 2 * t)
            wt = W[layer]["qkv"]
            for i, s in enumerate((s_q, s_k, s_v)):
                for k in range(CT):
                    last = nc.tensor.matmul(X[i][:], hT_of(t, k), wt[:, k, i * INNER:(i + 1) * INNER],
                                            start=(k == 0), stop=(k == CT - 1))
                last.then_inc(s, 1)

        tile_parity = {}

        def hT_of(t, k):
            p = tile_parity["next"]
            return hT0[p][:] if k == 0 else hT1[p][:, 0:P]

        def scores(T, w_, hf):
            need(pe, s_PTe, 2 * T + hf)
            cols = keys(w_)
            m = mask[w_ % 2][:].rearrange("p a q -> p (a q)")[:, cols]
            for e in range(2):
                nc.tensor.matmul(SB[:, 2 * e:2 * e + 2, cols], identb[:],
                                 m.unsqueeze(1).to_broadcast([P, 2, cols.stop]), start=True, stop=False,
                                 skip_group_check=True)
            if hf == 0:
                pe.wait_ge(s_qkTe, 2 * T + 2)
            for ps in range(2):
                for e in range(2):
                    rows = slice(64 * e, 64 * e + 64)
                    last = nc.tensor.matmul(SB[:, 2 * e + ps, cols], qT[rows, 2 * hf + ps],
                                            kT[rows, 2 * hf + ps].rearrange("p a q -> p (a q)")[:, cols],
                                            start=False, stop=True, skip_group_check=True)
            last.then_inc(s_S, 1)

        def transpose_probs(T, w_, hf):
            pe.wait_ge(s_pr, 2 * T + hf + 1)
            for i in range(4):
                for a in range(1 if w_ == 0 else 2):
                    last = nc.tensor.transpose(SB[:, i, a * P:(a + 1) * P], probs[hf][:, i, a * P:(a + 1) * P], ident[:])
            last.then_inc(s_PT, 1)

        def times_v(t, w_, hf):
            pe.wait_ge(s_PTe, 2 * t + hf + 1)
            slots = 1 if w_ == 0 else 2
            for e in range(2):
                for ps in range(2):
                    i, h = 2 * e + ps, 4 * hf + 2 * ps + e
                    for a in range(slots):
                        first = hf == 0 and i == 0 and a == 0
                        last = nc.tensor.matmul(M[:, h * LDIM:(h + 1) * LDIM], PT[hf][:, i, a * P:(a + 1) * P],
                                                v[:, w_ if a == w_ % 2 else w_ - 1, h * LDIM:(h + 1) * LDIM], start=first,
                                                stop=(hf == 1 and i == 3 and a == slots - 1), skip_group_check=True)
            if hf == 1:
                last.then_inc(s_AV, 1)

        def hidden(T, i, w_, layer):
            f = 3 * (T - TILES) + i
            c, hf = 3 * (w_ % 2) + i, w_ // 2
            if i == 0:
                need(pe, s_Fa, f)
            elif i == 1:
                need(pe, s_Fa, f - 2)
                if w_ % 2 == 1:
                    need(pe, s_xo, counts["halves"])
            else:
                pe.wait_ge(s_Fa, f - 1)
            size = P if c < CHUNKS - 1 else LAST
            w1 = W[layer(-1)]["w1"]
            for part in range(2):
                for k in range(CT):
                    col = part * HID + c * P
                    last = nc.tensor.matmul(F[i % 2][0:size, part], w1[:, k, col:col + size],
                                            hnT[:, k, hf * 2 * P:(hf + 1) * 2 * P], start=(k == 0), stop=(k == CT - 1))
            last.then_inc(s_F, 1)

        pe.wait_ge(s_w, WEIGHTS)
        pe.wait_ge(s_c, 12)
        tile_parity["next"] = 0
        transpose_h(-1, -1, 3, 1)
        qkv(0, 0)

        def one(n, par, r, layer):
            for w_ in range(TILES):
                T = TILES * n + w_
                live, feed = tile_exists(T), seq_exists(n - 1)
                counts["next"] = 16 * (r + 1 + par)
                counts["halves"] = 2 * n - 2 + (w_ == 3) if w_ % 2 else None
                tile_parity["next"] = (w_ + 1) % 2
                if tile_exists(T - 1):
                    n1, w1_ = back(n, w_, 1)
                    times_v(T - 1, w1_, 1)
                if live:
                    pe.wait_ge(s_qr, T + 1)
                    for b in range(PAIRS):
                        last = nc.tensor.transpose(X[0][:, b * P:(b + 1) * P], q_rot[:, 2 * b:2 * b + 2].rearrange("p h d -> p (h d)"), ident[:])
                    last.then_inc(s_qkT, 1)
                    pe.wait_ge(s_kr, T + 1)
                    for b in range(PAIRS):
                        last = nc.tensor.transpose(X[1][:, b * P:(b + 1) * P], k_rot[:, 2 * b:2 * b + 2].rearrange("p h d -> p (h d)"), ident[:])
                    last.then_inc(s_qkT, 1)
                if feed:
                    hidden(T, 0, w_, layer)
                if tile_exists(T - 1):
                    pe.wait_ge(s_on, T)
                    for b in range(IH):
                        last = nc.tensor.transpose(M[:, b * P:(b + 1) * P], o_n[:, b * P:(b + 1) * P], ident[:])
                    last.then_inc(s_oT, 1)
                if live:
                    scores(T, w_, 0)
                if tile_exists(T + 1) or tile_exists(T - 2):
                    transpose_h(T, n, w_, par)
                if tile_exists(T - 1):
                    pe.wait_ge(s_oTe, T)
                    wo = W[layer(0 if w_ >= 1 else -1)]["o"]
                    for b in range(IH):
                        last = nc.tensor.matmul(M[:, 0:CH], oT[:, b], wo[:, b], start=(b == 0), stop=(b == IH - 1))
                    last.then_inc(s_wo, 1)
                if tile_exists(T + 1):
                    qkv(T + 1, layer(0 if w_ < 3 else 1))
                if live:
                    transpose_probs(T, w_, 0)
                if feed:
                    hidden(T, 1, w_, layer)
                if live:
                    scores(T, w_, 1)
                    need(pe, s_x2, T)
                    pe.wait_ge(s_ve, T + 1)
                    times_v(T, w_, 0)
                if feed:
                    hidden(T, 2, w_, layer)
                if w_ % 2 == 0:
                    h, d = (1, 2) if w_ == 0 else (0, 1)
                    m = n - d
                    if seq_exists(m):
                        pe.wait_ge(s_um, 2 * m + h + 1)
                        if feed:
                            pe.wait_ge(s_Fa, 3 * (T - TILES) + 2)
                        w2 = W[layer(-d)]["w2"]
                        for t in range(2):
                            for c in range(CHUNKS):
                                rows = P if c < CHUNKS - 1 else LAST + 1
                                last = nc.tensor.matmul(F[1][:, t], a_sb[h][0:rows, c, t * P:(t + 1) * P],
                                                        w2[0:rows, c], start=(c == 0), stop=(c == CHUNKS - 1))
                        last.then_inc(s_w2, 1)
                if live:
                    transpose_probs(T, w_, 1)
                if isinstance(n, int) and n == ALL_SEQS + 1:
                    break

        sequences(pe, one)


def rotary_tables():
    d = np.arange(0, LDIM, 2, dtype=np.float32)
    t = np.arange(SEQ, dtype=np.float32)
    freqs = t[:, None] * (np.float32(1.0) / np.float32(10000.0) ** (d / np.float32(LDIM)))[None, :]
    base = (d + np.float32(0.4 * LDIM)) / np.float32(1.4 * LDIM)
    scale = base[None, :] ** ((t - np.float32(SEQ // 2)) / np.float32(64.0))[:, None]
    cos, sin = np.cos(freqs), np.sin(freqs)
    both = lambda a, b: np.concatenate([a, b], axis=1)
    q = [np.float32(8.0) * both(cos * scale, cos * scale), np.float32(8.0) * both(-sin * scale, sin * scale)]
    k = [both(cos / scale, cos / scale), both(-sin / scale, sin / scale)]
    return np.stack(q + k, axis=1).astype(np.float32)


def build(nc, w, y_out):
    x_a = nc.dram_tensor("x_after_heads", (SEQS, SEQ, CH), F32).ap()
    x_b = nc.dram_tensor("x_after_layer", (SEQS, SEQ, CH), F32).ap()
    with ExitStack() as ctx:
        consts = make_constants(nc, ctx)
        W0 = load_layer(nc, ctx, 0)
        with ExitStack() as stage:
            head_attention(nc, stage, w["x"], w, x_a, consts, W0)
        with ExitStack() as stage:
            W1 = load_layer(nc, stage, 1)
            layers(nc, stage, x_a, x_b, y_out, w, [W0, W1], consts)


def kernel(**inputs):
    import concourse.bacc as bacc
    from concourse.bass_utils import run_bass_kernel_spmd

    g = {name[3:]: np.asarray(value) for name, value in inputs.items()}

    def head_order(a):
        return a.reshape(a.shape[:-1] + (CT, JH, HDIM)).swapaxes(-1, -2).reshape(a.shape)

    def on_partitions(a):
        a = np.concatenate([a, np.zeros(a.shape[:-1] + (-a.shape[-1] % P,), a.dtype)], axis=-1)
        return np.moveaxis(a.reshape(a.shape[:-1] + (-1, P)), -1, 1)

    def swapped(a):
        return np.concatenate([a[..., LDIM // 2:], a[..., :LDIM // 2]], axis=-1)

    arrays = {
        "x": g["attn_x"],
        "Wq": head_order(g["attn_Wq"].T), "Wk": head_order(g["attn_Wk"].T),
        "Wv": g["attn_Wv"].T, "Wo": g["attn_Wo"].T,
        "bq": head_order(g["attn_bq"]).reshape(CT, P).T, "bk": head_order(g["attn_bk"]).reshape(CT, P).T,
        "bv": g["attn_bv"], "bo": g["attn_bo"],
        "wqkv": g["ffn_wqkv"], "wo2": g["ffn_wo"], "w1": g["ffn_w1"], "w2": g["ffn_w2"],
        "b1": on_partitions(g["ffn_b1"].reshape(LAYERS, 2, HID)), "b2": g["ffn_b2"],
        "ln_g": on_partitions(g["ffn_ln_g"]), "ln_b": on_partitions(g["ffn_ln_b"]),
        "q_scale": g["ffn_q_scale"], "k_scale": g["ffn_k_scale"],
        "q_scale_swapped": swapped(g["ffn_q_scale"]), "k_scale_swapped": swapped(g["ffn_k_scale"]),
        "tab": rotary_tables(),
    }
    arrays = {name: np.ascontiguousarray(a) for name, a in arrays.items()}
    nc = bacc.Bacc("TRN2", target_bir_lowering=False, num_devices=1)
    w = {name: nc.dram_tensor(f"in_{name}", a.shape, F32, kind="ExternalInput").ap() for name, a in arrays.items()}
    out = nc.dram_tensor("out_0", (SEQS, SEQ, CH), F32, kind="ExternalOutput").ap()
    build(nc, w, out)
    result = run_bass_kernel_spmd(nc, [{f"in_{name}": a for name, a in arrays.items()}], core_ids=[0])
    return result.results[0]["out_0"]
```

```python
from contextlib import ExitStack

import numpy as np

import concourse.bass as bass
from concourse import mybir

F32 = mybir.dt.float32
F32R = mybir.dt.float32r
BF16 = mybir.dt.bfloat16
ACT = mybir.ActivationFunctionType
ALU = mybir.AluOpType
AX = mybir.AxisListType

P = 128
SEQS, SEQ, CH = 16, 512, 256
TILES = SEQ // P
CT = CH // P
HEADS, HDIM = 16, 16
JH = HEADS // CT
UNITS = TILES * TILES
EPS = 1e-5
TERMS = [(0, 0), (0, 1), (1, 0), (1, 1), (0, 2), (2, 0), (1, 2), (2, 1)]


def need(engine, sem, value):
    if not (isinstance(value, int) and value <= 0):
        engine.wait_ge(sem, value)


def lagged(n, u, lag, steps):
    return (n, 0, u - lag) if u >= lag else (n - 1, 1, u - lag + steps)


def exists(n):
    return not isinstance(n, int) or 0 <= n < SEQS


def head_attention(nc, ctx, x_in, w, x_out, consts, W0=None):
    ident, identr, half = consts["ident"], consts["identr"], consts["minus_half"]
    ones_row, minus_identb = consts["ones_row"], consts["minus_identb"]

    def sb(name, shape, dtype=F32):
        return ctx.enter_context(nc.sbuf_tensor("a_" + name, shape, dtype))

    def sem(name):
        return ctx.enter_context(nc.semaphore("a_" + name))

    def bank(name, shape=(P, 512)):
        return ctx.enter_context(nc.psum_tensor("a_" + name, list(shape), F32))

    wq, wk, wv, wo = (sb(n, [P, CT, CH]) for n in ("wq", "wk", "wv", "wo"))
    bq, bk = (sb(n, [P, CT]) for n in ("bq", "bk"))
    bv_rows, bo_row = sb("bv", [P, CH]), sb("bo", [1, CH])
    x_tok = [sb(f"x{i}", [P, TILES, CH]) for i in range(2)]
    xT = sb("xT", [P, CT, SEQ])
    parts = [sb(f"parts{i}", [P, 3, CT, SEQ], BF16) for i in range(2)]
    qk8 = [[sb(f"{n}8{i}", [P, JH, CT, SEQ], BF16) for n in "qk"] for i in range(2)]
    v_pad = [sb(f"v{i}", [P, TILES, HEADS // 2, 64]) for i in range(2)]
    NE = 4
    probs = [sb(f"p{i}", [P, HEADS, P]) for i in range(NE)]
    z8, z4 = sb("z8", [P, 8, P]), [sb(f"z4{i}", [P, 4, P]) for i in range(4)]
    zinv = [sb(f"zi{i}", [P, P]) for i in range(2)]
    negmax = [sb(f"nm{i}", [P, P], F32R) for i in range(2)]
    oT = [sb(f"oT{i}", [P, CT, P]) for i in range(2)]
    resid = [sb(f"r{i}", [P, CH]) for i in range(2)]
    stats, carrier, mv = sb("stats", [P, 6]), sb("carrier", [P, 1]), [sb(f"mv{i}", [P, 2]) for i in range(2)]
    vareps, rstd = ([sb(f"{n}{i}", [P, 1]) for i in range(2)] for n in ("ve", "rs"))
    normed = [sb(f"n{i}", [P, CH]) for i in range(2)]

    S = bank("S", (P, HEADS, P))
    O = bank("O", (P, CT, P))
    YZ = bank("YZ", (P, 2, CH))
    Y = YZ[:, 0]
    Z = YZ[:, 1, :P]
    B = [bank("B0"), bank("B1")]

    s_w = sem("weights_loaded")
    s_w0 = sem("next_weights_loaded")
    s_x = [sem(f"x_loaded{i}") for i in range(2)]
    s_pz = sem("vpad_zeroed")
    s_pt = sem("proj_psum")
    s_xT = sem("xT_evacuated")
    s_part = sem("part")
    s_less = sem("less_part")
    s_vv = sem("v_evacuated")
    s_pack = [sem(f"packed{i}") for i in range(2)]
    s_S = sem("scores")
    s_nm = sem("negmax")
    s_sub = sem("scores_less_max")
    s_exp = sem("exp")
    s_zt = sem("z_tree")
    s_z = sem("z")
    s_zi = sem("zinv")
    s_p = sem("probs")
    s_pp = sem("probs_by_pool")
    s_av = sem("av")
    s_oT = sem("oT")
    s_Y = sem("Y")
    s_r = sem("resid")
    s_st = sem("stats_done")
    s_rs = sem("rstd")
    s_n = sem("normed")
    s_out = [sem(f"stored{i}") for i in range(2)]

    PACKED = 16 * 2 * len(TERMS)
    T_AT, QK_AT, V_AT, V_OUT_AT = 5, (6, 7, 9, 10), (12, 13, 14, 15), (14, 15)
    PARTS = 3
    DVE_HEADS = 12
    PART_ORDER = [(0, 0), (0, 1), (1, 0), (0, 2), (1, 1), (1, 2)]
    PACK_AT = (10, 13)
    LAST_LAG = 6

    block = ctx.enter_context(nc.Block())

    def sequences(engine, one):
        one(0, 0, 0)
        with engine.Fori(0, (SEQS - 2) // 2) as i:
            one(2 * i + 1, 1, i)
            one(2 * i + 2, 0, i + 1)
        one(SEQS - 1, 1, SEQS // 2 - 1)
        one(SEQS, 0, SEQS // 2)

    def part_count(n, i, part):
        return PARTS * 4 * n + PARTS * CT * (i // CT) + PART_ORDER.index((i % CT, part)) + 1

    def less_count(n, i, part):
        return 8 * n + 4 * (i // CT) + 2 * (i % CT) + part + 1

    def parts_at(u):
        return [(i, u - QK_AT[i]) for i in range(4) if 0 <= u - QK_AT[i] < PARTS]

    def units_of(n):
        return range(UNITS if exists(n) else LAST_LAG + 1)

    @block.sync
    def _(sp):
        def load_x(n, par):
            sp.dma_start(x_tok[par][:], x_in[bass.ts(n, 1), :, :].rearrange("a (t p) c -> p (a t) c", p=P)
                         ).then_inc(s_x[par], 16)

        def pack(n, par, which):
            sp.wait_ge(s_part, part_count(n, CT * which + CT - 1, 2))
            for t, (of_k, of_q) in enumerate(TERMS):
                part = of_k if which else of_q
                sp.dma_start(qk8[par][which][16 * t:16 * t + 16], parts[which][:, part]).then_inc(s_pack[par], 16)

        for dst, name in ((wq, "Wq"), (wk, "Wk"), (wv, "Wv"), (wo, "Wo")):
            sp.dma_start(dst[:], w[name].rearrange("(k p) o -> p k o", p=P)).then_inc(s_w, 16)
        sp.dma_start(bq[:], w["bq"]).then_inc(s_w, 16)
        sp.dma_start(bk[:], w["bk"]).then_inc(s_w, 16)
        sp.dma_start(bv_rows[:], w["bv"].partition_broadcast(P)).then_inc(s_w, 16)
        sp.dma_start(bo_row[:], w["bo"].unsqueeze(0)).then_inc(s_w, 16)
        load_x(0, 0)
        if W0 is not None:
            start_layer_loads(sp, W0, w, 0, s_w0)
        pack(0, 0, 0)
        pack(0, 0, 1)

        def one(n, par, r):
            for u in units_of(n):
                if u == LAST_LAG - 2 and exists(n) and exists(n + 1):
                    need(sp, s_r, TILES * n)
                    load_x(n + 1, 1 - par)
                if u in PACK_AT and exists(n) and exists(n + 1):
                    pack(n + 1, 1 - par, PACK_AT.index(u))
                nn, back, uu = lagged(n, u, 6, UNITS)
                if uu % TILES == TILES - 1 and exists(nn):
                    qt = uu // TILES
                    sp.wait_ge(s_n, TILES * nn + qt + 1)
                    sp.dma_start(x_out[bass.ts(nn, 1), qt * P:(qt + 1) * P, :].rearrange("a p c -> p (a c)"),
                                 normed[qt % 2][:]).then_inc(s_out[qt % 2], 16)

        sequences(sp, one)
        for i in range(2):
            sp.wait_ge(s_out[i], 16 * SEQS * TILES // 2)
        if W0 is not None:
            sp.wait_ge(s_w0, 16 * LAYER_LOADS)

    @block.gpsimd
    def _(pool):
        def sum_heads(n, u):
            U = UNITS * n + u
            e = probs[u % NE]
            need(pool, s_zt, 2 * U)
            pool.wait_ge(s_exp, 4 * U + 4)
            nc.gpsimd.tensor_tensor(z8[:], e[:, 0:8], e[:, 8:16], ALU.add).then_inc(s_zt, 1)
            pool.wait_ge(s_zt, 2 * U + 1)
            need(pool, s_z, U - 3)
            nc.gpsimd.tensor_tensor(z4[u % 4][:], z8[:, 0:4], z8[:, 4:8], ALU.add).then_inc(s_zt, 1)

        def normalise(n, u):
            e = probs[u % NE][:, DVE_HEADS:]
            pool.wait_ge(s_zi, UNITS * n + u + 1)
            nc.gpsimd.tensor_tensor(e, e, zinv[u % 2][:].unsqueeze(1).to_broadcast([P, HEADS - DVE_HEADS, P]),
                                    ALU.mult).then_inc(s_pp, 1)

        def rstd_of(n, qt):
            m = TILES * n + qt
            pool.wait_ge(s_st, 3 * m + 3)
            need(pool, s_n, m - 1)
            nc.gpsimd.tensor_tensor(rstd[qt % 2][:], vareps[qt % 2][:], half[:, 0:1], ALU.pow).then_inc(s_rs, 1)

        for i in range(2):
            nc.gpsimd.memset(v_pad[i][:], 0.0).then_inc(s_pz, 1)

        def one(n, par, r):
            for u in units_of(n):
                nn, back, uu = lagged(n, u, 2, UNITS)
                if exists(nn):
                    normalise(nn, uu)
                if exists(n):
                    sum_heads(n, u)
                nn, back, uu = lagged(n, u, 5, UNITS)
                if uu % TILES == TILES - 1 and exists(nn):
                    rstd_of(nn, uu // TILES)

        sequences(pool, one)

    @block.scalar
    def _(act):
        def evacuate_xT(n):
            for ct in range(CT):
                act.wait_ge(s_pt, 8 * n + ct + 1)
                nc.scalar.activation(xT[:, ct], B[ct][:], ACT.Copy).then_inc(s_xT, 1)

        def part_of_qk(n, i, part):
            which, ot = divmod(i, CT)
            if part == 0:
                act.wait_ge(s_pt, 8 * n + 3 + i)
            else:
                act.wait_ge(s_less, less_count(n, i, part - 1))
            nc.scalar.activation(parts[which][:, part, ot], B[ot][:], ACT.Identity,
                                 bias=(bq, bk)[which][:, ot:ot + 1]).then_inc(s_part, 1)

        act.wait_ge(s_w, 16 * 8)
        evacuate_xT(0)
        for which in range(2):
            for ot, part in PART_ORDER:
                part_of_qk(0, CT * which + ot, part)

        def one(n, par, r):
            for u in units_of(n):
                if exists(n):
                    U = UNITS * n + u
                    need(act, s_av, U - NE + 1)
                    for b in range(4):
                        hs = slice(4 * b, 4 * b + 4)
                        act.wait_ge(s_sub, 4 * U + b + 1)
                        nc.scalar.activation(probs[u % NE][:, hs], S[:, hs], ACT.Exp, scale=HDIM ** -0.5).then_inc(s_exp, 1)
                nn, back, uu = lagged(n, u, 3, UNITS)
                if uu % TILES == TILES - 1 and exists(nn):
                    qt = uu // TILES
                    act.wait_ge(s_av, UNITS * nn + uu + 1)
                    need(act, s_Y, TILES * nn + qt - 1)
                    nc.scalar.activation(oT[qt % 2][:], O[:], ACT.Copy).then_inc(s_oT, 1)
                if exists(n) and exists(n + 1):
                    if u == T_AT:
                        evacuate_xT(n + 1)
                    for i, part in parts_at(u):
                        part_of_qk(n + 1, i, part)

        sequences(act, one)

    @block.vector
    def _(dve):
        def evacuate_v(n, par, j):
            need(dve, s_av, UNITS * (n - 1))
            dve.wait_ge(s_pt, 8 * n + 7 + j)
            src = B[j][:].rearrange("p (t h e d) -> p t h e d", t=2, e=2, d=HDIM)
            bias = bv_rows[:].rearrange("p (h e d) -> p h e d", e=2, d=HDIM)
            for e in range(2):
                last = nc.vector.tensor_tensor(
                    v_pad[par][:, 2 * j:2 * j + 2, :, 48 * e:48 * e + HDIM], src[:, :, :, e],
                    bias[:, :, e].unsqueeze(1).to_broadcast([P, 2, HEADS // 2, HDIM]), ALU.add)
            last.then_inc(s_vv, 1)

        dve.wait_ge(s_w, 16 * 8)
        dve.wait_ge(s_pz, 2)
        evacuate_v(0, 0, 0)
        evacuate_v(0, 0, 1)

        def one(n, par, r):
            for u in units_of(n):
                if exists(n):
                    U = UNITS * n + u
                    dve.wait_ge(s_S, U + 1)
                    need(dve, s_sub, 4 * U - 4)
                    nc.vector.tensor_reduce(out=negmax[u % 2][:], in_=S[:].rearrange("p h q -> p q h"),
                                            axis=AX.X, op=ALU.max, negate=True).then_inc(s_nm, 1)
                nn, back, uu = lagged(n, u, 2, UNITS)
                if exists(nn):
                    U = UNITS * nn + uu
                    dve.wait_ge(s_z, U + 1)
                    need(dve, s_pp, U - 1)
                    nc.vector.reciprocal(zinv[uu % 2][:], Z).then_inc(s_zi, 1)
                    dve.wait_ge(s_zi, U + 1)
                    e = probs[uu % NE][:, :DVE_HEADS]
                    nc.vector.tensor_tensor(e, e, zinv[uu % 2][:].unsqueeze(1).to_broadcast([P, DVE_HEADS, P]),
                                            ALU.mult).then_inc(s_p, 1)
                nn, back, uu = lagged(n, u, 6, UNITS)
                if uu % TILES == TILES - 1 and exists(nn):
                    qt = uu // TILES
                    m = TILES * nn + qt
                    rn = r if not back else (r if par else r - 1)
                    dve.wait_ge(s_rs, m + 1)
                    need(dve, s_out[qt % 2], 16 * (2 * nn + qt // 2))
                    nc.vector.tensor_scalar(normed[qt % 2][:], resid[qt % 2][:], mv[qt % 2][:, 0:1],
                                            rstd[qt % 2][:, 0:1], ALU.subtract, ALU.mult).then_inc(s_n, 1)
                nn, back, uu = lagged(n, u, 5, UNITS)
                if uu % TILES == TILES - 1 and exists(nn):
                    qt = uu // TILES
                    m = TILES * nn + qt
                    pn = par if not back else 1 - par
                    dve.wait_ge(s_Y, m + 1)
                    nc.vector.tensor_tensor(resid[qt % 2][:], Y, x_tok[pn][:, qt], ALU.add).then_inc(s_r, 1)
                    dve.wait_ge(s_r, m + 1)
                    nc.vector.bn_stats(stats[:], resid[qt % 2][:]).then_inc(s_st, 1)
                    dve.wait_ge(s_st, 3 * m + 1)
                    nc.vector.memset(carrier[:], 0.0)
                    nc.vector.bn_aggr(mv[qt % 2][:], stats[:]).then_inc(s_st, 1)
                    dve.wait_ge(s_st, 3 * m + 2)
                    nc.vector.tensor_scalar(vareps[qt % 2][:], mv[qt % 2][:, 1:2], EPS, None, ALU.add).then_inc(s_st, 1)
                if u in V_OUT_AT and exists(n) and exists(n + 1):
                    evacuate_v(n + 1, 1 - par, V_OUT_AT.index(u))

        sequences(dve, one)

    @block.tensor
    def _(pe):
        def piece_free(n, piece):
            if piece < 2:
                need(pe, s_vv, 2 * n - 1 + piece)
            elif piece < 4:
                pe.wait_ge(s_xT, 2 * n + piece - 1)
            else:
                pe.wait_ge(s_part, part_count(n, piece - 4, PARTS - 1))

        def transpose_x(n, par):
            for ct in range(CT):
                piece_free(n, ct)
                for t in range(TILES):
                    last = nc.tensor.transpose(B[ct][:, t * P:(t + 1) * P], x_tok[par][:, t, ct * P:(ct + 1) * P], ident[:])
                last.then_inc(s_pt, 1)

        def project_qk(n, i, k):
            which, ot = divmod(i, CT)
            if k == 0:
                piece_free(n, 2 + i)
            if i == 0 and k == 0:
                pe.wait_ge(s_xT, 2 * n + 2)
            last = nc.tensor.matmul(B[ot][:], (wq, wk)[which][:, k, ot * P:(ot + 1) * P], xT[:, k],
                                    start=(k == 0), stop=(k == CT - 1), skip_group_check=True)
            if k == CT - 1:
                last.then_inc(s_pt, 1)

        def less_part(n, i, part):
            which, ot = divmod(i, CT)
            pe.wait_ge(s_part, part_count(n, i, part))
            nc.tensor.matmul(B[ot][:], minus_identb[:], parts[which][:, part, ot], start=False, stop=True,
                             skip_group_check=True).then_inc(s_less, 1)

        def project_v(n, tile, k):
            j, t = divmod(tile, 2)
            if t == 0 and k == 0:
                piece_free(n, 6 + j)
            last = nc.tensor.matmul(B[j][:, t * CH:(t + 1) * CH], xT[:, k, tile * P:(tile + 1) * P], wv[:, k],
                                    start=(k == 0), stop=(k == CT - 1), skip_group_check=True)
            if t == 1 and k == CT - 1:
                last.then_inc(s_pt, 1)

        def output(n, uu, k):
            qt = uu // TILES
            m = TILES * n + qt
            if k == 0:
                pe.wait_ge(s_oT, m + 1)
                need(pe, s_r, m)
                last_sum = UNITS * n + uu + 3
                pe.wait_ge(s_zi, min(last_sum, UNITS * SEQS) if isinstance(n, int) else last_sum)
                nc.tensor.matmul(Y, ones_row[0:1, :], bo_row[0:1, :], start=True, stop=False, skip_group_check=True)
            last = nc.tensor.matmul(Y, oT[qt % 2][:, k], wo[:, k], start=False, stop=(k == CT - 1),
                                    skip_group_check=True)
            if k == CT - 1:
                last.then_inc(s_Y, 1)

        def project(n, u, k):
            if exists(n) and exists(n + 1):
                for i, part in parts_at(u - 1):
                    if k == 0 and part < PARTS - 1:
                        less_part(n + 1, i, part)
                if u in QK_AT:
                    project_qk(n + 1, QK_AT.index(u), k)
                if u in V_AT:
                    project_v(n + 1, V_AT.index(u), k)

        pe.wait_ge(s_w, 16 * 8)
        pe.wait_ge(s_x[0], 16)
        transpose_x(0, 0)
        for i in range(2 * CT):
            for k in range(CT):
                project_qk(0, i, k)
            if i % CT == CT - 1:
                for ot, part in PART_ORDER:
                    if part < PARTS - 1:
                        less_part(0, i - 1 + ot, part)
        for tile in range(TILES):
            for k in range(CT):
                project_v(0, tile, k)

        def one(n, par, r):
            for u in units_of(n):
                if exists(n):
                    U = UNITS * n + u
                    if u == 0:
                        pe.wait_ge(s_pack[par], PACKED * (r + 1))
                    qt, kt = u // TILES, u % TILES
                    q8, k8 = qk8[par]
                    for h in range(HEADS):
                        if h % 4 == 0:
                            need(pe, s_exp, 4 * U - 3 + h // 4)
                        last = nc.tensor.matmul(S[:, h], k8[:, h % JH, h // JH, kt * P:(kt + 1) * P],
                                                q8[:, h % JH, h // JH, qt * P:(qt + 1) * P],
                                                start=(h % 4 == 0), stop=(h % 4 == 3))
                    last.then_inc(s_S, 1)
                nn, back, uu = lagged(n, u, 2, UNITS)
                if exists(nn):
                    U = UNITS * nn + uu
                    pe.wait_ge(s_zt, 2 * U + 2)
                    need(pe, s_zi, U)
                    np_, _, up = lagged(n, u, 6, UNITS)
                    if up % TILES == TILES - 1 and exists(np_):
                        pe.wait_ge(s_r, TILES * np_ + up // TILES + 1)
                    for j in range(4):
                        last = nc.tensor.matmul(Z, ident[:], z4[uu % 4][:, j], start=(j == 0), stop=(j == 3),
                                                skip_group_check=True)
                    last.then_inc(s_z, 1)
                nn, back, uu = lagged(n, u, 3, UNITS)
                if exists(nn):
                    qt, kt = uu // TILES, uu % TILES
                    pn = par if not back else 1 - par
                    if kt == 0:
                        need(pe, s_oT, TILES * nn + qt)
                    pe.wait_ge(s_p, UNITS * nn + uu + 1)
                    if uu == 0:
                        pe.wait_ge(s_vv, 2 * nn + 2)
                    for t in range(CT):
                        if t == DVE_HEADS // JH:
                            pe.wait_ge(s_pp, UNITS * nn + uu + 1)
                        for e in range(2):
                            for g in range(4):
                                last = nc.tensor.matmul(
                                    O[32 * g:32 * g + 32, t], v_pad[pn][:, kt, 4 * t + g, 32 * e:32 * e + 32],
                                    probs[uu % NE][:, JH * t + 2 * g + e], start=(kt == 0 and t == 0 and e == 0),
                                    stop=(kt == TILES - 1 and e == 1 and t == 1), tile_position=(0, 32 * g),
                                    skip_group_check=True)
                    last.then_inc(s_av, 1)
                project(n, u, 0)
                if exists(n):
                    U = UNITS * n + u
                    pe.wait_ge(s_nm, U + 1)
                    for b in range(4):
                        last = nc.tensor.matmul(S[:, 4 * b:4 * b + 4], identr[:],
                                                negmax[u % 2][:].unsqueeze(1).to_broadcast([P, 4, P]),
                                                start=False, stop=True, skip_group_check=True)
                        last.then_inc(s_sub, 1)
                project(n, u, 1)
                nn, back, uu = lagged(n, u, 4, UNITS)
                if uu % TILES == TILES - 1 and exists(nn):
                    for k in range(CT):
                        output(nn, uu, k)
                if exists(n) and exists(n + 1) and u == T_AT:
                    pe.wait_ge(s_x[1 - par], 16 * (r + 1 + par))
                    transpose_x(n + 1, 1 - par)

        sequences(pe, one)


def make_constants(nc, ctx):
    def sb(name, shape, dtype=F32):
        return ctx.enter_context(nc.sbuf_tensor("c_" + name, shape, dtype))

    c = {"ident": sb("ident", [P, P]), "identr": sb("identr", [P, P], F32R),
         "identb": sb("identb", [P, P], BF16), "minus_identb": sb("minus_identb", [P, P], BF16),
         "minus_half": sb("half", [P, 16]), "ones_row": sb("ones", [1, P])}
    s_i = ctx.enter_context(nc.semaphore("c_identity"))
    with nc.Block() as block:
        @block.gpsimd
        def _(pool):
            nc.gpsimd.memset(c["minus_half"][:], -0.5).then_inc(s_i, 1)
            nc.gpsimd.memset(c["ones_row"][:], 1.0).then_inc(s_i, 1)
            nc.gpsimd.memset(c["ident"][:], 0.0).then_inc(s_i, 1)
            pool.wait_ge(s_i, 3)
            nc.gpsimd.affine_select(out=c["ident"][:], in_=c["ident"][:], compare_op=ALU.not_equal, fill=1.0, base=0,
                                    pattern=[[-1, P]], channel_multiplier=1).then_inc(s_i, 1)

        @block.vector
        def _(dve):
            dve.wait_ge(s_i, 4)
            nc.vector.tensor_copy(c["identr"][:], c["ident"][:]).then_inc(s_i, 1)
            nc.vector.tensor_copy(c["identb"][:], c["ident"][:]).then_inc(s_i, 1)
            nc.vector.tensor_scalar(c["minus_identb"][:], c["ident"][:], -1.0, None, ALU.mult).then_inc(s_i, 1)
            dve.wait_ge(s_i, 7)
    return c


LAYERS = 2
LHEADS, LDIM = 8, 64
INNER = LHEADS * LDIM
HID = int(CH * 4 * 2 / 3)
CHUNKS = -(-HID // P)
LAST = HID - (CHUNKS - 1) * P
ALL_SEQS = LAYERS * SEQS
ALL_TILES = ALL_SEQS * TILES
MASKED = -1e30
PAIRS = INNER // P
IH = INNER // P


def layer_of(n):
    return n // SEQS


def load_layer(nc, ctx, tag):
    def sb(name, shape, dtype=F32):
        return ctx.enter_context(nc.sbuf_tensor(f"w{tag}_" + name, shape, dtype))

    return {"qkv": sb("qkv", [P, CT, 3 * INNER]), "o": sb("o", [P, IH, CH]),
            "w1": sb("w1", [P, CT, 2 * HID]), "w2": sb("w2", [P, CHUNKS, CH]),
            "b1": sb("b1", [P, 2, CHUNKS]), "ln_g": sb("g", [P, CT]), "ln_b": sb("b", [P, CT])}


LAYER_LOADS = 9


def start_layer_loads(engine, dst, w, layer, sem):
    full = (CHUNKS - 1) * P
    def load(out, src):
        engine.dma_start(out, src).then_inc(sem, 16)

    load(dst["qkv"][:], w["wqkv"][layer].rearrange("(k p) o -> p k o", p=P))
    load(dst["o"][:], w["wo2"][layer].rearrange("(k p) o -> p k o", p=P))
    load(dst["w1"][:], w["w1"][layer].rearrange("(k p) o -> p k o", p=P))
    load(dst["w2"][:, 0:CHUNKS - 1], w["w2"][layer, 0:full].rearrange("(k p) o -> p k o", p=P))
    load(dst["w2"][0:LAST, CHUNKS - 1], w["w2"][layer, full:HID])
    load(dst["w2"][LAST:LAST + 1, CHUNKS - 1], w["b2"][layer:layer + 1])
    for name in ("b1", "ln_g", "ln_b"):
        load(dst[name][:], w[name][layer])


def layers(nc, ctx, x_a, x_b, y_out, w, W, consts):
    ident, half, identb = consts["ident"], consts["minus_half"], consts["identb"]

    def sb(name, shape, dtype=F32):
        return ctx.enter_context(nc.sbuf_tensor("b_" + name, shape, dtype))

    def sem(name):
        return ctx.enter_context(nc.semaphore("b_" + name))

    def bank(name, shape=(P, 512)):
        return ctx.enter_context(nc.psum_tensor("b_" + name, list(shape), F32))

    x_tok = [sb(f"x{i}", [P, TILES, CH]) for i in range(2)]
    x2 = [sb(f"x2{i}", [P, TILES, CH]) for i in range(2)]
    base_tab = sb("base_tab", [P, TILES, 4, LDIM])
    tab = [sb(f"tab{i}", [P, TILES, 4, LDIM]) for i in range(LAYERS)]
    srow = [sb(f"srow{i}", [P, 4, LDIM]) for i in range(LAYERS)]
    mask = [sb(f"mask{i}", [P, 2, P], BF16) for i in range(2)]
    zero_col = sb("zero_col", [P, 1])
    carrier = sb("carrier", [P, 1])
    hT0 = [sb(f"hT0{i}", [P, P]) for i in range(2)]
    hT1 = [sb(f"hT1{i}", [P, P + 1]) for i in range(2)]
    sq = sb("sq", [P, 2, LHEADS, LDIM])
    t1 = [sb(f"t1{i}", [P, LHEADS, LDIM]) for i in range(2)]
    t2 = [sb(f"t2{i}", [P, LHEADS, LDIM]) for i in range(2)]
    q_rot, k_sum, k_rot = (sb(n, [P, LHEADS, LDIM]) for n in ("q_rot", "k_sum", "k_rot"))
    ss = sb("ss", [P, 2 * LHEADS])
    ssc = sb("ssc", [P, 2 * LHEADS])
    rn = [sb(f"rn{i}", [P, 2 * LHEADS]) for i in range(2)]
    qT = sb("qT", [P, PAIRS, P])
    kT = sb("kT", [P, PAIRS, 2, P])
    v = sb("v", [P, TILES, INNER])
    mx = sb("mx", [P, 4])
    nb = [sb(f"nb{i}", [P, 4]) for i in range(2)]
    probs = [sb(f"p{i}", [P, 4, 2 * P]) for i in range(2)]
    rs = [sb(f"rs{i}", [P, LHEADS]) for i in range(2)]
    rinv = sb("rinv", [P, LHEADS])
    PT = [sb(f"PT{i}", [P, 4, 2 * P]) for i in range(2)]
    o_n = sb("o_n", [P, INNER])
    oT = sb("oT", [P, IH, P])
    hs = sb("hs", [P, TILES, P])
    stats = sb("stats", [P, 2, 6])
    mv, ve, rstd = ([sb(f"{n}{i}", [P, 2]) for i in range(2)] for n in ("mv", "ve", "rstd"))
    hn = sb("hn", [P, CH])
    hnT = sb("hnT", [P, CT, SEQ])
    a_sb = [sb(f"a{i}", [P, CHUNKS, 2 * P]) for i in range(2)]
    g_sb = [sb(f"g{i}", [P, CHUNKS, 2 * P]) for i in range(2)]
    xo = [sb(f"xo{i}", [P, 2, CH]) for i in range(2)]
    x0 = [sb(f"x0{i}", [P, 2, CH]) for i in range(2)]
    fstats = sb("fstats", [P, 2, 6])
    fmv, fve, frstd = (sb(n, [P, 2, 2]) for n in ("fmv", "fve", "frstd"))
    y = [sb(f"y{i}", [P, 2, CH]) for i in range(2)]

    X = [bank(f"X{i}") for i in range(3)]
    SB = bank("S", (P, 4, 2 * P))
    M = bank("M")
    F = [bank(f"F{i}", (P, 2, 2 * P)) for i in range(2)]

    s_w = sem("weights")
    s_c = sem("constants")
    s_tab = sem("tables")
    s_x = [sem(f"x_loaded{i}") for i in range(2)]
    s_x0 = [sem(f"x0_loaded{i}") for i in range(2)]
    s_hT = sem("hT")
    s_hTe = sem("hT_evacuated")
    s_q, s_k, s_v = sem("q"), sem("k"), sem("v")
    s_sq = sem("squares")
    s_ve = sem("v_evacuated")
    s_rot = sem("rot_products")
    s_ss = sem("sums_of_squares")
    s_qr = sem("q_rotated")
    s_ks = sem("k_sum")
    s_rn = sem("norms")
    s_kr = sem("k_rotated")
    s_qkT = sem("qkT")
    s_qkTe = sem("qkT_evacuated")
    s_S = sem("scores")
    s_mx = sem("row_max")
    s_nb = sem("exp_bias")
    s_pr = sem("probs")
    s_PT = sem("probs_transposed")
    s_PTe = sem("PT_evacuated")
    s_AV = sem("av")
    s_ri = sem("row_sums_inverted")
    s_on = sem("o_normalised")
    s_oT = sem("oT")
    s_oTe = sem("oT_evacuated")
    s_wo = sem("o_projected")
    s_x2 = sem("x2")
    s_sh = [sem(f"shifted{i}") for i in range(TILES)]
    s_st = sem("ln_stats")
    s_rs = sem("ln_rstd")
    s_hn = sem("ln_normed")
    s_F = sem("F")
    s_Fg = sem("F_gate")
    s_Fa = sem("F_value")
    s_ge = sem("gelu")
    s_um = sem("gated")
    s_w2 = sem("w2")
    s_xo = sem("xo")
    s_fs = sem("final_stats")
    s_fr = sem("final_rstd")
    s_y = sem("y")
    s_stored = [sem(f"stored{i}") for i in range(2)]

    WEIGHTS = 16 * (LAYER_LOADS + 1 + 8)

    block = ctx.enter_context(nc.Block())

    def tile_exists(t):
        return not isinstance(t, int) or 0 <= t < ALL_TILES

    def seq_exists(n):
        return not isinstance(n, int) or 0 <= n < ALL_SEQS

    def sequences(engine, one):
        def peeled(n):
            one(n, n % 2, n // 2, lambda d: (n + d) // SEQS)

        for n in range(4):
            peeled(n)
        for layer, first, end in ((0, 4, SEQS - 2), (1, SEQS + 2, 2 * SEQS - 2)):
            with engine.Fori(0, (end - first) // 2) as i:
                for j in range(2):
                    one(2 * i + (first + j), j, i + first // 2, lambda d: layer)
            for n in range(end, end + 4):
                peeled(n)

    def back(n, w, lag):
        return (n, w - lag) if w >= lag else (n - 1, w - lag + TILES)

    @block.sync
    def _(sp):
        def load_x(n, par, r, layer):
            src = x_a if layer == 0 else x_b
            s = n - layer * SEQS
            sp.dma_start(x_tok[par][:], src[bass.ts(s, 1), :, :].rearrange("a (t p) c -> p (a t) c", p=P)
                         ).then_inc(s_x[par], 16)

        start_layer_loads(sp, W[1], w, 1, s_w)
        sp.dma_start(base_tab[:], w["tab"].rearrange("(t p) k d -> p t k d", p=P)).then_inc(s_w, 16)
        H = LDIM // 2
        for layer in range(LAYERS):
            for i, name in enumerate(("q_scale", "k_scale")):
                row = w[name][layer]
                sp.dma_start(srow[layer][:, 2 * i], row.partition_broadcast(P)).then_inc(s_w, 16)
                swapped = w[name + "_swapped"][layer]
                sp.dma_start(srow[layer][:, 2 * i + 1], swapped.partition_broadcast(P)).then_inc(s_w, 16)
        load_x(0, 0, 0, 0)

        def one(n, par, r, layer):
            for w_ in range(TILES):
                T = TILES * n + w_
                if w_ == 1 and seq_exists(n + 1) and seq_exists(n):
                    need(sp, s_x2, TILES * n)
                    if isinstance(n, int) and SEQS <= n + 1 <= SEQS + 2:
                        for h in range(2):
                            sp.wait_ge(s_stored[h], 16 * (n - SEQS + 2 if n + 1 < SEQS + 2 else SEQS))
                    load_x(n + 1, 1 - par, None, layer(1))
                n1, w1 = back(n, w_, 1)
                if tile_exists(T - 1):
                    p1 = par if w_ >= 1 else 1 - par
                    sp.wait_ge(s_x2, T)
                    src = x2[p1][:, w1, P:CH]
                    for lo, hi in ((0, 112), (112, 127)):
                        sp.dma_start(hs[lo + 1:hi + 1, w1], src[lo:hi]).then_inc(s_sh[w1], 16)
                    if w1 < TILES - 1:
                        sp.dma_start(hs[0:1, w1 + 1], src[127:128]).then_inc(s_sh[w1], 16)
                if w_ % 2 == 0:
                    h, d = (1, 2) if w_ == 0 else (0, 1)
                    m = n - d
                    if seq_exists(m):
                        if layer(-d) == LAYERS - 1:
                            sp.wait_ge(s_y, 2 * (m - SEQS) + h + 1)
                            dst, src, s = y_out, y[h], m - SEQS
                        else:
                            sp.wait_ge(s_xo, 2 * m + h + 1)
                            dst, src, s = x_b, xo[h], m
                        sp.dma_start(dst[bass.ts(s, 1), h * 2 * P:(h + 1) * 2 * P, :].rearrange("a (t p) c -> p (a t) c", p=P),
                                     src[:]).then_inc(s_stored[h], 16)
                if w_ % 2 == 1:
                    h, d = (0, 1) if w_ == 1 else (1, 1)
                    m = n - d
                    if seq_exists(m) and layer(-d) == LAYERS - 1:
                        if not (isinstance(m, int) and m == SEQS):
                            sp.wait_ge(s_fs, 6 * (2 * (m - SEQS - 1) + h) + 1)
                        sp.dma_start(x0[h][:], x_a[bass.ts(m - SEQS, 1), h * 2 * P:(h + 1) * 2 * P, :]
                                     .rearrange("a (t p) c -> p (a t) c", p=P)).then_inc(s_x0[h], 16)
                if isinstance(n, int) and n == ALL_SEQS + 1:
                    break

        sequences(sp, one)
        for h in range(2):
            sp.wait_ge(s_stored[h], 16 * ALL_SEQS)

    @block.gpsimd
    def _(pool):
        def rotate(t):
            pool.wait_ge(s_rot, 2 * t + 1)
            need(pool, s_qkT, 2 * t - 1)
            nc.gpsimd.tensor_tensor(q_rot[:], t1[0][:], t2[0][:], ALU.add).then_inc(s_qr, 1)
            pool.wait_ge(s_rot, 2 * t + 2)
            need(pool, s_kr, t)
            nc.gpsimd.tensor_tensor(k_sum[:], t1[1][:], t2[1][:], ALU.add).then_inc(s_ks, 1)

        def norms(t, p):
            pool.wait_ge(s_ss, 2 * t + 2)
            need(pool, s_pr, 2 * t - 2)
            nc.gpsimd.tensor_tensor(rn[p][:], ssc[:], half[:], ALU.pow).then_inc(s_rn, 1)

        nc.gpsimd.memset(zero_col[:], 0.0).then_inc(s_c, 1)
        for i in range(2):
            nc.gpsimd.memset(hT1[i][:], 0.0).then_inc(s_c, 1)
            nc.gpsimd.memset(a_sb[i][:], 1.0).then_inc(s_c, 1)
            nc.gpsimd.memset(mask[i][:], 0.0).then_inc(s_c, 1)
        nc.gpsimd.memset(hs[:], 0.0).then_inc(s_c, 1)
        pool.wait_ge(s_c, 8)
        for i in range(2):
            nc.gpsimd.affine_select(out=mask[i][:, i], in_=mask[i][:, i], compare_op=ALU.is_ge, fill=MASKED, base=0,
                                    pattern=[[-1, P]], channel_multiplier=1).then_inc(s_c, 1)
            nc.gpsimd.affine_select(out=mask[i][:, 1 - i], in_=mask[i][:, 1 - i], compare_op=ALU.is_ge, fill=MASKED,
                                    base=0, pattern=[[1, P]], channel_multiplier=-1).then_inc(s_c, 1)
        rotate(0)
        norms(0, 0)

        def one(n, par, r, layer):
            for w_ in range(TILES):
                T = TILES * n + w_
                if w_ % 2 == 0:
                    h, d = (1, 2) if w_ == 0 else (0, 1)
                    m = n - d
                    if seq_exists(m):
                        pool.wait_ge(s_ge, 2 * m + h + 1)
                        pool.wait_ge(s_Fa, 3 * (TILES * m + 2 * h + 2))
                        nc.gpsimd.tensor_tensor(a_sb[h][:, 0:CHUNKS - 1], a_sb[h][:, 0:CHUNKS - 1],
                                                g_sb[h][:, 0:CHUNKS - 1], ALU.mult)
                        nc.gpsimd.tensor_tensor(a_sb[h][0:LAST, CHUNKS - 1], a_sb[h][0:LAST, CHUNKS - 1],
                                                g_sb[h][0:LAST, CHUNKS - 1], ALU.mult).then_inc(s_um, 1)
                if tile_exists(T + 1):
                    rotate(T + 1)
                    norms(T + 1, (w_ + 1) % 2)
                if tile_exists(T - 1):
                    p = (w_ + 1) % 2
                    pool.wait_ge(s_st, 4 * (T - 1) + 4)
                    need(pool, s_hn, T - 2)
                    nc.gpsimd.tensor_tensor(rstd[p][:, 0:1], ve[p][:, 0:1], half[:, 0:1], ALU.pow).then_inc(s_rs, 1)
                if w_ % 2 == 0:
                    if seq_exists(m) and layer(-d) == LAYERS - 1:
                        j = 2 * (m - SEQS) + h
                        pool.wait_ge(s_fs, 6 * j + 6)
                        nc.gpsimd.tensor_tensor(frstd[:, :, 0], fve[:, :, 0], half[:, 0:2], ALU.pow).then_inc(s_fr, 1)
                if isinstance(n, int) and n == ALL_SEQS + 1:
                    break

        sequences(pool, one)

    @block.scalar
    def _(act):
        def evacuate_hT(T, n, w_, layer):
            act.wait_ge(s_hT, T + 2)
            if tile_exists(T + 1):
                p = (w_ + 1) % 2
                nc.scalar.activation(hT0[p][:], X[2][:, 0:P], ACT.Copy)
                nc.scalar.activation(hT1[p][:, 1:P + 1], X[2][:, P:2 * P], ACT.Copy)
                last_col = zero_col[:] if (w_ + 1) % TILES == TILES - 1 else X[2][:, 2 * P - 1:2 * P]
                last = nc.scalar.activation(hT1[1 - p][:, 0:1], last_col, ACT.Copy)
            if tile_exists(T - 2):
                n2, w2_ = back(n, w_, 2)
                W2 = W[layer(0 if w_ >= 2 else -1)]
                for ct in range(CT):
                    last = nc.scalar.activation(hnT[:, ct, w2_ * P:(w2_ + 1) * P], X[2][:, (2 + ct) * P:(3 + ct) * P],
                                                ACT.Identity, bias=W2["ln_b"][:, ct:ct + 1], scale=W2["ln_g"][:, ct:ct + 1])
            last.then_inc(s_hTe, 1)

        def squares_and_v(t, w_):
            act.wait_ge(s_q, t + 1)
            need(act, s_ss, 2 * t - 1)
            nc.scalar.activation(sq[:, 0], X[0][:], ACT.Square).then_inc(s_sq, 1)
            act.wait_ge(s_k, t + 1)
            nc.scalar.activation(sq[:, 1], X[1][:], ACT.Square).then_inc(s_sq, 1)
            act.wait_ge(s_v, t + 1)
            need(act, s_AV, t - 2)
            nc.scalar.activation(v[:, w_], X[2][:], ACT.Copy).then_inc(s_ve, 1)

        def gate(T, i, w_, layer):
            c = 3 * (w_ % 2) + i
            rows = P if c < CHUNKS - 1 else LAST
            act.wait_ge(s_F, 3 * (T - TILES) + i + 1)
            nc.scalar.activation(g_sb[w_ // 2][0:rows, c], F[i % 2][0:rows, 1], ACT.Identity,
                                 bias=W[layer(-1)]["b1"][0:rows, 1, c:c + 1]).then_inc(s_Fg, 1)

        act.wait_ge(s_w, WEIGHTS)
        act.wait_ge(s_c, 12)
        evacuate_hT(-1, -1, 3, lambda d: 0)
        squares_and_v(0, 0)

        def one(n, par, r, layer):
            for w_ in range(TILES):
                T = TILES * n + w_
                p = w_ % 2
                live, feed = tile_exists(T), seq_exists(n - 1)
                if live:
                    act.wait_ge(s_qkT, 2 * T + 1)
                    nc.scalar.activation(qT[:], X[0][:], ACT.Copy).then_inc(s_qkTe, 1)
                    act.wait_ge(s_qkT, 2 * T + 2)
                    nc.scalar.activation(kT[:, :, p], X[1][:].rearrange("p (b q) -> p b q", q=P), ACT.Copy
                                         ).then_inc(s_qkTe, 1)
                if w_ % 2 == 0:
                    h, d = (1, 2) if w_ == 0 else (0, 1)
                    m = n - d
                    if seq_exists(m):
                        act.wait_ge(s_Fg, 3 * (TILES * m + 2 * h + 2))
                        nc.scalar.activation(g_sb[h][:, 0:CHUNKS - 1], g_sb[h][:, 0:CHUNKS - 1], ACT.Gelu)
                        nc.scalar.activation(g_sb[h][0:LAST, CHUNKS - 1], g_sb[h][0:LAST, CHUNKS - 1], ACT.Gelu
                                             ).then_inc(s_ge, 1)
                if feed:
                    gate(T, 0, w_, layer)
                if tile_exists(T - 1):
                    act.wait_ge(s_oT, T)
                    nc.scalar.activation(oT[:], M[:], ACT.Copy).then_inc(s_oTe, 1)
                if tile_exists(T + 1) or tile_exists(T - 2):
                    evacuate_hT(T, n, w_, layer)
                if live:
                    exps(T, w_, 0)
                if tile_exists(T + 1):
                    squares_and_v(T + 1, (w_ + 1) % TILES)
                if live:
                    act.wait_ge(s_PT, 2 * T + 1)
                    evacuate_PT(w_, 0)
                if feed:
                    gate(T, 1, w_, layer)
                if live:
                    exps(T, w_, 1)
                if feed:
                    gate(T, 2, w_, layer)
                if live:
                    act.wait_ge(s_PT, 2 * T + 2)
                    evacuate_PT(w_, 1)
                if isinstance(n, int) and n == ALL_SEQS + 1:
                    break

        def keys(w_):
            return slice(0, P) if w_ == 0 else slice(0, 2 * P)

        def exps(T, w_, hf):
            act.wait_ge(s_nb, 2 * T + hf + 1)
            for e in range(2):
                for ps in range(2):
                    i, h = 2 * e + ps, 4 * hf + 2 * ps + e
                    last = nc.scalar.activation(probs[hf][:, i, keys(w_)], SB[:, i, keys(w_)], ACT.Exp,
                                                bias=nb[hf][:, i:i + 1], scale=rn[w_ % 2][:, h:h + 1],
                                                accum_out=rs[w_ % 2][:, h:h + 1])
            last.then_inc(s_pr, 1)

        def evacuate_PT(w_, hf):
            nc.scalar.activation(PT[hf][:, :, keys(w_)], SB[:, :, keys(w_)], ACT.Copy).then_inc(s_PTe, 1)

        sequences(act, one)

    @block.vector
    def _(dve):
        def rot_products(t, w_, layer):
            for i in range(2):
                dve.wait_ge(s_sq, 2 * t + i + 1)
                if i == 0:
                    need(dve, s_qr, t)
                else:
                    need(dve, s_ks, t)
                src = X[i][:].rearrange("p (h d) -> p h d", d=LDIM)
                rows = tab[layer][:, w_]
                cos = rows[:, 2 * i].unsqueeze(1).to_broadcast([P, LHEADS, LDIM])
                sin = rows[:, 2 * i + 1].unsqueeze(1).to_broadcast([P, LHEADS, LDIM])
                H = LDIM // 2
                nc.vector.tensor_tensor(t1[i][:], src, cos, ALU.mult)
                nc.vector.tensor_tensor(t2[i][:, :, 0:H], src[:, :, H:LDIM], sin[:, :, 0:H], ALU.mult)
                nc.vector.tensor_tensor(t2[i][:, :, H:LDIM], src[:, :, 0:H], sin[:, :, H:LDIM], ALU.mult
                                        ).then_inc(s_rot, 1)
            nc.vector.tensor_reduce(out=ss[:].rearrange("p (a h) -> p a h", a=2), in_=sq[:], axis=AX.X, op=ALU.add
                                    ).then_inc(s_ss, 1)
            dve.wait_ge(s_ss, 2 * t + 1)
            need(dve, s_rn, t)
            nc.vector.tensor_scalar(ssc[:], ss[:], 1e-24, None, ALU.max).then_inc(s_ss, 1)

        def scale_k(t, p):
            dve.wait_ge(s_rn, t + 1)
            need(dve, s_qkT, 2 * t)
            nc.vector.tensor_tensor(k_rot[:], k_sum[:], rn[p][:, LHEADS:2 * LHEADS].unsqueeze(2)
                                    .to_broadcast([P, LHEADS, LDIM]), ALU.mult).then_inc(s_kr, 1)

        def row_max(T, w_, hf):
            cols = slice(0, P) if w_ == 0 else slice(0, 2 * P)
            dve.wait_ge(s_S, 2 * T + hf + 1)
            nc.vector.tensor_reduce(out=mx[:], in_=SB[:, :, cols], axis=AX.X, op=ALU.max).then_inc(s_mx, 1)
            dve.wait_ge(s_mx, 2 * T + hf + 1)
            nc.vector.scalar_tensor_tensor(
                out=nb[hf][:].rearrange("p (e s) -> p e s", e=2), in0=mx[:].rearrange("p (e s) -> p e s", e=2),
                scalar=-1.0, in1=rn[w_ % 2][:, 4 * hf:4 * hf + 4].rearrange("p (s e) -> p e s", e=2),
                op0=ALU.mult, op1=ALU.mult).then_inc(s_nb, 1)

        def value(T, i, w_, layer):
            c = 3 * (w_ % 2) + i
            rows = P if c < CHUNKS - 1 else LAST
            dve.wait_ge(s_Fg, 3 * (T - TILES) + i + 1)
            nc.vector.tensor_scalar(a_sb[w_ // 2][0:rows, c], F[i % 2][0:rows, 0],
                                    W[layer(-1)]["b1"][0:rows, 0, c:c + 1], None, ALU.add).then_inc(s_Fa, 1)

        dve.wait_ge(s_w, WEIGHTS)
        dve.wait_ge(s_c, 12)
        for layer in range(LAYERS):
            for t in range(TILES):
                nc.vector.tensor_tensor(tab[layer][:, t], base_tab[:, t], srow[layer][:], ALU.mult).then_inc(s_tab, 1)
        dve.wait_ge(s_tab, LAYERS * TILES)
        rot_products(0, 0, 0)
        scale_k(0, 0)

        def one(n, par, r, layer):
            for w_ in range(TILES):
                T = TILES * n + w_
                p = w_ % 2
                live, feed = tile_exists(T), seq_exists(n - 1)
                if tile_exists(T - 1):
                    dve.wait_ge(s_AV, T)
                    nc.vector.reciprocal(rinv[:], rs[1 - p][:]).then_inc(s_ri, 1)
                    dve.wait_ge(s_ri, T)
                    nc.vector.tensor_tensor(o_n[:].rearrange("p (h d) -> p h d", d=LDIM),
                                            M[:].rearrange("p (h d) -> p h d", d=LDIM),
                                            rinv[:].unsqueeze(2).to_broadcast([P, LHEADS, LDIM]), ALU.mult
                                            ).then_inc(s_on, 1)
                if tile_exists(T - 2):
                    n2, w2_ = back(n, w_, 2)
                    p2 = par if w_ >= 2 else 1 - par
                    dve.wait_ge(s_rs, T - 1)
                    need(dve, s_hT, T + 1)
                    nc.vector.tensor_scalar(hn[:, 0:P], x2[p2][:, w2_, 0:P], mv[p][:, 0:1], rstd[p][:, 0:1],
                                            ALU.subtract, ALU.mult)
                    nc.vector.tensor_scalar(hn[:, P:CH], hs[:, w2_], mv[p][:, 0:1], rstd[p][:, 0:1],
                                            ALU.subtract, ALU.mult).then_inc(s_hn, 1)
                if feed:
                    value(T, 0, w_, layer)
                if live:
                    row_max(T, w_, 0)
                if tile_exists(T - 1):
                    n1, w1_ = back(n, w_, 1)
                    p1 = par if w_ >= 1 else 1 - par
                    dve.wait_ge(s_wo, T)
                    nc.vector.tensor_tensor(x2[p1][:, w1_], M[:, 0:CH], x_tok[p1][:, w1_], ALU.add).then_inc(s_x2, 1)
                if tile_exists(T + 1):
                    rot_products(T + 1, (w_ + 1) % TILES, layer(0 if w_ < 3 else 1))
                if feed:
                    value(T, 1, w_, layer)
                if live:
                    row_max(T, w_, 1)
                if tile_exists(T + 1):
                    scale_k(T + 1, 1 - p)
                if feed:
                    value(T, 2, w_, layer)
                if tile_exists(T - 1):
                    q = 1 - p
                    n1_count = n1 + 1
                    dve.wait_ge(s_sh[w1_], (48 if w1_ < TILES - 1 else 32) * n1_count)
                    if w1_ > 0:
                        dve.wait_ge(s_sh[w1_ - 1], 48 * n1_count)
                    nc.vector.bn_stats(stats[:, 0], x2[p1][:, w1_, 0:P]).then_inc(s_st, 1)
                    nc.vector.bn_stats(stats[:, 1], hs[:, w1_]).then_inc(s_st, 1)
                    dve.wait_ge(s_st, 4 * (T - 1) + 2)
                    nc.vector.memset(carrier[:], 0.0)
                    nc.vector.bn_aggr(mv[q][:], stats[:]).then_inc(s_st, 1)
                    dve.wait_ge(s_st, 4 * (T - 1) + 3)
                    nc.vector.tensor_scalar(ve[q][:, 0:1], mv[q][:, 1:2], EPS, None, ALU.add).then_inc(s_st, 1)
                if w_ % 2 == 0:
                    h, d = (1, 2) if w_ == 0 else (0, 1)
                    m = n - d
                    pm = par if d == 2 else 1 - par
                    if seq_exists(m):
                        dve.wait_ge(s_w2, 2 * m + h + 1)
                        if not (isinstance(m, int) and m == 0):
                            dve.wait_ge(s_stored[h], 16 * m)
                        nc.vector.tensor_tensor(xo[h][:], F[1][:], x2[pm][:, 2 * h:2 * h + 2], ALU.add).then_inc(s_xo, 1)
                        if layer(-d) == LAYERS - 1:
                            final(m, h)
                if isinstance(n, int) and n == ALL_SEQS + 1:
                    break

        def final(m, h):
            j = 2 * (m - SEQS) + h
            dve.wait_ge(s_xo, 2 * m + h + 1)
            dve.wait_ge(s_x0[h], 16 * (m - SEQS + 1))
            nc.vector.tensor_tensor(xo[h][:], xo[h][:], x0[h][:], ALU.add).then_inc(s_fs, 1)
            dve.wait_ge(s_fs, 6 * j + 1)
            for t in range(2):
                nc.vector.bn_stats(fstats[:, t], xo[h][:, t]).then_inc(s_fs, 1)
            dve.wait_ge(s_fs, 6 * j + 3)
            nc.vector.memset(carrier[:], 0.0)
            for t in range(2):
                nc.vector.bn_aggr(fmv[:, t], fstats[:, t]).then_inc(s_fs, 1)
            dve.wait_ge(s_fs, 6 * j + 5)
            nc.vector.tensor_scalar(fve[:, :, 0], fmv[:, :, 1], EPS, None, ALU.add).then_inc(s_fs, 1)
            dve.wait_ge(s_fr, j + 1)
            for t in range(2):
                last = nc.vector.tensor_scalar(y[h][:, t], xo[h][:, t], fmv[:, t, 0:1], frstd[:, t, 0:1],
                                               ALU.subtract, ALU.mult)
            last.then_inc(s_y, 1)

        sequences(dve, one)

    @block.tensor
    def _(pe):
        def keys(w_):
            return slice(0, P) if w_ == 0 else slice(0, 2 * P)

        def transpose_h(T, n, w_, par):
            need(pe, s_ve, min(T + 1, ALL_TILES) if isinstance(T, int) else T + 1)
            if not (isinstance(T, int) and T < 0):
                pe.wait_ge(s_hTe, T + 1)
            if tile_exists(T + 1):
                wn = (w_ + 1) % TILES
                pn = par if w_ < TILES - 1 else 1 - par
                if wn == 0:
                    pe.wait_ge(s_x[pn], x_count(n + 1, pn))
                for ct in range(CT):
                    last = nc.tensor.transpose(X[2][:, ct * P:(ct + 1) * P], x_tok[pn][:, wn, ct * P:(ct + 1) * P], ident[:])
            if tile_exists(T - 2):
                pe.wait_ge(s_hn, T - 1)
                for ct in range(CT):
                    last = nc.tensor.transpose(X[2][:, (2 + ct) * P:(3 + ct) * P], hn[:, ct * P:(ct + 1) * P], ident[:])
            last.then_inc(s_hT, 1)

        counts = {}

        def x_count(n, pn):
            return 16 * (n // 2 + 1) if isinstance(n, int) else counts["next"]

        def qkv(t, layer):
            pe.wait_ge(s_hTe, t + 1)
            need(pe, s_qkTe, 2 * t)
            wt = W[layer]["qkv"]
            for i, s in enumerate((s_q, s_k, s_v)):
                for k in range(CT):
                    last = nc.tensor.matmul(X[i][:], hT_of(t, k), wt[:, k, i * INNER:(i + 1) * INNER],
                                            start=(k == 0), stop=(k == CT - 1))
                last.then_inc(s, 1)

        tile_parity = {}

        def hT_of(t, k):
            p = tile_parity["next"]
            return hT0[p][:] if k == 0 else hT1[p][:, 0:P]

        def scores(T, w_, hf):
            need(pe, s_PTe, 2 * T + hf)
            cols = keys(w_)
            m = mask[w_ % 2][:].rearrange("p a q -> p (a q)")[:, cols]
            for e in range(2):
                nc.tensor.matmul(SB[:, 2 * e:2 * e + 2, cols], identb[:],
                                 m.unsqueeze(1).to_broadcast([P, 2, cols.stop]), start=True, stop=False,
                                 skip_group_check=True)
            if hf == 0:
                pe.wait_ge(s_qkTe, 2 * T + 2)
            for ps in range(2):
                for e in range(2):
                    rows = slice(64 * e, 64 * e + 64)
                    last = nc.tensor.matmul(SB[:, 2 * e + ps, cols], qT[rows, 2 * hf + ps],
                                            kT[rows, 2 * hf + ps].rearrange("p a q -> p (a q)")[:, cols],
                                            start=False, stop=True, skip_group_check=True)
            last.then_inc(s_S, 1)

        def transpose_probs(T, w_, hf):
            pe.wait_ge(s_pr, 2 * T + hf + 1)
            for i in range(4):
                for a in range(1 if w_ == 0 else 2):
                    last = nc.tensor.transpose(SB[:, i, a * P:(a + 1) * P], probs[hf][:, i, a * P:(a + 1) * P], ident[:])
            last.then_inc(s_PT, 1)

        def times_v(t, w_, hf):
            pe.wait_ge(s_PTe, 2 * t + hf + 1)
            slots = 1 if w_ == 0 else 2
            for e in range(2):
                for ps in range(2):
                    i, h = 2 * e + ps, 4 * hf + 2 * ps + e
                    for a in range(slots):
                        first = hf == 0 and i == 0 and a == 0
                        last = nc.tensor.matmul(M[:, h * LDIM:(h + 1) * LDIM], PT[hf][:, i, a * P:(a + 1) * P],
                                                v[:, w_ if a == w_ % 2 else w_ - 1, h * LDIM:(h + 1) * LDIM], start=first,
                                                stop=(hf == 1 and i == 3 and a == slots - 1), skip_group_check=True)
            if hf == 1:
                last.then_inc(s_AV, 1)

        def hidden(T, i, w_, layer):
            f = 3 * (T - TILES) + i
            c, hf = 3 * (w_ % 2) + i, w_ // 2
            if i == 0:
                need(pe, s_Fa, f)
            elif i == 1:
                need(pe, s_Fa, f - 2)
                if w_ % 2 == 1:
                    need(pe, s_xo, counts["halves"])
            else:
                pe.wait_ge(s_Fa, f - 1)
            size = P if c < CHUNKS - 1 else LAST
            w1 = W[layer(-1)]["w1"]
            for part in range(2):
                for k in range(CT):
                    col = part * HID + c * P
                    last = nc.tensor.matmul(F[i % 2][0:size, part], w1[:, k, col:col + size],
                                            hnT[:, k, hf * 2 * P:(hf + 1) * 2 * P], start=(k == 0), stop=(k == CT - 1))
            last.then_inc(s_F, 1)

        pe.wait_ge(s_w, WEIGHTS)
        pe.wait_ge(s_c, 12)
        tile_parity["next"] = 0
        transpose_h(-1, -1, 3, 1)
        qkv(0, 0)

        def one(n, par, r, layer):
            for w_ in range(TILES):
                T = TILES * n + w_
                live, feed = tile_exists(T), seq_exists(n - 1)
                counts["next"] = 16 * (r + 1 + par)
                counts["halves"] = 2 * n - 2 + (w_ == 3) if w_ % 2 else None
                tile_parity["next"] = (w_ + 1) % 2
                if tile_exists(T - 1):
                    n1, w1_ = back(n, w_, 1)
                    times_v(T - 1, w1_, 1)
                if live:
                    pe.wait_ge(s_qr, T + 1)
                    for b in range(PAIRS):
                        last = nc.tensor.transpose(X[0][:, b * P:(b + 1) * P], q_rot[:, 2 * b:2 * b + 2].rearrange("p h d -> p (h d)"), ident[:])
                    last.then_inc(s_qkT, 1)
                    pe.wait_ge(s_kr, T + 1)
                    for b in range(PAIRS):
                        last = nc.tensor.transpose(X[1][:, b * P:(b + 1) * P], k_rot[:, 2 * b:2 * b + 2].rearrange("p h d -> p (h d)"), ident[:])
                    last.then_inc(s_qkT, 1)
                if feed:
                    hidden(T, 0, w_, layer)
                if tile_exists(T - 1):
                    pe.wait_ge(s_on, T)
                    for b in range(IH):
                        last = nc.tensor.transpose(M[:, b * P:(b + 1) * P], o_n[:, b * P:(b + 1) * P], ident[:])
                    last.then_inc(s_oT, 1)
                if live:
                    scores(T, w_, 0)
                if tile_exists(T + 1) or tile_exists(T - 2):
                    transpose_h(T, n, w_, par)
                if tile_exists(T - 1):
                    pe.wait_ge(s_oTe, T)
                    wo = W[layer(0 if w_ >= 1 else -1)]["o"]
                    for b in range(IH):
                        last = nc.tensor.matmul(M[:, 0:CH], oT[:, b], wo[:, b], start=(b == 0), stop=(b == IH - 1))
                    last.then_inc(s_wo, 1)
                if tile_exists(T + 1):
                    qkv(T + 1, layer(0 if w_ < 3 else 1))
                if live:
                    transpose_probs(T, w_, 0)
                if feed:
                    hidden(T, 1, w_, layer)
                if live:
                    scores(T, w_, 1)
                    need(pe, s_x2, T)
                    pe.wait_ge(s_ve, T + 1)
                    times_v(T, w_, 0)
                if feed:
                    hidden(T, 2, w_, layer)
                if w_ % 2 == 0:
                    h, d = (1, 2) if w_ == 0 else (0, 1)
                    m = n - d
                    if seq_exists(m):
                        pe.wait_ge(s_um, 2 * m + h + 1)
                        if feed:
                            pe.wait_ge(s_Fa, 3 * (T - TILES) + 2)
                        w2 = W[layer(-d)]["w2"]
                        for t in range(2):
                            for c in range(CHUNKS):
                                rows = P if c < CHUNKS - 1 else LAST + 1
                                last = nc.tensor.matmul(F[1][:, t], a_sb[h][0:rows, c, t * P:(t + 1) * P],
                                                        w2[0:rows, c], start=(c == 0), stop=(c == CHUNKS - 1))
                        last.then_inc(s_w2, 1)
                if live:
                    transpose_probs(T, w_, 1)
                if isinstance(n, int) and n == ALL_SEQS + 1:
                    break

        sequences(pe, one)


def rotary_tables():
    d = np.arange(0, LDIM, 2, dtype=np.float32)
    t = np.arange(SEQ, dtype=np.float32)
    freqs = t[:, None] * (np.float32(1.0) / np.float32(10000.0) ** (d / np.float32(LDIM)))[None, :]
    base = (d + np.float32(0.4 * LDIM)) / np.float32(1.4 * LDIM)
    scale = base[None, :] ** ((t - np.float32(SEQ // 2)) / np.float32(64.0))[:, None]
    cos, sin = np.cos(freqs), np.sin(freqs)
    both = lambda a, b: np.concatenate([a, b], axis=1)
    q = [np.float32(8.0) * both(cos * scale, cos * scale), np.float32(8.0) * both(-sin * scale, sin * scale)]
    k = [both(cos / scale, cos / scale), both(-sin / scale, sin / scale)]
    return np.stack(q + k, axis=1).astype(np.float32)


def build(nc, w, y_out):
    x_a = nc.dram_tensor("x_after_heads", (SEQS, SEQ, CH), F32).ap()
    x_b = nc.dram_tensor("x_after_layer", (SEQS, SEQ, CH), F32).ap()
    with ExitStack() as ctx:
        consts = make_constants(nc, ctx)
        W0 = load_layer(nc, ctx, 0)
        with ExitStack() as stage:
            head_attention(nc, stage, w["x"], w, x_a, consts, W0)
        with ExitStack() as stage:
            W1 = load_layer(nc, stage, 1)
            layers(nc, stage, x_a, x_b, y_out, w, [W0, W1], consts)


def kernel(**inputs):
    import concourse.bacc as bacc
    from concourse.bass_utils import run_bass_kernel_spmd

    g = {name[3:]: np.asarray(value) for name, value in inputs.items()}

    def head_order(a):
        return a.reshape(a.shape[:-1] + (CT, JH, HDIM)).swapaxes(-1, -2).reshape(a.shape)

    def on_partitions(a):
        a = np.concatenate([a, np.zeros(a.shape[:-1] + (-a.shape[-1] % P,), a.dtype)], axis=-1)
        return np.moveaxis(a.reshape(a.shape[:-1] + (-1, P)), -1, 1)

    def swapped(a):
        return np.concatenate([a[..., LDIM // 2:], a[..., :LDIM // 2]], axis=-1)

    arrays = {
        "x": g["attn_x"],
        "Wq": head_order(g["attn_Wq"].T), "Wk": head_order(g["attn_Wk"].T),
        "Wv": g["attn_Wv"].T, "Wo": g["attn_Wo"].T,
        "bq": head_order(g["attn_bq"]).reshape(CT, P).T, "bk": head_order(g["attn_bk"]).reshape(CT, P).T,
        "bv": g["attn_bv"], "bo": g["attn_bo"],
        "wqkv": g["ffn_wqkv"], "wo2": g["ffn_wo"], "w1": g["ffn_w1"], "w2": g["ffn_w2"],
        "b1": on_partitions(g["ffn_b1"].reshape(LAYERS, 2, HID)), "b2": g["ffn_b2"],
        "ln_g": on_partitions(g["ffn_ln_g"]), "ln_b": on_partitions(g["ffn_ln_b"]),
        "q_scale": g["ffn_q_scale"], "k_scale": g["ffn_k_scale"],
        "q_scale_swapped": swapped(g["ffn_q_scale"]), "k_scale_swapped": swapped(g["ffn_k_scale"]),
        "tab": rotary_tables(),
    }
    arrays = {name: np.ascontiguousarray(a) for name, a in arrays.items()}
    nc = bacc.Bacc("TRN2", target_bir_lowering=False, num_devices=1)
    w = {name: nc.dram_tensor(f"in_{name}", a.shape, F32, kind="ExternalInput").ap() for name, a in arrays.items()}
    out = nc.dram_tensor("out_0", (SEQS, SEQ, CH), F32, kind="ExternalOutput").ap()
    build(nc, w, out)
    result = run_bass_kernel_spmd(nc, [{f"in_{name}": a for name, a in arrays.items()}], core_ids=[0])
    return result.results[0]["out_0"]
```

```python
from contextlib import ExitStack

import numpy as np

import concourse.bass as bass
from concourse import mybir

F32 = mybir.dt.float32
F32R = mybir.dt.float32r
BF16 = mybir.dt.bfloat16
ACT = mybir.ActivationFunctionType
ALU = mybir.AluOpType
AX = mybir.AxisListType

P = 128
SEQS, SEQ, CH = 16, 512, 256
TILES = SEQ // P
CT = CH // P
HEADS, HDIM = 16, 16
JH = HEADS // CT
UNITS = TILES * TILES
EPS = 1e-5
TERMS = [(0, 0), (0, 1), (1, 0), (1, 1), (0, 2), (2, 0), (1, 2), (2, 1)]


def need(engine, sem, value):
    if not (isinstance(value, int) and value <= 0):
        engine.wait_ge(sem, value)


def lagged(n, u, lag, steps):
    return (n, 0, u - lag) if u >= lag else (n - 1, 1, u - lag + steps)


def exists(n):
    return not isinstance(n, int) or 0 <= n < SEQS


def head_attention(nc, ctx, x_in, w, x_out, consts, W0=None, raw=None):
    ident, identr, half = consts["ident"], consts["identr"], consts["minus_half"]
    ones_row, minus_identb = consts["ones_row"], consts["minus_identb"]

    def sb(name, shape, dtype=F32):
        return ctx.enter_context(nc.sbuf_tensor("a_" + name, shape, dtype))

    def sem(name):
        return ctx.enter_context(nc.semaphore("a_" + name))

    def bank(name, shape=(P, 512)):
        return ctx.enter_context(nc.psum_tensor("a_" + name, list(shape), F32))

    wq, wk, wv, wo = (sb(n, [P, CT, CH]) for n in ("wq", "wk", "wv", "wo"))
    bq, bk = (sb(n, [P, CT]) for n in ("bq", "bk"))
    bv_rows, bo_row = sb("bv", [P, CH]), sb("bo", [1, CH])
    x_tok = [sb(f"x{i}", [P, TILES, CH]) for i in range(2)]
    xT = sb("xT", [P, CT, SEQ])
    parts = [sb(f"parts{i}", [P, 3, CT, SEQ], BF16) for i in range(2)]
    qk8 = [[sb(f"{n}8{i}", [P, JH, CT, SEQ], BF16) for n in "qk"] for i in range(2)]
    v_pad = [sb(f"v{i}", [P, TILES, HEADS // 2, 64]) for i in range(2)]
    NE = 4
    probs = [sb(f"p{i}", [P, HEADS, P]) for i in range(NE)]
    z8, z4 = sb("z8", [P, 8, P]), [sb(f"z4{i}", [P, 4, P]) for i in range(4)]
    zinv = [sb(f"zi{i}", [P, P]) for i in range(2)]
    negmax = [sb(f"nm{i}", [P, P], F32R) for i in range(2)]
    oT = [sb(f"oT{i}", [P, CT, P]) for i in range(2)]
    resid = [sb(f"r{i}", [P, CH]) for i in range(2)]
    stats, carrier, mv = sb("stats", [P, 6]), sb("carrier", [P, 1]), [sb(f"mv{i}", [P, 2]) for i in range(2)]
    vareps, rstd = ([sb(f"{n}{i}", [P, 1]) for i in range(2)] for n in ("ve", "rs"))
    normed = [sb(f"n{i}", [P, CH]) for i in range(2)]

    S = bank("S", (P, HEADS, P))
    O = bank("O", (P, CT, P))
    YZ = bank("YZ", (P, 2, CH))
    Y = YZ[:, 0]
    Z = YZ[:, 1, :P]
    B = [bank("B0"), bank("B1")]

    s_w = sem("weights_loaded")
    s_w0 = sem("next_weights_loaded")
    s_x = [sem(f"x_loaded{i}") for i in range(2)]
    s_pz = sem("vpad_zeroed")
    s_pt = sem("proj_psum")
    s_xT = sem("xT_evacuated")
    s_part = sem("part")
    s_less = sem("less_part")
    s_vv = sem("v_evacuated")
    s_pack = [sem(f"packed{i}") for i in range(2)]
    s_S = sem("scores")
    s_nm = sem("negmax")
    s_sub = sem("scores_less_max")
    s_exp = sem("exp")
    s_zt = sem("z_tree")
    s_z = sem("z")
    s_zi = sem("zinv")
    s_p = sem("probs")
    s_pp = sem("probs_by_pool")
    s_av = sem("av")
    s_oT = sem("oT")
    s_Y = sem("Y")
    s_r = sem("resid")
    s_st = sem("stats_done")
    s_rs = sem("rstd")
    s_n = sem("normed")
    s_out = [sem(f"stored{i}") for i in range(2)]

    PACKED = 16 * 2 * len(TERMS)
    T_AT, QK_AT, V_AT, V_OUT_AT = 5, (6, 7, 9, 10), (12, 13, 14, 15), (14, 15)
    PARTS = 3
    DVE_HEADS = 12
    PART_ORDER = [(0, 0), (0, 1), (1, 0), (0, 2), (1, 1), (1, 2)]
    X_AT = 4
    PACK_AT = (10, 13)
    LAST_LAG = 7

    block = ctx.enter_context(nc.Block())

    def sequences(engine, one):
        one(0, 0, 0)
        with engine.Fori(0, (SEQS - 2) // 2) as i:
            one(2 * i + 1, 1, i)
            one(2 * i + 2, 0, i + 1)
        one(SEQS - 1, 1, SEQS // 2 - 1)
        one(SEQS, 0, SEQS // 2)

    def part_count(n, i, part):
        return PARTS * 4 * n + PARTS * CT * (i // CT) + PART_ORDER.index((i % CT, part)) + 1

    def less_count(n, i, part):
        return 8 * n + 4 * (i // CT) + 2 * (i % CT) + part + 1

    def parts_at(u):
        return [(i, u - QK_AT[i]) for i in range(4) if 0 <= u - QK_AT[i] < PARTS]

    def units_of(n):
        return range(UNITS if exists(n) else LAST_LAG + 1)

    @block.sync
    def _(sp):
        def load_x(n, par):
            sp.dma_start(x_tok[par][:], x_in[bass.ts(n, 1), :, :].rearrange("a (t p) c -> p (a t) c", p=P)
                         ).then_inc(s_x[par], 16)

        def pack(n, par, which):
            sp.wait_ge(s_part, part_count(n, CT * which + CT - 1, 2))
            for t, (of_k, of_q) in enumerate(TERMS):
                part = of_k if which else of_q
                sp.dma_start(qk8[par][which][16 * t:16 * t + 16], parts[which][:, part]).then_inc(s_pack[par], 16)

        for dst, name in ((wq, "Wq"), (wk, "Wk"), (wv, "Wv"), (wo, "Wo")):
            sp.dma_start(dst[:], w[name].rearrange("(k p) o -> p k o", p=P)).then_inc(s_w, 16)
        sp.dma_start(bq[:], w["bq"]).then_inc(s_w, 16)
        sp.dma_start(bk[:], w["bk"]).then_inc(s_w, 16)
        sp.dma_start(bv_rows[:], w["bv"].partition_broadcast(P)).then_inc(s_w, 16)
        sp.dma_start(bo_row[:], w["bo"].unsqueeze(0)).then_inc(s_w, 16)
        load_x(0, 0)
        if W0 is not None:
            start_layer_loads(sp, W0, w, 0, s_w0)
            load_raw(sp, raw, w, 0, s_w0)
        pack(0, 0, 0)
        pack(0, 0, 1)

        def one(n, par, r):
            for u in units_of(n):
                if u == X_AT and exists(n) and exists(n + 1):
                    need(sp, s_r, TILES * n)
                    load_x(n + 1, 1 - par)
                if u in PACK_AT and exists(n) and exists(n + 1):
                    pack(n + 1, 1 - par, PACK_AT.index(u))
                nn, back, uu = lagged(n, u, 7, UNITS)
                if uu % TILES == TILES - 1 and exists(nn):
                    qt = uu // TILES
                    sp.wait_ge(s_n, TILES * nn + qt + 1)
                    sp.dma_start(x_out[bass.ts(nn, 1), qt * P:(qt + 1) * P, :].rearrange("a p c -> p (a c)"),
                                 normed[qt % 2][:]).then_inc(s_out[qt % 2], 16)

        sequences(sp, one)
        for i in range(2):
            sp.wait_ge(s_out[i], 16 * SEQS * TILES // 2)
        if W0 is not None:
            sp.wait_ge(s_w0, 16 * (LAYER_LOADS + 1))

    @block.gpsimd
    def _(pool):
        def sum_heads(n, u):
            U = UNITS * n + u
            e = probs[u % NE]
            need(pool, s_zt, 2 * U)
            pool.wait_ge(s_exp, 4 * U + 4)
            nc.gpsimd.tensor_tensor(z8[:], e[:, 0:8], e[:, 8:16], ALU.add).then_inc(s_zt, 1)
            pool.wait_ge(s_zt, 2 * U + 1)
            need(pool, s_z, U - 3)
            nc.gpsimd.tensor_tensor(z4[u % 4][:], z8[:, 0:4], z8[:, 4:8], ALU.add).then_inc(s_zt, 1)

        def normalise(n, u):
            e = probs[u % NE][:, DVE_HEADS:]
            pool.wait_ge(s_zi, UNITS * n + u + 1)
            nc.gpsimd.tensor_tensor(e, e, zinv[u % 2][:].unsqueeze(1).to_broadcast([P, HEADS - DVE_HEADS, P]),
                                    ALU.mult).then_inc(s_pp, 1)

        def rstd_of(n, qt):
            m = TILES * n + qt
            pool.wait_ge(s_st, 3 * m + 3)
            need(pool, s_n, m - 1)
            nc.gpsimd.tensor_tensor(rstd[qt % 2][:], vareps[qt % 2][:], half[:, 0:1], ALU.pow).then_inc(s_rs, 1)

        for i in range(2):
            nc.gpsimd.memset(v_pad[i][:], 0.0).then_inc(s_pz, 1)

        def one(n, par, r):
            for u in units_of(n):
                nn, back, uu = lagged(n, u, 2, UNITS)
                if exists(nn):
                    normalise(nn, uu)
                if exists(n):
                    sum_heads(n, u)
                nn, back, uu = lagged(n, u, 6, UNITS)
                if uu % TILES == TILES - 1 and exists(nn):
                    rstd_of(nn, uu // TILES)

        sequences(pool, one)

    @block.scalar
    def _(act):
        def evacuate_xT(n):
            for ct in range(CT):
                act.wait_ge(s_pt, 8 * n + ct + 1)
                nc.scalar.activation(xT[:, ct], B[ct][:], ACT.Copy).then_inc(s_xT, 1)

        def part_of_qk(n, i, part):
            which, ot = divmod(i, CT)
            if part == 0:
                act.wait_ge(s_pt, 8 * n + 3 + i)
            else:
                act.wait_ge(s_less, less_count(n, i, part - 1))
            nc.scalar.activation(parts[which][:, part, ot], B[ot][:], ACT.Identity,
                                 bias=(bq, bk)[which][:, ot:ot + 1]).then_inc(s_part, 1)

        act.wait_ge(s_w, 16 * 8)
        evacuate_xT(0)
        for which in range(2):
            for ot, part in PART_ORDER:
                part_of_qk(0, CT * which + ot, part)

        def one(n, par, r):
            for u in units_of(n):
                if exists(n):
                    U = UNITS * n + u
                    need(act, s_av, U - NE + 1)
                    for b in range(4):
                        hs = slice(4 * b, 4 * b + 4)
                        act.wait_ge(s_sub, 4 * U + b + 1)
                        nc.scalar.activation(probs[u % NE][:, hs], S[:, hs], ACT.Exp, scale=HDIM ** -0.5).then_inc(s_exp, 1)
                nn, back, uu = lagged(n, u, 3, UNITS)
                if uu % TILES == TILES - 1 and exists(nn):
                    qt = uu // TILES
                    act.wait_ge(s_av, UNITS * nn + uu + 1)
                    need(act, s_Y, TILES * nn + qt - 1)
                    nc.scalar.activation(oT[qt % 2][:], O[:], ACT.Copy).then_inc(s_oT, 1)
                if exists(n) and exists(n + 1):
                    if u == T_AT:
                        evacuate_xT(n + 1)
                    for i, part in parts_at(u):
                        part_of_qk(n + 1, i, part)

        sequences(act, one)

    @block.vector
    def _(dve):
        def evacuate_v(n, par, j):
            need(dve, s_av, UNITS * (n - 1))
            dve.wait_ge(s_pt, 8 * n + 7 + j)
            src = B[j][:].rearrange("p (t h e d) -> p t h e d", t=2, e=2, d=HDIM)
            bias = bv_rows[:].rearrange("p (h e d) -> p h e d", e=2, d=HDIM)
            for e in range(2):
                last = nc.vector.tensor_tensor(
                    v_pad[par][:, 2 * j:2 * j + 2, :, 48 * e:48 * e + HDIM], src[:, :, :, e],
                    bias[:, :, e].unsqueeze(1).to_broadcast([P, 2, HEADS // 2, HDIM]), ALU.add)
            last.then_inc(s_vv, 1)

        dve.wait_ge(s_w, 16 * 8)
        dve.wait_ge(s_pz, 2)
        evacuate_v(0, 0, 0)
        evacuate_v(0, 0, 1)

        def one(n, par, r):
            for u in units_of(n):
                if exists(n):
                    U = UNITS * n + u
                    dve.wait_ge(s_S, U + 1)
                    need(dve, s_sub, 4 * U - 4)
                    nc.vector.tensor_reduce(out=negmax[u % 2][:], in_=S[:].rearrange("p h q -> p q h"),
                                            axis=AX.X, op=ALU.max, negate=True).then_inc(s_nm, 1)
                nn, back, uu = lagged(n, u, 2, UNITS)
                if exists(nn):
                    U = UNITS * nn + uu
                    dve.wait_ge(s_z, U + 1)
                    need(dve, s_pp, U - 1)
                    nc.vector.reciprocal(zinv[uu % 2][:], Z).then_inc(s_zi, 1)
                    dve.wait_ge(s_zi, U + 1)
                    e = probs[uu % NE][:, :DVE_HEADS]
                    nc.vector.tensor_tensor(e, e, zinv[uu % 2][:].unsqueeze(1).to_broadcast([P, DVE_HEADS, P]),
                                            ALU.mult).then_inc(s_p, 1)
                nn, back, uu = lagged(n, u, 7, UNITS)
                if uu % TILES == TILES - 1 and exists(nn):
                    qt = uu // TILES
                    m = TILES * nn + qt
                    dve.wait_ge(s_rs, m + 1)
                    need(dve, s_out[qt % 2], 16 * (2 * nn + qt // 2))
                    nc.vector.tensor_scalar(normed[qt % 2][:], resid[qt % 2][:], mv[qt % 2][:, 0:1],
                                            rstd[qt % 2][:, 0:1], ALU.subtract, ALU.mult).then_inc(s_n, 1)
                nn, back, uu = lagged(n, u, 6, UNITS)
                if uu % TILES == TILES - 1 and exists(nn):
                    qt = uu // TILES
                    m = TILES * nn + qt
                    dve.wait_ge(s_st, 3 * m + 1)
                    nc.vector.memset(carrier[:], 0.0)
                    nc.vector.bn_aggr(mv[qt % 2][:], stats[:]).then_inc(s_st, 1)
                    dve.wait_ge(s_st, 3 * m + 2)
                    nc.vector.tensor_scalar(vareps[qt % 2][:], mv[qt % 2][:, 1:2], EPS, None, ALU.add).then_inc(s_st, 1)
                nn, back, uu = lagged(n, u, 5, UNITS)
                if uu % TILES == TILES - 1 and exists(nn):
                    qt = uu // TILES
                    m = TILES * nn + qt
                    pn = par if not back else 1 - par
                    dve.wait_ge(s_Y, m + 1)
                    nc.vector.tensor_tensor(resid[qt % 2][:], Y, x_tok[pn][:, qt], ALU.add).then_inc(s_r, 1)
                    dve.wait_ge(s_r, m + 1)
                    nc.vector.bn_stats(stats[:], resid[qt % 2][:]).then_inc(s_st, 1)
                if u in V_OUT_AT and exists(n) and exists(n + 1):
                    evacuate_v(n + 1, 1 - par, V_OUT_AT.index(u))

        sequences(dve, one)

    @block.tensor
    def _(pe):
        def piece_free(n, piece):
            if piece < 2:
                need(pe, s_vv, 2 * n - 1 + piece)
            elif piece < 4:
                pe.wait_ge(s_xT, 2 * n + piece - 1)
            else:
                pe.wait_ge(s_part, part_count(n, piece - 4, PARTS - 1))

        def transpose_x(n, par):
            for ct in range(CT):
                piece_free(n, ct)
                for t in range(TILES):
                    last = nc.tensor.transpose(B[ct][:, t * P:(t + 1) * P], x_tok[par][:, t, ct * P:(ct + 1) * P], ident[:])
                last.then_inc(s_pt, 1)

        def project_qk(n, i, k):
            which, ot = divmod(i, CT)
            if k == 0:
                piece_free(n, 2 + i)
            if i == 0 and k == 0:
                pe.wait_ge(s_xT, 2 * n + 2)
            last = nc.tensor.matmul(B[ot][:], (wq, wk)[which][:, k, ot * P:(ot + 1) * P], xT[:, k],
                                    start=(k == 0), stop=(k == CT - 1), skip_group_check=True)
            if k == CT - 1:
                last.then_inc(s_pt, 1)

        def less_part(n, i, part):
            which, ot = divmod(i, CT)
            pe.wait_ge(s_part, part_count(n, i, part))
            nc.tensor.matmul(B[ot][:], minus_identb[:], parts[which][:, part, ot], start=False, stop=True,
                             skip_group_check=True).then_inc(s_less, 1)

        def project_v(n, tile, k):
            j, t = divmod(tile, 2)
            if t == 0 and k == 0:
                piece_free(n, 6 + j)
            last = nc.tensor.matmul(B[j][:, t * CH:(t + 1) * CH], xT[:, k, tile * P:(tile + 1) * P], wv[:, k],
                                    start=(k == 0), stop=(k == CT - 1), skip_group_check=True)
            if t == 1 and k == CT - 1:
                last.then_inc(s_pt, 1)

        def output(n, uu, k):
            qt = uu // TILES
            m = TILES * n + qt
            if k == 0:
                pe.wait_ge(s_oT, m + 1)
                need(pe, s_r, m)
                last_sum = UNITS * n + uu + 3
                pe.wait_ge(s_zi, min(last_sum, UNITS * SEQS) if isinstance(n, int) else last_sum)
                nc.tensor.matmul(Y, ones_row[0:1, :], bo_row[0:1, :], start=True, stop=False, skip_group_check=True)
            last = nc.tensor.matmul(Y, oT[qt % 2][:, k], wo[:, k], start=False, stop=(k == CT - 1),
                                    skip_group_check=True)
            if k == CT - 1:
                last.then_inc(s_Y, 1)

        def project(n, u, k):
            if exists(n) and exists(n + 1):
                for i, part in parts_at(u - 1):
                    if k == 0 and part < PARTS - 1:
                        less_part(n + 1, i, part)
                if u in QK_AT:
                    project_qk(n + 1, QK_AT.index(u), k)
                if u in V_AT:
                    project_v(n + 1, V_AT.index(u), k)

        pe.wait_ge(s_w, 16 * 8)
        pe.wait_ge(s_x[0], 16)
        transpose_x(0, 0)
        for i in range(2 * CT):
            for k in range(CT):
                project_qk(0, i, k)
            if i % CT == CT - 1:
                for ot, part in PART_ORDER:
                    if part < PARTS - 1:
                        less_part(0, i - 1 + ot, part)
        for tile in range(TILES):
            for k in range(CT):
                project_v(0, tile, k)

        def one(n, par, r):
            for u in units_of(n):
                if exists(n):
                    U = UNITS * n + u
                    if u == 0:
                        pe.wait_ge(s_pack[par], PACKED * (r + 1))
                    qt, kt = u // TILES, u % TILES
                    q8, k8 = qk8[par]
                    for h in range(HEADS):
                        if h % 4 == 0:
                            need(pe, s_exp, 4 * U - 3 + h // 4)
                        last = nc.tensor.matmul(S[:, h], k8[:, h % JH, h // JH, kt * P:(kt + 1) * P],
                                                q8[:, h % JH, h // JH, qt * P:(qt + 1) * P],
                                                start=(h % 4 == 0), stop=(h % 4 == 3))
                    last.then_inc(s_S, 1)
                nn, back, uu = lagged(n, u, 2, UNITS)
                if exists(nn):
                    U = UNITS * nn + uu
                    pe.wait_ge(s_zt, 2 * U + 2)
                    need(pe, s_zi, U)
                    of, _, last_unit = lagged(n, u, 6, UNITS)
                    if last_unit % TILES == TILES - 1 and exists(of):
                        pe.wait_ge(s_r, TILES * of + last_unit // TILES + 1)
                    for j in range(4):
                        last = nc.tensor.matmul(Z, ident[:], z4[uu % 4][:, j], start=(j == 0), stop=(j == 3),
                                                skip_group_check=True)
                    last.then_inc(s_z, 1)
                nn, back, uu = lagged(n, u, 3, UNITS)
                if exists(nn):
                    qt, kt = uu // TILES, uu % TILES
                    pn = par if not back else 1 - par
                    if kt == 0:
                        need(pe, s_oT, TILES * nn + qt)
                    pe.wait_ge(s_p, UNITS * nn + uu + 1)
                    if uu == 0:
                        pe.wait_ge(s_vv, 2 * nn + 2)
                    for t in range(CT):
                        if t == DVE_HEADS // JH:
                            pe.wait_ge(s_pp, UNITS * nn + uu + 1)
                        for e in range(2):
                            for g in range(4):
                                last = nc.tensor.matmul(
                                    O[32 * g:32 * g + 32, t], v_pad[pn][:, kt, 4 * t + g, 32 * e:32 * e + 32],
                                    probs[uu % NE][:, JH * t + 2 * g + e], start=(kt == 0 and t == 0 and e == 0),
                                    stop=(kt == TILES - 1 and e == 1 and t == 1), tile_position=(0, 32 * g),
                                    skip_group_check=True)
                    last.then_inc(s_av, 1)
                project(n, u, 0)
                if exists(n):
                    U = UNITS * n + u
                    pe.wait_ge(s_nm, U + 1)
                    for b in range(4):
                        last = nc.tensor.matmul(S[:, 4 * b:4 * b + 4], identr[:],
                                                negmax[u % 2][:].unsqueeze(1).to_broadcast([P, 4, P]),
                                                start=False, stop=True, skip_group_check=True)
                        last.then_inc(s_sub, 1)
                project(n, u, 1)
                nn, back, uu = lagged(n, u, 4, UNITS)
                if uu % TILES == TILES - 1 and exists(nn):
                    for k in range(CT):
                        output(nn, uu, k)
                if exists(n) and exists(n + 1) and u == T_AT:
                    pe.wait_ge(s_x[1 - par], 16 * (r + 1 + par))
                    transpose_x(n + 1, 1 - par)

        sequences(pe, one)


def make_constants(nc, ctx):
    def sb(name, shape, dtype=F32):
        return ctx.enter_context(nc.sbuf_tensor("c_" + name, shape, dtype))

    c = {"ident": sb("ident", [P, P]), "identr": sb("identr", [P, P], F32R),
         "identb": sb("identb", [P, P], BF16), "minus_identb": sb("minus_identb", [P, P], BF16),
         "minus_half": sb("half", [P, 16]), "ones_row": sb("ones", [1, P])}
    s_i = ctx.enter_context(nc.semaphore("c_identity"))
    with nc.Block() as block:
        @block.gpsimd
        def _(pool):
            nc.gpsimd.memset(c["minus_half"][:], -0.5).then_inc(s_i, 1)
            nc.gpsimd.memset(c["ones_row"][:], 1.0).then_inc(s_i, 1)
            nc.gpsimd.memset(c["ident"][:], 0.0).then_inc(s_i, 1)
            pool.wait_ge(s_i, 3)
            nc.gpsimd.affine_select(out=c["ident"][:], in_=c["ident"][:], compare_op=ALU.not_equal, fill=1.0, base=0,
                                    pattern=[[-1, P]], channel_multiplier=1).then_inc(s_i, 1)

        @block.vector
        def _(dve):
            dve.wait_ge(s_i, 4)
            nc.vector.tensor_copy(c["identr"][:], c["ident"][:]).then_inc(s_i, 1)
            nc.vector.tensor_copy(c["identb"][:], c["ident"][:]).then_inc(s_i, 1)
            nc.vector.tensor_scalar(c["minus_identb"][:], c["ident"][:], -1.0, None, ALU.mult).then_inc(s_i, 1)
            dve.wait_ge(s_i, 7)
    return c


LAYERS = 2
LHEADS, LDIM = 8, 64
INNER = LHEADS * LDIM
HID = int(CH * 4 * 2 / 3)
CHUNKS = -(-HID // P)
HC = -(-HID // CHUNKS)
LAST = HID - (CHUNKS - 1) * HC
ALL_SEQS = LAYERS * SEQS
ALL_TILES = ALL_SEQS * TILES
MASKED = -1e30
PAIRS = INNER // P
IH = INNER // P


def room_for_layer(nc, ctx, tag):
    def sb(name, shape, dtype=F32):
        return ctx.enter_context(nc.sbuf_tensor(f"w{tag}_" + name, shape, dtype))

    return {"o": sb("o", [P, IH, CH]), "w2": sb("w2", [P, CHUNKS, CH]),
            "b1": sb("b1", [P, 2, CHUNKS]), "ln_g": sb("g", [P, CT]), "ln_b": sb("b", [P, CT])}


LAYER_LOADS = 7
SPLITS = [("wqkv", 0), ("w1", 0), ("wqkv", 1), ("w1", 1)]


def load_raw(engine, stage, w, j, sem):
    name, layer = SPLITS[j]
    src = w[name][layer].rearrange("(k p) o -> p k o", p=P)
    engine.dma_start(stage[:, :, 0:src.shape[-1]], src).then_inc(sem, 16)


def start_layer_loads(engine, dst, w, layer, sem):
    full = (CHUNKS - 1) * HC

    def load(out, src):
        engine.dma_start(out, src).then_inc(sem, 16)

    load(dst["o"][:], w["wo2"][layer].rearrange("(k p) o -> p k o", p=P))
    load(dst["w2"][0:HC, 0:CHUNKS - 1], w["w2"][layer, 0:full].rearrange("(k p) o -> p k o", p=HC))
    load(dst["w2"][0:LAST, CHUNKS - 1], w["w2"][layer, full:HID])
    load(dst["w2"][LAST:LAST + 1, CHUNKS - 1], w["b2"][layer:layer + 1])
    load(dst["b1"][0:HC], w["b1"][layer])
    for name in ("ln_g", "ln_b"):
        load(dst[name][:], w[name][layer])


def layers(nc, ctx, x_a, x_b, y_out, w, W, raw, consts):
    ident, half, identb = consts["ident"], consts["minus_half"], consts["identb"]

    def sb(name, shape, dtype=F32):
        return ctx.enter_context(nc.sbuf_tensor("b_" + name, shape, dtype))

    def sem(name):
        return ctx.enter_context(nc.semaphore("b_" + name))

    def bank(name, shape=(P, 512)):
        return ctx.enter_context(nc.psum_tensor("b_" + name, list(shape), F32))

    x_tok = [sb(f"x{i}", [P, TILES, CH]) for i in range(2)]
    x2 = [sb(f"x2{i}", [P, TILES, CH]) for i in range(2)]
    base_tab = sb("base_tab", [P, TILES, 4, LDIM])
    tab = [sb("tab0", [P, TILES, 4, LDIM]), base_tab]
    srow = [sb(f"srow{i}", [P, 4, LDIM]) for i in range(LAYERS)]
    mask = [sb(f"mask{i}", [P, 2, P], BF16) for i in range(2)]
    zero_col = sb("zero_col", [P, 1])
    carrier = sb("carrier", [P, 1])
    HIGH, LOW = 0, 1
    wqkv = sb("wqkv", [P, 2, CT, 3 * INNER], F32R)
    w1 = sb("w1", [P, 2, CT, 2 * HID], F32R)
    hT0 = [sb(f"hT0{i}", [P, 2, P], F32R) for i in range(2)]
    hT1 = [sb(f"hT1{i}", [P, 2, P + 2], F32R) for i in range(2)]
    sq = sb("sq", [P, 2, LHEADS, LDIM])
    t1 = [sb(f"t1{i}", [P, LHEADS, LDIM]) for i in range(2)]
    t2 = [sb(f"t2{i}", [P, LHEADS, LDIM]) for i in range(2)]
    ss = sb("ss", [P, 2 * LHEADS])
    ssc = sb("ssc", [P, 2 * LHEADS])
    rn = [sb(f"rn{i}", [P, 2 * LHEADS]) for i in range(2)]
    qT = sb("qT", [P, 2, PAIRS, P], F32R)
    kT = sb("kT", [P, 2, PAIRS, 2, P], F32R)
    v = sb("v", [P, TILES, INNER])
    mx = sb("mx", [P, 4])
    nb = [sb(f"nb{i}", [P, 4]) for i in range(2)]
    probs = [sb(f"p{i}", [P, 4, 2 * P]) for i in range(2)]
    rs = [sb(f"rs{i}", [P, LHEADS]) for i in range(2)]
    rinv = sb("rinv", [P, LHEADS])
    PT = [sb(f"PT{i}", [P, 4, 2 * P]) for i in range(2)]
    o_n = sb("o_n", [P, INNER])
    oT = sb("oT", [P, IH, P])
    hs = sb("hs", [P, TILES, P])
    stats = sb("stats", [P, 2, 6])
    mv, ve, rstd = ([sb(f"{n}{i}", [P, 2]) for i in range(2)] for n in ("mv", "ve", "rstd"))
    hn = sb("hn", [P, CH])
    hnT = sb("hnT", [P, 2, CT, SEQ], F32R)
    hnT32 = sb("hnT32", [P, CT, P])
    a_sb = [sb(f"a{i}", [P, CHUNKS, 2 * P]) for i in range(2)]
    g_sb = [sb(f"g{i}", [P, CHUNKS, 2 * P]) for i in range(2)]
    xo = [sb(f"xo{i}", [P, 2, CH]) for i in range(2)]
    x0 = [sb(f"x0{i}", [P, 2, CH]) for i in range(2)]
    fstats = sb("fstats", [P, 2, 6])
    fmv, fve, frstd = (sb(n, [P, 2, 2]) for n in ("fmv", "fve", "frstd"))
    y = x0

    X = [bank(f"X{i}") for i in range(3)]
    SB = bank("S", (P, 4, 2 * P))
    M = bank("M")
    F = [bank(f"F{i}", (P, 2, 2 * P)) for i in range(2)]

    s_w = sem("weights")
    s_c = sem("constants")
    s_tab = sem("tables")
    s_x = [sem(f"x_loaded{i}") for i in range(2)]
    s_x0 = [sem(f"x0_loaded{i}") for i in range(2)]
    s_hT = sem("hT")
    s_hTe = sem("hT_evacuated")
    s_hTl = sem("hT_low")
    s_hnl = sem("hnT_low")
    s_raw = sem("raw_weights")
    s_high, s_split = sem("weights_high"), sem("weights_split")
    s_q, s_k, s_v = sem("q"), sem("k"), sem("v")
    s_sq = sem("squares")
    s_ve = sem("v_evacuated")
    s_rot = sem("rot_products")
    s_ss = sem("sums_of_squares")
    s_qr = sem("q_rotated")
    s_ks = sem("k_sum")
    s_rn = sem("norms")
    s_kr = sem("k_rotated")
    s_qkT = sem("qkT")
    s_qkTe = sem("qkT_evacuated")
    s_qkTl = sem("qkT_low")
    s_S = sem("scores")
    s_mx = sem("row_max")
    s_nb = sem("exp_bias")
    s_pr = sem("probs")
    s_PT = sem("probs_transposed")
    s_PTe = sem("PT_evacuated")
    s_AV = sem("av")
    s_ri = sem("row_sums_inverted")
    s_on = sem("o_normalised")
    s_oT = sem("oT")
    s_oTe = sem("oT_evacuated")
    s_wo = sem("o_projected")
    s_x2 = sem("x2")
    s_sh = [sem(f"shifted{i}") for i in range(TILES)]
    s_st = sem("ln_stats")
    s_rs = sem("ln_rstd")
    s_hn = sem("ln_normed")
    s_F = sem("F")
    s_Fg = sem("F_gate")
    s_Fa = sem("F_value")
    s_ge = sem("gelu")
    s_um = [sem("gated_first"), sem("gated_second")]
    s_w2 = sem("w2")
    s_xo = sem("xo")
    s_fs = sem("final_stats")
    s_fr = sem("final_rstd")
    s_y = sem("y")
    s_stored = [sem(f"stored{i}") for i in range(2)]

    WEIGHTS = 16 * (LAYER_LOADS + 1 + 8)

    block = ctx.enter_context(nc.Block())

    def split_weights(j):
        dst, cols = (wqkv, 3 * INNER) if SPLITS[j][0] == "wqkv" else (w1, 2 * HID)
        return raw[:, :, 0:cols], dst[:, HIGH], dst[:, LOW]

    def split_at(n, w_):
        return {(0, 2): 1, (SEQS - 1, 2): 2, (SEQS, 3): 3}.get((n, w_)) if isinstance(n, int) else None

    def output_half(n, w_):
        h, d = (1, 2) if w_ < 2 else (0, 1)
        return h, d, n - d

    def finished_half(n, w_):
        return (0 if w_ == 0 else 1), 2, n - 2

    def gated(engine, unit, n, w_, t):
        h, _, m = output_half(n, w_)
        if not seq_exists(m):
            return
        cols = slice(t * P, (t + 1) * P)
        engine.wait_ge(s_ge, 2 * m + h + 1)
        engine.wait_ge(s_Fa, 3 * (TILES * m + 2 * h + 2))
        unit.tensor_tensor(a_sb[h][0:HC, 0:CHUNKS - 1, cols], a_sb[h][0:HC, 0:CHUNKS - 1, cols],
                           g_sb[h][0:HC, 0:CHUNKS - 1, cols], ALU.mult)
        unit.tensor_tensor(a_sb[h][0:LAST, CHUNKS - 1, cols], a_sb[h][0:LAST, CHUNKS - 1, cols],
                           g_sb[h][0:LAST, CHUNKS - 1, cols], ALU.mult).then_inc(s_um[t], 1)

    def tile_exists(t):
        return not isinstance(t, int) or 0 <= t < ALL_TILES

    def seq_exists(n):
        return not isinstance(n, int) or 0 <= n < ALL_SEQS

    def sequences(engine, one):
        def peeled(n):
            one(n, n % 2, n // 2, lambda d: (n + d) // SEQS)

        for n in range(4):
            peeled(n)
        for layer, first, end in ((0, 4, SEQS - 2), (1, SEQS + 2, 2 * SEQS - 2)):
            with engine.Fori(0, (end - first) // 2) as i:
                for j in range(2):
                    one(2 * i + (first + j), j, i + first // 2, lambda d: layer)
            for n in range(end, end + 4):
                peeled(n)

    def back(n, w, lag):
        return (n, w - lag) if w >= lag else (n - 1, w - lag + TILES)

    @block.sync
    def _(sp):
        def load_x(n, par, layer):
            src = x_a if layer == 0 else x_b
            s = n - layer * SEQS
            sp.dma_start(x_tok[par][:], src[bass.ts(s, 1), :, :].rearrange("a (t p) c -> p (a t) c", p=P)
                         ).then_inc(s_x[par], 16)

        start_layer_loads(sp, W[1], w, 1, s_w)
        sp.dma_start(base_tab[:], w["tab"].rearrange("(t p) k d -> p t k d", p=P)).then_inc(s_w, 16)
        for layer in range(LAYERS):
            for i, name in enumerate(("q_scale", "k_scale")):
                row = w[name][layer]
                sp.dma_start(srow[layer][:, 2 * i], row.partition_broadcast(P)).then_inc(s_w, 16)
                swapped = w[name + "_swapped"][layer]
                sp.dma_start(srow[layer][:, 2 * i + 1], swapped.partition_broadcast(P)).then_inc(s_w, 16)
        load_x(0, 0, 0)

        def one(n, par, r, layer):
            for w_ in range(TILES):
                T = TILES * n + w_
                j = {(0, 0): 1, (0, 3): 2, (SEQS - 1, 3): 3}.get((n, w_)) if isinstance(n, int) else None
                if j is not None:
                    sp.wait_ge(s_split, j)
                    load_raw(sp, raw, w, j, s_raw)
                n1, w1 = back(n, w_, 1)
                if tile_exists(T - 1):
                    p1 = par if w_ >= 1 else 1 - par
                    sp.wait_ge(s_x2, T)
                    src = x2[p1][:, w1, P:CH]
                    for lo, hi in ((0, 112), (112, 127)):
                        sp.dma_start(hs[lo + 1:hi + 1, w1], src[lo:hi]).then_inc(s_sh[w1], 16)
                    if w1 < TILES - 1:
                        sp.dma_start(hs[0:1, w1 + 1], src[127:128]).then_inc(s_sh[w1], 16)
                if w_ % 2 == 0:
                    h, d, m = finished_half(n, w_)
                    if seq_exists(m):
                        if layer(-d) == LAYERS - 1:
                            sp.wait_ge(s_y, 2 * (m - SEQS) + h + 1)
                            dst, src, s = y_out, y[h], m - SEQS
                        else:
                            sp.wait_ge(s_xo, 4 * m + 2 * h + 2)
                            dst, src, s = x_b, xo[h], m
                        sp.dma_start(dst[bass.ts(s, 1), h * 2 * P:(h + 1) * 2 * P, :].rearrange("a (t p) c -> p (a t) c", p=P),
                                     src[:]).then_inc(s_stored[h], 16)
                if w_ == (2 if isinstance(n, int) and n == SEQS + 1 else 1) and seq_exists(n + 1) and seq_exists(n):
                    need(sp, s_x2, TILES * n)
                    if isinstance(n, int) and SEQS <= n + 1 <= SEQS + 2:
                        for h in range(2):
                            sp.wait_ge(s_stored[h], 16 * (n - SEQS + 2 if n + 1 < SEQS + 2 else SEQS))
                    load_x(n + 1, 1 - par, layer(1))
                if w_ % 2 == 1:
                    h, d, m = output_half(n, w_)
                    if seq_exists(m) and layer(-d) == LAYERS - 1:
                        sp.wait_ge(s_stored[h], 16 * m)
                        sp.dma_start(x0[h][:], x_a[bass.ts(m - SEQS, 1), h * 2 * P:(h + 1) * 2 * P, :]
                                     .rearrange("a (t p) c -> p (a t) c", p=P)).then_inc(s_x0[h], 16)
                if isinstance(n, int) and n == ALL_SEQS + 1 and w_ == 2:
                    break

        sequences(sp, one)
        for h in range(2):
            sp.wait_ge(s_stored[h], 16 * ALL_SEQS)

    @block.gpsimd
    def _(pool):
        def rotate(t):
            pool.wait_ge(s_rot, 2 * t + 1)
            nc.gpsimd.tensor_tensor(t1[0][:], t1[0][:], t2[0][:], ALU.add).then_inc(s_qr, 1)
            pool.wait_ge(s_rot, 2 * t + 2)
            nc.gpsimd.tensor_tensor(t1[1][:], t1[1][:], t2[1][:], ALU.add).then_inc(s_ks, 1)

        def norms(t, p):
            pool.wait_ge(s_ss, 2 * t + 2)
            need(pool, s_pr, 2 * t - 2)
            nc.gpsimd.tensor_tensor(rn[p][:], ssc[:], half[:], ALU.pow).then_inc(s_rn, 1)

        nc.gpsimd.memset(zero_col[:], 0.0).then_inc(s_c, 1)
        for i in range(2):
            nc.gpsimd.memset(hT1[i][:].bitcast(F32), 0.0).then_inc(s_c, 1)
            nc.gpsimd.memset(a_sb[i][:], 1.0).then_inc(s_c, 1)
            nc.gpsimd.memset(mask[i][:], 0.0).then_inc(s_c, 1)
        nc.gpsimd.memset(hs[:], 0.0).then_inc(s_c, 1)
        pool.wait_ge(s_c, 8)
        for i in range(2):
            nc.gpsimd.affine_select(out=mask[i][:, i], in_=mask[i][:, i], compare_op=ALU.is_ge, fill=MASKED, base=0,
                                    pattern=[[-1, P]], channel_multiplier=1).then_inc(s_c, 1)
            nc.gpsimd.affine_select(out=mask[i][:, 1 - i], in_=mask[i][:, 1 - i], compare_op=ALU.is_ge, fill=MASKED,
                                    base=0, pattern=[[1, P]], channel_multiplier=-1).then_inc(s_c, 1)
        rotate(0)
        norms(0, 0)

        def one(n, par, r, layer):
            for w_ in range(TILES):
                T = TILES * n + w_
                if tile_exists(T - 2):
                    slot = (w_ - 2) % TILES
                    cols = slice(slot * P, (slot + 1) * P)
                    pool.wait_ge(s_hTe, T + 2)
                    nc.gpsimd.tensor_tensor(hnT[:, LOW, :, cols], hnT32[:], hnT[:, HIGH, :, cols], ALU.subtract
                                            ).then_inc(s_hnl, 1)
                if tile_exists(T + 1):
                    rotate(T + 1)
                if tile_exists(T + 1):
                    norms(T + 1, (w_ + 1) % 2)
                if w_ % 2 == 0:
                    h, d, m = finished_half(n, w_)
                    if seq_exists(m) and layer(-d) == LAYERS - 1:
                        j = 2 * (m - SEQS) + h
                        pool.wait_ge(s_fs, 6 * j + 6)
                        nc.gpsimd.tensor_tensor(frstd[:, :, 0], fve[:, :, 0], half[:, 0:2], ALU.pow).then_inc(s_fr, 1)
                if tile_exists(T - 1):
                    p = (w_ + 1) % 2
                    pool.wait_ge(s_st, 4 * (T - 1) + 4)
                    need(pool, s_hn, T - 2)
                    nc.gpsimd.tensor_tensor(rstd[p][:, 0:1], ve[p][:, 0:1], half[:, 0:1], ALU.pow).then_inc(s_rs, 1)
                if w_ % 2 == 0:
                    gated(pool, nc.gpsimd, n, w_, 1)
                if isinstance(n, int) and n == ALL_SEQS + 1 and w_ == 2:
                    break

        sequences(pool, one)

    @block.scalar
    def _(act):
        def evacuate_hT(T, n, w_, layer):
            act.wait_ge(s_hT, T + 2)
            if tile_exists(T + 1):
                p = (w_ + 1) % 2
                nc.scalar.activation(hT0[p][:, HIGH], X[2][:, 0:P], ACT.Copy)
                nc.scalar.activation(hT1[p][:, HIGH, 1:P + 1], X[2][:, P:2 * P], ACT.Copy)
                last_col = zero_col[:] if (w_ + 1) % TILES == TILES - 1 else X[2][:, 2 * P - 1:2 * P]
                last = nc.scalar.activation(hT1[1 - p][:, HIGH, 0:1], last_col, ACT.Copy)
            if tile_exists(T - 2):
                n2, w2_ = back(n, w_, 2)
                W2 = W[layer(0 if w_ >= 2 else -1)]
                need(act, s_hnl, T - 2)
                for ct in range(CT):
                    for dst in (hnT[:, HIGH, ct, w2_ * P:(w2_ + 1) * P], hnT32[:, ct]):
                        last = nc.scalar.activation(dst, X[2][:, (2 + ct) * P:(3 + ct) * P], ACT.Identity,
                                                    bias=W2["ln_b"][:, ct:ct + 1], scale=W2["ln_g"][:, ct:ct + 1])
            last.then_inc(s_hTe, 1)

        def squares(t):
            act.wait_ge(s_q, t + 1)
            need(act, s_ss, 2 * t - 1)
            nc.scalar.activation(sq[:, 0], X[0][:], ACT.Square).then_inc(s_sq, 1)
            act.wait_ge(s_k, t + 1)
            nc.scalar.activation(sq[:, 1], X[1][:], ACT.Square).then_inc(s_sq, 1)

        def evacuate_v(t, w_):
            act.wait_ge(s_v, t + 1)
            need(act, s_AV, t - 2)
            nc.scalar.activation(v[:, w_], X[2][:], ACT.Copy).then_inc(s_ve, 1)

        def gate(T, i, w_, layer):
            c = 3 * (w_ % 2) + i
            rows = HC if c < CHUNKS - 1 else LAST
            act.wait_ge(s_F, 3 * (T - TILES) + i + 1)
            nc.scalar.activation(g_sb[w_ // 2][0:rows, c], F[i % 2][0:rows, 1], ACT.Identity,
                                 bias=W[layer(-1)]["b1"][0:rows, 1, c:c + 1]).then_inc(s_Fg, 1)

        def split_high(j):
            need(act, s_raw, 16 * j)
            if j == 2:
                act.wait_ge(s_v, TILES * SEQS)
            if j == 3:
                act.wait_ge(s_F, 3 * TILES * SEQS)
            src, high, _ = split_weights(j)
            nc.scalar.activation(high, src, ACT.Copy).then_inc(s_high, 1)

        split_high(0)
        act.wait_ge(s_w, WEIGHTS)
        act.wait_ge(s_c, 12)
        evacuate_hT(-1, -1, 3, lambda d: 0)
        squares(0)
        evacuate_v(0, 0)

        def one(n, par, r, layer):
            for w_ in range(TILES):
                T = TILES * n + w_
                p = w_ % 2
                live, feed = tile_exists(T), seq_exists(n - 1)
                if live:
                    act.wait_ge(s_qkT, 2 * T + 1)
                    nc.scalar.activation(qT[:, HIGH], X[0][:].rearrange("p (b q) -> p b q", q=P), ACT.Copy).then_inc(s_qkTe, 1)
                    act.wait_ge(s_qkT, 2 * T + 2)
                    nc.scalar.activation(kT[:, HIGH, :, p], X[1][:].rearrange("p (b q) -> p b q", q=P), ACT.Copy
                                         ).then_inc(s_qkTe, 1)
                if feed:
                    gate(T, 0, w_, layer)
                if tile_exists(T + 1) or tile_exists(T - 2):
                    evacuate_hT(T, n, w_, layer)
                if tile_exists(T - 1):
                    act.wait_ge(s_oT, T)
                    nc.scalar.activation(oT[:], M[:], ACT.Copy).then_inc(s_oTe, 1)
                if live:
                    exps(T, w_, 0)
                if tile_exists(T + 1):
                    squares(T + 1)
                if live:
                    act.wait_ge(s_PT, 2 * T + 1)
                    evacuate_PT(w_, 0)
                if w_ % 2 == 0:
                    h, d = (1, 2) if w_ == 0 else (0, 1)
                    m = n - d
                    if seq_exists(m):
                        act.wait_ge(s_Fg, 3 * (TILES * m + 2 * h + 2))
                        nc.scalar.activation(g_sb[h][0:HC, 0:CHUNKS - 1], g_sb[h][0:HC, 0:CHUNKS - 1], ACT.Gelu)
                        nc.scalar.activation(g_sb[h][0:LAST, CHUNKS - 1], g_sb[h][0:LAST, CHUNKS - 1], ACT.Gelu
                                             ).then_inc(s_ge, 1)
                if feed:
                    gate(T, 1, w_, layer)
                if live:
                    exps(T, w_, 1)
                if tile_exists(T + 1):
                    evacuate_v(T + 1, (w_ + 1) % TILES)
                if feed:
                    gate(T, 2, w_, layer)
                if live:
                    act.wait_ge(s_PT, 2 * T + 2)
                    evacuate_PT(w_, 1)
                if split_at(n, w_) is not None:
                    split_high(split_at(n, w_))
                if isinstance(n, int) and n == ALL_SEQS + 1 and w_ == 2:
                    break

        def keys(w_):
            return slice(0, P) if w_ == 0 else slice(0, 2 * P)

        def exps(T, w_, hf):
            act.wait_ge(s_nb, 2 * T + hf + 1)
            for e in range(2):
                for ps in range(2):
                    i, h = 2 * e + ps, 4 * hf + 2 * ps + e
                    last = nc.scalar.activation(probs[hf][:, i, keys(w_)], SB[:, i, keys(w_)], ACT.Exp,
                                                bias=nb[hf][:, i:i + 1], scale=rn[w_ % 2][:, h:h + 1],
                                                accum_out=rs[w_ % 2][:, h:h + 1])
            last.then_inc(s_pr, 1)

        def evacuate_PT(w_, hf):
            nc.scalar.activation(PT[hf][:, :, keys(w_)], SB[:, :, keys(w_)], ACT.Copy).then_inc(s_PTe, 1)

        sequences(act, one)

    @block.vector
    def _(dve):
        def rot_products(t, w_, layer):
            for i in range(2):
                dve.wait_ge(s_sq, 2 * t + i + 1)
                need(dve, s_qkT, 2 * t - 1 + i)
                src = X[i][:].rearrange("p (h d) -> p h d", d=LDIM)
                rows = tab[layer][:, w_]
                cos = rows[:, 2 * i].unsqueeze(1).to_broadcast([P, LHEADS, LDIM])
                sin = rows[:, 2 * i + 1].unsqueeze(1).to_broadcast([P, LHEADS, LDIM])
                H = LDIM // 2
                nc.vector.tensor_tensor(t1[i][:], src, cos, ALU.mult)
                nc.vector.tensor_tensor(t2[i][:, :, 0:H], src[:, :, H:LDIM], sin[:, :, 0:H], ALU.mult)
                nc.vector.tensor_tensor(t2[i][:, :, H:LDIM], src[:, :, 0:H], sin[:, :, H:LDIM], ALU.mult
                                        ).then_inc(s_rot, 1)
            nc.vector.tensor_reduce(out=ss[:].rearrange("p (a h) -> p a h", a=2), in_=sq[:], axis=AX.X, op=ALU.add
                                    ).then_inc(s_ss, 1)
            dve.wait_ge(s_ss, 2 * t + 1)
            need(dve, s_rn, t)
            nc.vector.tensor_scalar(ssc[:], ss[:], 1e-24, None, ALU.max).then_inc(s_ss, 1)

        def scale_k(t, p):
            dve.wait_ge(s_rn, t + 1)
            nc.vector.tensor_tensor(t1[1][:], t1[1][:], rn[p][:, LHEADS:2 * LHEADS].unsqueeze(2)
                                    .to_broadcast([P, LHEADS, LDIM]), ALU.mult).then_inc(s_kr, 1)

        def low_qkT(T, i, p):
            dst, high = ((qT[:, LOW], qT[:, HIGH]), (kT[:, LOW, :, p], kT[:, HIGH, :, p]))[i]
            dve.wait_ge(s_qkTe, 2 * T + i + 1)
            nc.vector.tensor_tensor(dst, X[i][:].rearrange("p (b q) -> p b q", q=P), high, ALU.subtract
                                    ).then_inc(s_qkTl, 1)

        def row_max(T, w_, hf):
            cols = slice(0, P) if w_ == 0 else slice(0, 2 * P)
            dve.wait_ge(s_S, 2 * T + hf + 1)
            nc.vector.tensor_reduce(out=mx[:], in_=SB[:, :, cols], axis=AX.X, op=ALU.max).then_inc(s_mx, 1)
            dve.wait_ge(s_mx, 2 * T + hf + 1)
            nc.vector.scalar_tensor_tensor(
                out=nb[hf][:].rearrange("p (e s) -> p e s", e=2), in0=mx[:].rearrange("p (e s) -> p e s", e=2),
                scalar=-1.0, in1=rn[w_ % 2][:, 4 * hf:4 * hf + 4].rearrange("p (s e) -> p e s", e=2),
                op0=ALU.mult, op1=ALU.mult).then_inc(s_nb, 1)

        def value(T, i, w_, layer):
            c = 3 * (w_ % 2) + i
            rows = HC if c < CHUNKS - 1 else LAST
            dve.wait_ge(s_Fg, 3 * (T - TILES) + i + 1)
            nc.vector.tensor_scalar(a_sb[w_ // 2][0:rows, c], F[i % 2][0:rows, 0],
                                    W[layer(-1)]["b1"][0:rows, 0, c:c + 1], None, ALU.add).then_inc(s_Fa, 1)

        def split_low(j):
            dve.wait_ge(s_high, j + 1)
            src, high, low = split_weights(j)
            nc.vector.tensor_tensor(low, src, high, ALU.subtract).then_inc(s_split, 1)

        def low_hT(T, w_):
            p = (w_ + 1) % 2
            dve.wait_ge(s_hTe, T + 2)
            nc.vector.tensor_tensor(hT0[p][:, LOW], X[2][:, 0:P], hT0[p][:, HIGH], ALU.subtract)
            nc.vector.tensor_tensor(hT1[p][:, LOW, 1:P + 1], X[2][:, P:2 * P], hT1[p][:, HIGH, 1:P + 1], ALU.subtract)
            last_col = zero_col[:] if (w_ + 1) % TILES == TILES - 1 else X[2][:, 2 * P - 1:2 * P]
            nc.vector.tensor_tensor(hT1[1 - p][:, LOW, 0:1], last_col, hT1[1 - p][:, HIGH, 0:1], ALU.subtract
                                    ).then_inc(s_hTl, 1)

        dve.wait_ge(s_c, 12)
        split_low(0)
        low_hT(-1, 3)
        dve.wait_ge(s_w, WEIGHTS)
        for layer in range(LAYERS):
            need(dve, s_tab, TILES * layer)
            for t in range(TILES):
                nc.vector.tensor_tensor(tab[layer][:, t], base_tab[:, t], srow[layer][:], ALU.mult).then_inc(s_tab, 1)
        dve.wait_ge(s_tab, LAYERS * TILES)
        rot_products(0, 0, 0)
        scale_k(0, 0)

        def one(n, par, r, layer):
            for w_ in range(TILES):
                T = TILES * n + w_
                p = w_ % 2
                live, feed = tile_exists(T), seq_exists(n - 1)
                if tile_exists(T - 2):
                    n2, w2_ = back(n, w_, 2)
                    p2 = par if w_ >= 2 else 1 - par
                    dve.wait_ge(s_rs, T - 1)
                    need(dve, s_hT, T + 1)
                    nc.vector.tensor_scalar(hn[:, 0:P], x2[p2][:, w2_, 0:P], mv[p][:, 0:1], rstd[p][:, 0:1],
                                            ALU.subtract, ALU.mult)
                    nc.vector.tensor_scalar(hn[:, P:CH], hs[:, w2_], mv[p][:, 0:1], rstd[p][:, 0:1],
                                            ALU.subtract, ALU.mult).then_inc(s_hn, 1)
                if live:
                    low_qkT(T, 0, p)
                if live:
                    low_qkT(T, 1, p)
                if feed:
                    value(T, 0, w_, layer)
                if tile_exists(T - 1):
                    dve.wait_ge(s_AV, T)
                    nc.vector.reciprocal(rinv[:], rs[1 - p][:]).then_inc(s_ri, 1)
                    dve.wait_ge(s_ri, T)
                    nc.vector.tensor_tensor(o_n[:].rearrange("p (h d) -> p h d", d=LDIM),
                                            M[:].rearrange("p (h d) -> p h d", d=LDIM),
                                            rinv[:].unsqueeze(2).to_broadcast([P, LHEADS, LDIM]), ALU.mult
                                            ).then_inc(s_on, 1)
                if tile_exists(T + 1):
                    low_hT(T, w_)
                if live:
                    row_max(T, w_, 0)
                if tile_exists(T - 1):
                    n1, w1_ = back(n, w_, 1)
                    p1 = par if w_ >= 1 else 1 - par
                    dve.wait_ge(s_wo, T)
                    nc.vector.tensor_tensor(x2[p1][:, w1_], M[:, 0:CH], x_tok[p1][:, w1_], ALU.add).then_inc(s_x2, 1)
                if finished(n, w_, layer):
                    final_stats(*finished(n, w_, layer))
                if tile_exists(T + 1):
                    rot_products(T + 1, (w_ + 1) % TILES, layer(0 if w_ < 3 else 1))
                if feed:
                    value(T, 1, w_, layer)
                if live:
                    row_max(T, w_, 1)
                if w_ % 2 == 0:
                    gated(dve, nc.vector, n, w_, 0)
                if feed:
                    value(T, 2, w_, layer)
                if tile_exists(T + 1):
                    scale_k(T + 1, 1 - p)
                if finished(n, w_, layer):
                    final_norm(*finished(n, w_, layer))
                if tile_exists(T - 1):
                    q = 1 - p
                    n1_count = n1 + 1
                    dve.wait_ge(s_sh[w1_], (48 if w1_ < TILES - 1 else 32) * n1_count)
                    if w1_ > 0:
                        dve.wait_ge(s_sh[w1_ - 1], 48 * n1_count)
                    nc.vector.bn_stats(stats[:, 0], x2[p1][:, w1_, 0:P]).then_inc(s_st, 1)
                    nc.vector.bn_stats(stats[:, 1], hs[:, w1_]).then_inc(s_st, 1)
                    dve.wait_ge(s_st, 4 * (T - 1) + 2)
                    nc.vector.memset(carrier[:], 0.0)
                    nc.vector.bn_aggr(mv[q][:], stats[:]).then_inc(s_st, 1)
                    dve.wait_ge(s_st, 4 * (T - 1) + 3)
                    nc.vector.tensor_scalar(ve[q][:, 0:1], mv[q][:, 1:2], EPS, None, ALU.add).then_inc(s_st, 1)
                h, d, m = output_half(n, w_)
                if seq_exists(m):
                    t, pm = w_ % 2, par if d == 2 else 1 - par
                    dve.wait_ge(s_w2, 4 * m + 2 * h + t + 1)
                    if t == 0 and not (isinstance(m, int) and m == 0):
                        dve.wait_ge(s_stored[h], 16 * m)
                    nc.vector.tensor_tensor(xo[h][:, t], F[1][:, t], x2[pm][:, 2 * h + t], ALU.add).then_inc(s_xo, 1)
                if split_at(n, w_) is not None:
                    split_low(split_at(n, w_))
                if isinstance(n, int) and n == ALL_SEQS + 1 and w_ == 2:
                    break

        def finished(n, w_, layer):
            h, d, m = finished_half(n, w_)
            return (m, h) if w_ % 2 == 0 and seq_exists(m) and layer(-d) == LAYERS - 1 else None

        def final_stats(m, h):
            j = 2 * (m - SEQS) + h
            dve.wait_ge(s_xo, 4 * m + 2 * h + 2)
            dve.wait_ge(s_x0[h], 16 * (m - SEQS + 1))
            nc.vector.tensor_tensor(xo[h][:], xo[h][:], x0[h][:], ALU.add).then_inc(s_fs, 1)
            dve.wait_ge(s_fs, 6 * j + 1)
            for t in range(2):
                nc.vector.bn_stats(fstats[:, t], xo[h][:, t]).then_inc(s_fs, 1)
            dve.wait_ge(s_fs, 6 * j + 3)
            nc.vector.memset(carrier[:], 0.0)
            for t in range(2):
                nc.vector.bn_aggr(fmv[:, t], fstats[:, t]).then_inc(s_fs, 1)
            dve.wait_ge(s_fs, 6 * j + 5)
            nc.vector.tensor_scalar(fve[:, :, 0], fmv[:, :, 1], EPS, None, ALU.add).then_inc(s_fs, 1)

        def final_norm(m, h):
            j = 2 * (m - SEQS) + h
            dve.wait_ge(s_fr, j + 1)
            for t in range(2):
                last = nc.vector.tensor_scalar(y[h][:, t], xo[h][:, t], fmv[:, t, 0:1], frstd[:, t, 0:1],
                                               ALU.subtract, ALU.mult)
            last.then_inc(s_y, 1)

        sequences(dve, one)

    @block.tensor
    def _(pe):
        PART_PAIRS = [(HIGH, HIGH), (HIGH, LOW), (LOW, HIGH)]

        def keys(w_):
            return slice(0, P) if w_ == 0 else slice(0, 2 * P)

        def transpose_h(T, n, w_, par, x_loads):
            need(pe, s_ve, min(T + 1, ALL_TILES) if isinstance(T, int) else T + 1)
            if not (isinstance(T, int) and T < 0):
                pe.wait_ge(s_hTe, T + 1)
            if tile_exists(T + 1):
                wn = (w_ + 1) % TILES
                pn = par if w_ < TILES - 1 else 1 - par
                if wn == 0:
                    pe.wait_ge(s_x[pn], 16 * x_loads)
                for ct in range(CT):
                    last = nc.tensor.transpose(X[2][:, ct * P:(ct + 1) * P], x_tok[pn][:, wn, ct * P:(ct + 1) * P], ident[:])
            if tile_exists(T - 2):
                pe.wait_ge(s_hn, T - 1)
                for ct in range(CT):
                    last = nc.tensor.transpose(X[2][:, (2 + ct) * P:(3 + ct) * P], hn[:, ct * P:(ct + 1) * P], ident[:])
            last.then_inc(s_hT, 1)

        def projection_ready(t, layer):
            pe.wait_ge(s_hTl, t + 1)
            if isinstance(t, int) and t % (TILES * SEQS) == 0:
                pe.wait_ge(s_split, SPLITS.index(("wqkv", layer)) + 1)
            need(pe, s_qkTl, 2 * t)

        def project(i, p, signal):
            hT = (hT0[p][:], hT1[p][:, :, 0:P])
            for k in range(CT):
                for a, b in PART_PAIRS:
                    last = nc.tensor.matmul(X[i][:], hT[k][:, a], wqkv[:, b, k, i * INNER:(i + 1) * INNER],
                                            start=(k == 0 and (a, b) == PART_PAIRS[0]),
                                            stop=(k == CT - 1 and (a, b) == PART_PAIRS[-1]))
            last.then_inc(signal, 1)

        def scores(T, w_, hf):
            need(pe, s_PTe, 2 * T + hf)
            cols = keys(w_)
            m = mask[w_ % 2][:].rearrange("p a q -> p (a q)")[:, cols]
            for e in range(2):
                nc.tensor.matmul(SB[:, 2 * e:2 * e + 2, cols], identb[:],
                                 m.unsqueeze(1).to_broadcast([P, 2, cols.stop]), start=True, stop=False,
                                 skip_group_check=True)
            if hf == 0:
                pe.wait_ge(s_qkTl, 2 * T + 2)
            for ps in range(2):
                for e in range(2):
                    rows = slice(64 * e, 64 * e + 64)
                    for a, b in PART_PAIRS:
                        last = nc.tensor.matmul(SB[:, 2 * e + ps, cols], qT[rows, a, 2 * hf + ps],
                                                kT[rows, b, 2 * hf + ps].rearrange("p a q -> p (a q)")[:, cols],
                                                start=False, stop=True, skip_group_check=True)
            last.then_inc(s_S, 1)

        def transpose_probs(T, w_, hf):
            pe.wait_ge(s_pr, 2 * T + hf + 1)
            for i in range(4):
                for a in range(1 if w_ == 0 else 2):
                    last = nc.tensor.transpose(SB[:, i, a * P:(a + 1) * P], probs[hf][:, i, a * P:(a + 1) * P], ident[:])
            last.then_inc(s_PT, 1)

        def times_v(t, w_, hf):
            pe.wait_ge(s_PTe, 2 * t + hf + 1)
            slots = 1 if w_ == 0 else 2
            for e in range(2):
                for ps in range(2):
                    i, h = 2 * e + ps, 4 * hf + 2 * ps + e
                    for a in range(slots):
                        first = hf == 0 and i == 0 and a == 0
                        last = nc.tensor.matmul(M[:, h * LDIM:(h + 1) * LDIM], PT[hf][:, i, a * P:(a + 1) * P],
                                                v[:, w_ if a == w_ % 2 else w_ - 1, h * LDIM:(h + 1) * LDIM], start=first,
                                                stop=(hf == 1 and i == 3 and a == slots - 1), skip_group_check=True)
            if hf == 1:
                last.then_inc(s_AV, 1)

        def hidden(T, i, w_, layer):
            f = 3 * (T - TILES) + i
            c, hf = 3 * (w_ % 2) + i, w_ // 2
            if i == 0:
                if w_ % 2 == 0:
                    pe.wait_ge(s_hnl, T - 2)
                if isinstance(T, int) and T % (TILES * SEQS) == TILES:
                    pe.wait_ge(s_split, SPLITS.index(("w1", layer(-1))) + 1)
                need(pe, s_Fa, f)
            elif i == 1:
                need(pe, s_Fa, f - 2)
                need(pe, s_xo, T - 6)
            else:
                pe.wait_ge(s_Fa, f - 1)
            size = HC if c < CHUNKS - 1 else LAST
            for part in range(2):
                for k in range(CT):
                    col = part * HID + c * HC
                    for a, b in PART_PAIRS:
                        last = nc.tensor.matmul(F[i % 2][0:size, part], w1[:, a, k, col:col + size],
                                                hnT[:, b, k, hf * 2 * P:(hf + 1) * 2 * P],
                                                start=(k == 0 and (a, b) == PART_PAIRS[0]),
                                                stop=(k == CT - 1 and (a, b) == PART_PAIRS[-1]))
            last.then_inc(s_F, 1)

        pe.wait_ge(s_w, WEIGHTS)
        pe.wait_ge(s_c, 12)
        transpose_h(-1, -1, 3, 1, 1)
        projection_ready(0, 0)
        for i, signal in enumerate((s_q, s_k, s_v)):
            project(i, 0, signal)

        def one(n, par, r, layer):
            for w_ in range(TILES):
                T = TILES * n + w_
                live, feed = tile_exists(T), seq_exists(n - 1)
                next_hT = (w_ + 1) % 2
                if live:
                    pe.wait_ge(s_qr, T + 1)
                    for b in range(PAIRS):
                        last = nc.tensor.transpose(X[0][:, b * P:(b + 1) * P],
                                                   t1[0][:, 2 * b:2 * b + 2].rearrange("p h d -> p (h d)"), ident[:])
                    last.then_inc(s_qkT, 1)
                    pe.wait_ge(s_kr, T + 1)
                    for b in range(PAIRS):
                        last = nc.tensor.transpose(X[1][:, b * P:(b + 1) * P],
                                                   t1[1][:, 2 * b:2 * b + 2].rearrange("p h d -> p (h d)"), ident[:])
                    last.then_inc(s_qkT, 1)
                if feed:
                    hidden(T, 0, w_, layer)
                if tile_exists(T + 1) or tile_exists(T - 2):
                    transpose_h(T, n, w_, par, r + 1 + par)
                if tile_exists(T - 1):
                    n1, w1_ = back(n, w_, 1)
                    times_v(T - 1, w1_, 1)
                if live:
                    scores(T, w_, 0)
                if tile_exists(T - 1):
                    pe.wait_ge(s_on, T)
                    for b in range(IH):
                        last = nc.tensor.transpose(M[:, b * P:(b + 1) * P], o_n[:, b * P:(b + 1) * P], ident[:])
                    last.then_inc(s_oT, 1)
                if tile_exists(T + 1):
                    projection_ready(T + 1, layer(0 if w_ < 3 else 1))
                    project(0, next_hT, s_q)
                if tile_exists(T - 1):
                    pe.wait_ge(s_oTe, T)
                    wo = W[layer(0 if w_ >= 1 else -1)]["o"]
                    for b in range(IH):
                        last = nc.tensor.matmul(M[:, 0:CH], oT[:, b], wo[:, b], start=(b == 0), stop=(b == IH - 1))
                    last.then_inc(s_wo, 1)
                if tile_exists(T + 1):
                    project(1, next_hT, s_k)
                if live:
                    transpose_probs(T, w_, 0)
                if feed:
                    hidden(T, 1, w_, layer)
                if live:
                    scores(T, w_, 1)
                    need(pe, s_x2, T)
                    pe.wait_ge(s_ve, T + 1)
                    times_v(T, w_, 0)
                if tile_exists(T + 1):
                    project(2, next_hT, s_v)
                if feed:
                    hidden(T, 2, w_, layer)
                h, d, m = output_half(n, w_)
                if seq_exists(m):
                    t = w_ % 2
                    pe.wait_ge(s_um[t], 2 * m + h + 1)
                    if feed:
                        pe.wait_ge(s_Fa, 3 * (T - TILES) + 2)
                    else:
                        pe.wait_ge(s_xo, T - 6)
                    for c in range(CHUNKS):
                        rows = HC if c < CHUNKS - 1 else LAST + 1
                        last = nc.tensor.matmul(F[1][:, t], a_sb[h][0:rows, c, t * P:(t + 1) * P],
                                                W[layer(-d)]["w2"][0:rows, c], start=(c == 0), stop=(c == CHUNKS - 1))
                    last.then_inc(s_w2, 1)
                if live:
                    transpose_probs(T, w_, 1)
                if isinstance(n, int) and n == ALL_SEQS + 1 and w_ == 2:
                    break

        sequences(pe, one)


def rotary_tables():
    d = np.arange(0, LDIM, 2, dtype=np.float32)
    t = np.arange(SEQ, dtype=np.float32)
    freqs = t[:, None] * (np.float32(1.0) / np.float32(10000.0) ** (d / np.float32(LDIM)))[None, :]
    base = (d + np.float32(0.4 * LDIM)) / np.float32(1.4 * LDIM)
    scale = base[None, :] ** ((t - np.float32(SEQ // 2)) / np.float32(64.0))[:, None]
    cos, sin = np.cos(freqs), np.sin(freqs)
    both = lambda a, b: np.concatenate([a, b], axis=1)
    q = [np.float32(8.0) * both(cos * scale, cos * scale), np.float32(8.0) * both(-sin * scale, sin * scale)]
    k = [both(cos / scale, cos / scale), both(-sin / scale, sin / scale)]
    return np.stack(q + k, axis=1).astype(np.float32)


def build(nc, w, y_out):
    x_a = nc.dram_tensor("x_after_heads", (SEQS, SEQ, CH), F32).ap()
    x_b = nc.dram_tensor("x_after_layer", (SEQS, SEQ, CH), F32).ap()
    with ExitStack() as ctx:
        consts = make_constants(nc, ctx)
        W0 = room_for_layer(nc, ctx, 0)
        raw = ctx.enter_context(nc.sbuf_tensor("raw_weights", [P, CT, 3 * INNER], F32))
        with ExitStack() as stage:
            head_attention(nc, stage, w["x"], w, x_a, consts, W0, raw)
        with ExitStack() as stage:
            W1 = room_for_layer(nc, stage, 1)
            layers(nc, stage, x_a, x_b, y_out, w, [W0, W1], raw, consts)


def kernel(**inputs):
    import concourse.bacc as bacc
    from concourse.bass_utils import run_bass_kernel_spmd

    g = {name[3:]: np.asarray(value) for name, value in inputs.items()}

    def head_order(a):
        return a.reshape(a.shape[:-1] + (CT, JH, HDIM)).swapaxes(-1, -2).reshape(a.shape)

    def on_partitions(a, size=P):
        a = np.concatenate([a, np.zeros(a.shape[:-1] + (-a.shape[-1] % size,), a.dtype)], axis=-1)
        return np.moveaxis(a.reshape(a.shape[:-1] + (-1, size)), -1, 1)

    def swapped(a):
        return np.concatenate([a[..., LDIM // 2:], a[..., :LDIM // 2]], axis=-1)

    arrays = {
        "x": g["attn_x"],
        "Wq": head_order(g["attn_Wq"].T), "Wk": head_order(g["attn_Wk"].T),
        "Wv": g["attn_Wv"].T, "Wo": g["attn_Wo"].T,
        "bq": head_order(g["attn_bq"]).reshape(CT, P).T, "bk": head_order(g["attn_bk"]).reshape(CT, P).T,
        "bv": g["attn_bv"], "bo": g["attn_bo"],
        "wqkv": g["ffn_wqkv"], "wo2": g["ffn_wo"], "w1": g["ffn_w1"], "w2": g["ffn_w2"],
        "b1": on_partitions(g["ffn_b1"].reshape(LAYERS, 2, HID), HC), "b2": g["ffn_b2"],
        "ln_g": on_partitions(g["ffn_ln_g"]), "ln_b": on_partitions(g["ffn_ln_b"]),
        "q_scale": g["ffn_q_scale"], "k_scale": g["ffn_k_scale"],
        "q_scale_swapped": swapped(g["ffn_q_scale"]), "k_scale_swapped": swapped(g["ffn_k_scale"]),
        "tab": rotary_tables(),
    }
    arrays = {name: np.ascontiguousarray(a) for name, a in arrays.items()}
    nc = bacc.Bacc("TRN2", target_bir_lowering=False, num_devices=1)
    w = {name: nc.dram_tensor(f"in_{name}", a.shape, F32, kind="ExternalInput").ap() for name, a in arrays.items()}
    out = nc.dram_tensor("out_0", (SEQS, SEQ, CH), F32, kind="ExternalOutput").ap()
    build(nc, w, out)
    result = run_bass_kernel_spmd(nc, [{f"in_{name}": a for name, a in arrays.items()}], core_ids=[0])
    return result.results[0]["out_0"]
```
